# Optimizing a Trainium2 kernel written in Bass

```python
import numpy as np
import jax
import jax.numpy as jnp

def _softmax(x, axis=-1):
    return jax.nn.softmax(x, axis=axis)

def _gelu(x):
    return jax.nn.gelu(x, approximate=True)

def _silu(x):
    return jax.nn.silu(x)

def _sigmoid(x):
    return jax.nn.sigmoid(x)

def _layernorm(x, axis=-1, eps=1e-05):
    m = jnp.mean(x, axis=axis, keepdims=True)
    v = jnp.var(x, axis=axis, keepdims=True)
    return (x - m) / jnp.sqrt(v + eps)

def _scatter_add(tgt, idx, src, axis=0):
    return tgt.at[idx].add(src)

def _segment_sum(src, seg, n):
    return jax.ops.segment_sum(src, seg, n)
kernel_name = 'mk_xattn_ffn_d2_seqx_r8_789dbe'

def setup_inputs(seed: int=0):
    np.random.seed(seed)
    _w = jnp.asarray

    def _rec_inputs():
        import jax
        import jax.numpy as jnp
        _rk = jax.random.key(seed)
        x = -0.0002928 + 1 * jax.random.normal(jax.random.fold_in(_rk, 1), (64, 64, 128), jnp.float32)
        _lenS = 64 - jax.random.randint(jax.random.fold_in(_rk, 7), (64,), 0, max(1, 64 // 4) + 1, jnp.int32)
        _lenS2 = 64 - jax.random.randint(jax.random.fold_in(_rk, 8), (64,), 0, max(1, 64 // 4) + 1, jnp.int32)
        _ctx_1024P = jax.random.normal(jax.random.fold_in(_rk, 11), (64, 16, 128), jnp.float32)
        _ctx_1024c = jax.random.dirichlet(jax.random.fold_in(_rk, 511), 0.3 * jnp.ones((16,), jnp.float32), (64, 64))
        _ctx_1024t = jnp.einsum('bsk,bkd->bsd', _ctx_1024c, _ctx_1024P)
        _ctx_1024t = _ctx_1024t * jax.lax.rsqrt(jnp.mean(jnp.square(_ctx_1024t)) + 1e-12) * 0.953939
        ctx_1024 = -1.39393e-06 + 0.999914 * (_ctx_1024t + 0.3 * jax.random.normal(jax.random.fold_in(_rk, 611), (64, 64, 128), jnp.float32))
        return (x, ctx_1024)
    x, ctx_1024 = _rec_inputs()

    def _L0_xattn_setup():
        import jax, jax.numpy as jnp
        import numpy as np
        D_MODEL = 128
        NUM_HEADS = 16
        D_HEAD = D_MODEL // NUM_HEADS
        WINDOW = 128

        def _to_heads(x):
            B, S, _ = x.shape
            return x.reshape(B, S, NUM_HEADS, D_HEAD).transpose(0, 2, 1, 3)
        key = jax.random.key(seed)
        ks = jax.random.split(key, 12)
        B, S, D = (2, 256, D_MODEL)
        scale = 1.0 / np.sqrt(D)
        inp = {'query': jax.random.normal(ks[0], (B, S, D), jnp.float32), 'key': jax.random.normal(ks[1], (B, S, D), jnp.float32), 'value': jax.random.normal(ks[2], (B, S, D), jnp.float32), 'Wq': jax.random.normal(ks[3], (D, D), jnp.float32) * scale, 'bq': jnp.zeros((D,), jnp.float32), 'Wk': jax.random.normal(ks[4], (D, D), jnp.float32) * scale, 'bk': jnp.zeros((D,), jnp.float32), 'Wv': jax.random.normal(ks[5], (D, D), jnp.float32) * scale, 'bv': jnp.zeros((D,), jnp.float32), 'Wo': jax.random.normal(ks[6], (D, D), jnp.float32) * scale, 'bo': jnp.zeros((D,), jnp.float32)}
        return inp
    _L0_xattn_all = _L0_xattn_setup()
    _L0_xattn_in = {k: v for k, v in _L0_xattn_all.items() if k in ('Wq', 'bq', 'Wk', 'bk', 'Wv', 'bv', 'Wo', 'bo')}
    del _L0_xattn_all

    def _L0_ffn_setup():
        import math
        import jax, jax.numpy as jnp
        from jax import lax
        import numpy as np
        E = 16
        K = 2
        CF = 1.25
        key = jax.random.key(seed)
        k0, k1, k2, k3, k4 = jax.random.split(key, 5)
        B, S, D, H = (2, 256, 128, 128)
        scale = 0.02
        return {'x': jax.random.normal(k0, (B, S, D), dtype=jnp.float32), 'router_w': jax.random.normal(k1, (D, E), dtype=jnp.float32) * scale, 'gate_w': jax.random.normal(k2, (E, D, H), dtype=jnp.float32) * scale, 'up_w': jax.random.normal(k3, (E, D, H), dtype=jnp.float32) * scale, 'down_w': jax.random.normal(k4, (E, H, D), dtype=jnp.float32) * scale}
    _L0_ffn_all = _L0_ffn_setup()
    _L0_ffn_in = {k: v for k, v in _L0_ffn_all.items() if k in ('router_w', 'gate_w', 'up_w', 'down_w')}
    del _L0_ffn_all

    def _L1_xattn_setup():
        import jax, jax.numpy as jnp
        import numpy as np
        B, S, DM = (4, 256, 128)
        H, HD = (16, 64)
        key = jax.random.key(seed)
        ks = jax.random.split(key, 11)
        s = 0.02
        return {'queries': jax.random.normal(ks[0], (B, S, DM), dtype=jnp.float32), 'keys': jax.random.normal(ks[1], (B, S, DM), dtype=jnp.float32), 'values': jax.random.normal(ks[2], (B, S, DM), dtype=jnp.float32), 'Wq': jax.random.normal(ks[3], (DM, H * HD), dtype=jnp.float32) * s, 'bq': jnp.zeros((H * HD,), dtype=jnp.float32), 'Wk': jax.random.normal(ks[4], (DM, H * HD), dtype=jnp.float32) * s, 'bk': jnp.zeros((H * HD,), dtype=jnp.float32), 'Wv': jax.random.normal(ks[5], (DM, H * HD), dtype=jnp.float32) * s, 'bv': jnp.zeros((H * HD,), dtype=jnp.float32), 'Wo': jax.random.normal(ks[6], (H * HD, DM), dtype=jnp.float32) * s, 'bo': jnp.zeros((DM,), dtype=jnp.float32)}
    _L1_xattn_all = _L1_xattn_setup()
    _L1_xattn_in = {k: v for k, v in _L1_xattn_all.items() if k in ('Wq', 'bq', 'Wk', 'bk', 'Wv', 'bv', 'Wo', 'bo')}
    del _L1_xattn_all

    def _L1_ffn_setup():
        import jax, jax.numpy as jnp
        import numpy as np
        EMBED_DIM = 128
        HIDDEN = 4 * EMBED_DIM
        BATCH, SEQ = (4, 512)
        EPS = 1e-05

        def _quant_weight(w):
            s = jnp.clip(jnp.mean(jnp.abs(w)), EPS, None)
            wq = jnp.clip(jnp.round(w / s), -1.0, 1.0) * s
            return w + jax.lax.stop_gradient(wq - w)

        def _quant_act(x):
            scale = 127.0 / jnp.clip(jnp.max(jnp.abs(x), axis=-1, keepdims=True), EPS, None)
            xq = jnp.clip(jnp.round(x * scale), -128.0, 127.0) / scale
            return x + jax.lax.stop_gradient(xq - x)

        def _bitlinear(x, w):
            return jnp.einsum('bsi,oi->bso', _quant_act(x), _quant_weight(w))
        key = jax.random.key(seed)
        k1, k2, k3 = jax.random.split(key, 3)
        x = jax.random.normal(k1, (BATCH, SEQ, EMBED_DIM), dtype=jnp.float32)
        w1 = jax.random.normal(k2, (HIDDEN, EMBED_DIM), dtype=jnp.float32) * (1.0 / np.sqrt(EMBED_DIM))
        w2 = jax.random.normal(k3, (EMBED_DIM, HIDDEN), dtype=jnp.float32) * (1.0 / np.sqrt(HIDDEN))
        return {'x': x, 'w1': w1, 'w2': w2}
    _L1_ffn_all = _L1_ffn_setup()
    _L1_ffn_in = {k: v for k, v in _L1_ffn_all.items() if k in ('w1', 'w2')}
    del _L1_ffn_all
    return {'x': x, 'ctx_1024': ctx_1024, 'L0_xattn_Wq': _L0_xattn_in['Wq'], 'L0_xattn_bq': _L0_xattn_in['bq'], 'L0_xattn_Wk': _L0_xattn_in['Wk'], 'L0_xattn_bk': _L0_xattn_in['bk'], 'L0_xattn_Wv': _L0_xattn_in['Wv'], 'L0_xattn_bv': _L0_xattn_in['bv'], 'L0_xattn_Wo': _L0_xattn_in['Wo'], 'L0_xattn_bo': _L0_xattn_in['bo'], 'L0_ffn_router_w': _L0_ffn_in['router_w'], 'L0_ffn_gate_w': _L0_ffn_in['gate_w'], 'L0_ffn_up_w': _L0_ffn_in['up_w'], 'L0_ffn_down_w': _L0_ffn_in['down_w'], 'L1_xattn_Wq': _L1_xattn_in['Wq'], 'L1_xattn_bq': _L1_xattn_in['bq'], 'L1_xattn_Wk': _L1_xattn_in['Wk'], 'L1_xattn_bk': _L1_xattn_in['bk'], 'L1_xattn_Wv': _L1_xattn_in['Wv'], 'L1_xattn_bv': _L1_xattn_in['bv'], 'L1_xattn_Wo': _L1_xattn_in['Wo'], 'L1_xattn_bo': _L1_xattn_in['bo'], 'L1_ffn_w1': _L1_ffn_in['w1'], 'L1_ffn_w2': _L1_ffn_in['w2']}

def reference(x, ctx_1024, L0_xattn_Wq, L0_xattn_bq, L0_xattn_Wk, L0_xattn_bk, L0_xattn_Wv, L0_xattn_bv, L0_xattn_Wo, L0_xattn_bo, L0_ffn_router_w, L0_ffn_gate_w, L0_ffn_up_w, L0_ffn_down_w, L1_xattn_Wq, L1_xattn_bq, L1_xattn_Wk, L1_xattn_bk, L1_xattn_Wv, L1_xattn_bv, L1_xattn_Wo, L1_xattn_bo, L1_ffn_w1, L1_ffn_w2):
    import jax
    import jax.numpy as jnp

    def _L0_xattn_ref(query, key, value, Wq, bq, Wk, bk, Wv, bv, Wo, bo):
        import jax, jax.numpy as jnp
        import numpy as np
        D_MODEL = 128
        NUM_HEADS = 16
        D_HEAD = D_MODEL // NUM_HEADS
        WINDOW = 128

        def _to_heads(x):
            B, S, _ = x.shape
            return x.reshape(B, S, NUM_HEADS, D_HEAD).transpose(0, 2, 1, 3)
        B, S, D = query.shape
        q = _to_heads(query @ Wq + bq)
        k = _to_heads(key @ Wk + bk)
        v = _to_heads(value @ Wv + bv)
        scores = jnp.einsum('bhqd,bhkd->bhqk', q, k) / jnp.sqrt(jnp.float32(D_HEAD))
        i = jnp.arange(S)[:, None]
        j = jnp.arange(S)[None, :]
        local_mask = jnp.abs(i - j) <= WINDOW // 2
        scores = jnp.where(local_mask[None, None], scores, -jnp.inf)
        attn = jax.nn.softmax(scores, axis=-1)
        ctx = jnp.einsum('bhqk,bhkd->bhqd', attn, v)
        ctx = ctx.transpose(0, 2, 1, 3).reshape(B, S, D)
        return ctx @ Wo + bo

    def _L0_ffn_ref(x, router_w, gate_w, up_w, down_w):
        import math
        import jax, jax.numpy as jnp
        from jax import lax
        import numpy as np
        E = 16
        K = 2
        CF = 1.25
        B, S, D = x.shape
        xf = x.reshape(-1, D)
        T = B * S
        capacity = max(1, math.ceil(T * K / E * CF))
        Cbuf = K * capacity
        logits = xf @ router_w
        probs = jax.nn.softmax(logits, axis=-1)
        w, idx = lax.top_k(probs, K)
        oh = jax.nn.one_hot(idx, E, dtype=w.dtype)
        rank = jnp.cumsum(oh, axis=0) - oh
        myrank = jnp.sum(rank * oh, axis=-1)
        keep = myrank < capacity
        w = jnp.where(keep, w, 0.0)
        flat_e = idx.reshape(-1)
        flat_w = w.reshape(-1)
        keep_f = keep.reshape(-1)
        tok = jnp.repeat(jnp.arange(T, dtype=jnp.int32), K)
        ohk = jax.nn.one_hot(flat_e, E, dtype=jnp.int32) * keep_f[:, None].astype(jnp.int32)
        pos = jnp.cumsum(ohk, axis=0) - ohk
        slot = jnp.sum(pos * ohk, axis=-1)
        e_idx = jnp.where(keep_f, flat_e, E)
        dispatch = jnp.full((E + 1, Cbuf), T, dtype=jnp.int32).at[e_idx, slot].set(tok)
        wbuf = jnp.zeros((E + 1, Cbuf), dtype=w.dtype).at[e_idx, slot].set(flat_w)
        dispatch = dispatch[:E]
        wbuf = wbuf[:E]
        x_pad = jnp.concatenate([xf, jnp.zeros((1, D), xf.dtype)], axis=0)
        xe = x_pad[dispatch]
        gate = jnp.einsum('ecd,edh->ech', xe, gate_w)
        up = jnp.einsum('ecd,edh->ech', xe, up_w)
        hidden = jax.nn.silu(gate) * up
        out = jnp.einsum('ech,ehd->ecd', hidden, down_w)
        out = out * wbuf[:, :, None]
        combined = jnp.zeros((T + 1, D), dtype=xf.dtype).at[dispatch.reshape(-1)].add(out.reshape(-1, D))
        return combined[:T].reshape(B, S, D)

    def _L1_xattn_ref(queries, keys, values, Wq, bq, Wk, bk, Wv, bv, Wo, bo):
        import jax, jax.numpy as jnp
        import numpy as np
        B, S, DM = (4, 256, 128)
        H, HD = (16, 64)
        b, s, _ = queries.shape

        def split(x):
            return x.reshape(b, s, H, HD).transpose(0, 2, 1, 3)
        q = split(queries @ Wq + bq)
        k = split(keys @ Wk + bk)
        v = split(values @ Wv + bv)
        attn = jnp.einsum('bhqd,bhkd->bhqk', q, k)
        attn = jax.nn.softmax(attn, axis=2) / jnp.sqrt(jnp.float32(HD))
        out = jnp.einsum('bhqk,bhkd->bhqd', attn, v)
        out = out.transpose(0, 2, 1, 3).reshape(b, s, H * HD)
        return out @ Wo + bo

    def _L1_ffn_ref(x, w1, w2):
        import jax, jax.numpy as jnp
        import numpy as np
        EMBED_DIM = 128
        HIDDEN = 4 * EMBED_DIM
        BATCH, SEQ = (4, 512)
        EPS = 1e-05

        def _quant_weight(w):
            s = jnp.clip(jnp.mean(jnp.abs(w)), EPS, None)
            wq = jnp.clip(jnp.round(w / s), -1.0, 1.0) * s
            return w + jax.lax.stop_gradient(wq - w)

        def _quant_act(x):
            scale = 127.0 / jnp.clip(jnp.max(jnp.abs(x), axis=-1, keepdims=True), EPS, None)
            xq = jnp.clip(jnp.round(x * scale), -128.0, 127.0) / scale
            return x + jax.lax.stop_gradient(xq - x)

        def _bitlinear(x, w):
            return jnp.einsum('bsi,oi->bso', _quant_act(x), _quant_weight(w))
        h = jax.nn.gelu(_bitlinear(x, w1), approximate=False)
        return _bitlinear(h, w2)
    x = x + _L0_xattn_ref(_layernorm(x, axis=-1), ctx_1024, ctx_1024, L0_xattn_Wq, L0_xattn_bq, L0_xattn_Wk, L0_xattn_bk, L0_xattn_Wv, L0_xattn_bv, L0_xattn_Wo, L0_xattn_bo)
    x = x + _L0_ffn_ref(_layernorm(x, axis=-1), L0_ffn_router_w, L0_ffn_gate_w, L0_ffn_up_w, L0_ffn_down_w)
    x = x + _L1_xattn_ref(_layernorm(x, axis=-1), ctx_1024, ctx_1024, L1_xattn_Wq, L1_xattn_bq, L1_xattn_Wk, L1_xattn_bk, L1_xattn_Wv, L1_xattn_bv, L1_xattn_Wo, L1_xattn_bo)
    x = x + _L1_ffn_ref(_layernorm(x, axis=-1), L1_ffn_w1, L1_ffn_w2)
    return x

_drawn_inputs = setup_inputs


def setup_inputs(seed=0):
    import zlib

    import numpy as np

    out = dict(_drawn_inputs(seed))
    spreads = {'L0_xattn_bq': (0.0, 0.322),
     'L0_xattn_bk': (0.0, 0.8),
     'L0_xattn_bv': (0.0, 0.1),
     'L0_xattn_bo': (0.0, 0.1),
     'L1_xattn_bq': (0.0, 0.8),
     'L1_xattn_bk': (0.0, 0.8),
     'L1_xattn_bv': (0.0, 0.8),
     'L1_xattn_bo': (0.0, 0.1)}
    factors = {'L0_ffn_router_w': 8.0,
     'L0_ffn_gate_w': 8.0,
     'L0_ffn_up_w': 8.0,
     'L0_ffn_down_w': 8.0,
     'L1_xattn_Wq': 8.0,
     'L1_xattn_Wk': 8.0,
     'L1_xattn_Wv': 6.372,
     'L1_xattn_Wo': 4.99}
    for name, (base, spread) in spreads.items():
        noise = np.random.default_rng([zlib.crc32(name.encode()), seed]).standard_normal(out[name].shape)
        drawn = base * np.exp(spread * noise) if base else spread * noise
        out[name] = jnp.asarray(drawn.astype(out[name].dtype))
    for name, factor in factors.items():
        out[name] = (out[name] * factor).astype(out[name].dtype)
    return out
```

```python
from contextlib import ExitStack

import concourse.bass as bass
from concourse import mybir

F32 = mybir.dt.float32
BF16 = mybir.dt.bfloat16
I32 = mybir.dt.int32
U32 = mybir.dt.uint32
ALU = mybir.AluOpType
ACT = mybir.ActivationFunctionType
AX = mybir.AxisListType

P = 128
S = 64
D = 128
E = 16
CAP = 640
REG = 2 * CAP + P
H0, D0 = 16, 8
H1, D1 = 16, 64
ZERO = E * REG
FF = 512
EPS = 1e-5
MAGIC = 12582912.0

C_ID, C_TRI, C_ONES = 0, 128, 256
C_MASK = 384
C_EVEN, C_ODD = 392, 393
C_IOTA = 394
C_BASE = 410
C_DROP = 427
C_HALF = 428
C_JOTA = 429
N_CONST = 512


def slot_tiles(tokens):
    return (2 * tokens + E * (P - 1)) // P + 1


def constants(tokens):
    import numpy as np

    c = np.zeros((P, N_CONST), np.float32)
    part = np.arange(P)
    c[:, C_ID:C_ID + P] = np.eye(P)
    c[:, C_TRI:C_TRI + P] = part[:, None] < part[None, :]
    c[:, C_ONES:C_ONES + P] = 1.0
    c[:, C_MASK:C_MASK + 8] = (part[:, None] % 64) // D0 == np.arange(8)[None, :]
    c[:, C_EVEN] = (part // D0) % 2 == 0
    c[:, C_ODD] = (part // D0) % 2 == 1
    c[:, C_IOTA:C_IOTA + E] = np.arange(E)
    c[:, C_BASE:C_BASE + E + 1] = np.arange(E + 1) * REG
    c[:, C_DROP] = ZERO + P + part
    c[:, C_HALF] = -0.5
    c[:, C_JOTA:C_JOTA + slot_tiles(tokens)] = np.arange(slot_tiles(tokens))
    return c


def ge(eng, sem, value):
    if isinstance(value, int) and value <= 0:
        return
    eng.wait_ge(sem, value)


def alone(eng, passed):
    eng.sem_inc(passed, 1)


class Tiles:

    def __init__(self, total, reg, const, unroll):
        self.total, self.reg, self.const, self.unroll = total, reg, const, unroll

    def at(self, off):
        k = self.const + off
        return (k if self.reg is None else self.reg * self.unroll + k), k % self.unroll

    def lap(self, off):
        k = (self.const + off) // self.unroll
        return k if self.reg is None else self.reg + k

    def has(self, off):
        return self.reg is not None or 0 <= self.const + off < self.total


def turns(eng, total, back, ahead, body, unroll=2):
    first = back + 4
    steady = max(0, (total - ahead - first) // unroll)
    for n in range(-ahead, first if steady else total + back):
        body(Tiles(total, None, n, unroll))
    if steady:
        with eng.Fori(0, steady) as i:
            for k in range(unroll):
                body(Tiles(total, i, first + k, unroll))
        for n in range(first + unroll * steady, total + back):
            body(Tiles(total, None, n, unroll))


class Steps:

    def __init__(self, eng, sem):
        self.eng, self.sem, self.before, self.k = eng, sem, 0, 0

    def turn(self, ts, total, kinds):
        if ts.reg is None:
            self.before = sum(c * max(0, min(total, ts.const + off)) for off, c in kinds.values())
        else:
            self.before = sum(c * (ts.const + off) for off, c in kinds.values()) + ts.reg * (ts.unroll * sum(c for _, c in kinds.values()))
        self.k = 0

    def did(self, kind, ins):
        ins.then_inc(self.sem, 1)
        self.k += 1
        self.eng.wait_ge(self.sem, self.before + self.k)


def cols(vec):
    return vec.rearrange("(p a) -> p a", a=1)


def spread(vec, n=P):
    return vec.partition_broadcast(n)


def one(ap, t):
    if isinstance(t, int):
        return ap[t]
    return ap[bass.ds(t, 1)].squeeze(0)


def mid(ap, t):
    if isinstance(t, int):
        return ap[:, t]
    return ap[:, bass.ds(t, 1)].squeeze(1)


def phase1(nc, NT, x_in, ctx_dup, consts_in, w, keep, xbuf):
    x_all, idx_all, w_all, counts = keep["x_all"], keep["idx_all"], keep["w_all"], keep["counts"]
    with ExitStack() as ctx:
        def sb(name, shape, dt=F32):
            return ctx.enter_context(nc.sbuf_tensor(name, shape, dt))

        def sem(name):
            return ctx.enter_context(nc.semaphore(name))

        cst = keep["cst"]
        ident = cst[:, C_ID:C_ID + P]
        wq, wk, wv, wo = (sb(f"p1_{n}", [D, D]) for n in ("wq", "wk", "wv", "wo"))
        wr = sb("p1_wr", [D, E])
        bq, bk = sb("p1_bq", [P, 1]), sb("p1_bk", [P, 1])
        bv, bo = sb("p1_bv", [P, D]), sb("p1_bo", [P, D])
        tri, ones = sb("p1_tri", [P, P], BF16), sb("p1_ones", [P, P], BF16)

        cT = [sb(f"p1_cT{i}", [D, 2, 2, S]) for i in range(2)]
        stat, mv, rstd = ([sb(f"p1_{n}{i}", [P, k]) for i in range(2)] for n, k in (("st", 6), ("mv", 2), ("rs", 1)))
        stat2, mv2, rstd2 = ([sb(f"p1_{n}{i}", [P, k]) for i in range(2)] for n, k in (("st2", 6), ("mv2", 2), ("rs2", 1)))
        xln = [sb(f"p1_xln{i}", [P, D]) for i in range(2)]
        xT = [sb(f"p1_xT{i}", [D, P]) for i in range(2)]
        qT = [sb(f"p1_qT{i}", [P, 2, S]) for i in range(2)]
        kT = [sb(f"p1_kT{i}", [P, 2, S]) for i in range(2)]
        qm = [sb(f"p1_qm{i}", [P, 2, 8, S]) for i in range(2)]
        pr = [sb(f"p1_pr{i}", [P, 2, 8, S]) for i in range(2)]
        mx, sm, rc = ([sb(f"p1_{n}{i}", [P, 16]) for i in range(2)] for n in ("mx", "sm", "rc"))
        pT = [sb(f"p1_pT{i}", [P, 2, 4, P]) for i in range(2)]
        vb = [sb(f"p1_vb{i}", [P, 2, 4, 4, D0]) for i in range(2)]
        od = sb("p1_od", [P, 2, S])
        oT = [sb(f"p1_oT{i}", [P, 2, S]) for i in range(2)]
        x2 = [sb(f"p1_x2{i}", [P, D]) for i in range(2)]
        x2T = [sb(f"p1_x2T{i}", [D, P]) for i in range(2)]
        lg = [sb(f"p1_lg{i}", [P, 24]) for i in range(2)]
        ex = [sb(f"p1_ex{i}", [P, 24]) for i in range(2)]
        i8 = sb("p1_i8", [P, 8], U32)
        nm0, idf, z, wk2 = sb("p1_nm0", [P, 1]), sb("p1_idf", [P, 2]), sb("p1_z", [P, 1]), sb("p1_wk2", [P, 2])
        oh = [sb(f"p1_oh{i}", [P, 2, E], BF16) for i in range(2)]
        carry = [sb(f"p1_carry{i}", [P, 2, E]) for i in range(2)]
        rk, cl, slot = sb("p1_rk", [P, 2, E]), sb("p1_cl", [P, 2, E]), sb("p1_slot", [P, E])
        mm, red, kp, pos = sb("p1_mm", [P, 4, E]), sb("p1_red", [P, 4]), sb("p1_kp", [P, 2]), sb("p1_pos", [P, 2])
        idx = [sb(f"p1_idx{i}", [P, 2], I32) for i in range(2)]

        ps_s = ctx.enter_context(nc.psum_tensor("ps_s", [P, 2, 8, S], F32))
        ps_p = ctx.enter_context(nc.psum_tensor("ps_p", [P, 2, 4, P], F32))
        ps_x = ctx.enter_context(nc.psum_tensor("ps_x", [P, 4, P], F32))
        ps_q = ctx.enter_context(nc.psum_tensor("ps_q", [P, 4, P], F32))
        ps_v = ctx.enter_context(nc.psum_tensor("ps_v", [P, 512], F32))
        ps_o = ctx.enter_context(nc.psum_tensor("ps_o", [P, 4, P], F32))

        w_in = sem("w_in"); x_ld = sem("x_ld"); c_ld = [sem(f"c_ld{i}") for i in range(2)]
        setup = sem("setup")
        mv_done, rs_done, xln_done = sem("mv_done"), sem("rs_done"), sem("xln_done")
        turned_x, xT_done = sem("turned_x"), sem("xT_done")
        qk_mm, qk_done = sem("qk_mm"), sem("qk_done")
        v_mm, vb_done = sem("v_mm"), sem("vb_done")
        qm_done, s_mm, sub_done, exp_done = sem("qm_done"), sem("s_mm"), sem("sub_done"), sem("exp_done")
        rc_done, pr_done, turned_p, pT_done = sem("rc_done"), sem("pr_done"), sem("turned_p"), sem("pT_done")
        o_mm, oT_done, ao_mm, x1_done = sem("o_mm"), sem("oT_done"), sem("ao_mm"), sem("x1_done")
        mv2_done, rs2_done, x2_done = sem("mv2_done"), sem("rs2_done"), sem("x2_done")
        turned_x2, x2T_done, lg_mm, top_done = sem("turned_x2"), sem("x2T_done"), sem("lg_mm"), sem("top_done")
        rexp_done, oh_done, rk_mm, rk_done = sem("rexp_done"), sem("oh_done"), sem("rk_mm"), sem("rk_done")
        idx_done, idx_kept = sem("idx_done"), sem("idx_kept")
        sc = [sem(f"scattered{i}") for i in range(2)]
        v_step, g_step = sem("v_step"), sem("g_step")
        passed = sem("passed")
        block = ctx.enter_context(nc.Block())

        XG = 4
        xg = x_in.rearrange("(g t p) d -> g p t d", t=XG, p=P)

        @block.sync
        def _(sp):
            sp.dma_start(cst[:, :], consts_in).then_inc(w_in, 16)
            for n, g in enumerate(range(NT // XG)):
                sp.dma_start(x_all[:, g * XG:(g + 1) * XG, :], xg[g]).then_inc(x_ld, 16)
                if n == 0:
                    for dst, src in ((wq, w["wq"]), (wk, w["wk"]), (wv, w["wv"]), (wo, w["wo"]), (wr, w["wr"]),
                                     (bq, cols(w["bq"])), (bk, cols(w["bk"])), (bv, spread(w["bv"])), (bo, spread(w["bo"]))):
                        sp.dma_start(dst[:, :], src).then_inc(w_in, 16)

            def turn(ts):
                if ts.has(3):
                    t, p = ts.at(3)
                    ge(sp, v_mm, t - 1)
                    sp.dma_start(cT[p][:, :, :, :], one(ctx_dup, t)).then_inc(c_ld[p], 16)
            turns(sp, NT, 2, 4, turn)

        @block.tensor
        def _(pe):
            pe.wait_ge(w_in, 160)
            pe.wait_ge(x_ld, 16 * (NT // XG))
            pe.wait_ge(setup, 2)

            def turn(ts):
                if ts.has(0):
                    t, p = ts.at(0)
                    pe.wait_ge(qm_done, t + 1)
                    pe.wait_ge(qk_done, 2 * t + 2)
                    for r in range(2):
                        ge(pe, sub_done, 2 * t - 1 + r)
                        for b in range(2):
                            for j in range(4):
                                last = pe.matmul(ps_s[:, r, 4 * b + j, :], qm[p][64 * r:64 * r + 64, b, 2 * j:2 * j + 2, :],
                                                 kT[p][64 * r:64 * r + 64, b, :], start=True, stop=True)
                        last.then_inc(s_mm, 1)
                if ts.has(-2):
                    t, p = ts.at(-2)
                    pe.wait_ge(x2_done, t + 1)
                    pe.wait_ge(xT_done, (t + 5) if not isinstance(t, int) else min(t + 5, NT))
                    pe.transpose(ps_x[:, 1, :], x2[p][:, :], ident).then_inc(turned_x2, 1)
                if ts.has(-1):
                    t, p = ts.at(-1)
                    pe.wait_ge(pr_done, t + 1)
                    for r in range(2):
                        ge(pe, pT_done, 2 * t - 1 + r)
                        for c in range(4):
                            last = pe.transpose(ps_p[:, r, c, :], pr[p][:, r, 2 * c:2 * c + 2, :], ident)
                        last.then_inc(turned_p, 1)
                if ts.has(-2):
                    t, p = ts.at(-2)
                    pe.wait_ge(x2T_done, t + 1)
                    pe.wait_ge(vb_done, (t + 3) if not isinstance(t, int) else min(t + 3, NT))
                    pe.matmul(ps_v[:, 256:272], x2T[p][:, :], wr[:, :], start=True, stop=True).then_inc(lg_mm, 1)
                if ts.has(-1):
                    t, p = ts.at(-1)
                    ge(pe, x1_done, t)
                    for r in range(2):
                        pe.wait_ge(pT_done, 2 * t + 1 + r)
                        for b in range(2):
                            for jp in range(2):
                                g = 2 * r + jp
                                last = pe.matmul(ps_o[32 * g:32 * g + 32, b, :], vb[p][:, b, g, :, :], pT[p][:, r, 2 * b + jp, :],
                                                 start=True, stop=True)
                    last.then_inc(o_mm, 1)
                if ts.has(-2):
                    t, p = ts.at(-2)
                    pe.wait_ge(oh_done, t + 1)
                    pe.matmul(ps_v[:, 272:304], tri[:, :], oh[p][:, :, :], start=True, stop=True)
                    pe.matmul(ps_v[:, 304:336], ones[:, :], oh[p][:, :, :], start=True, stop=True).then_inc(rk_mm, 1)
                if ts.has(2):
                    t, p = ts.at(2)
                    pe.wait_ge(xT_done, t + 1)
                    ge(pe, qk_done, 2 * t)
                    pe.wait_ge(c_ld[p], (ts.lap(2) + 1) * 16)
                    pe.matmul(ps_q[:, 0, :], wq[:, :], xT[p][:, :], start=True, stop=True)
                    pe.matmul(ps_q[:, 1, :], wk[:, :], cT[p][:, :, 0, :], start=True, stop=True).then_inc(qk_mm, 1)
                if ts.has(1):
                    t, p = ts.at(1)
                    ge(pe, vb_done, t)
                    ge(pe, rk_done, t - 2)
                    for b in range(2):
                        last = pe.matmul(ps_v[:, 128 * b:128 * b + 128], cT[p][:, b, :, :], wv[:, :], start=True, stop=True)
                    last.then_inc(v_mm, 1)
                if ts.has(-1):
                    t, p = ts.at(-1)
                    pe.wait_ge(oT_done, t + 1)
                    pe.matmul(ps_o[:, 2, :], oT[p][:, :, :], wo[:, :], start=True, stop=True).then_inc(ao_mm, 1)
                if ts.has(3):
                    t, p = ts.at(3)
                    pe.wait_ge(xln_done, t + 1)
                    ge(pe, x2T_done, t - 4)
                    pe.transpose(ps_x[:, 0, :], xln[p][:, :], ident).then_inc(turned_x, 1)
            turns(pe, NT, 2, 4, turn)

        @block.scalar
        def _(act):
            act.wait_ge(w_in, 160)

            def turn(ts):
                if ts.has(-2):
                    t, p = ts.at(-2)
                    act.wait_ge(turned_x2, t + 1)
                    ge(act, lg_mm, t - 1)
                    act.activation(x2T[p][:, :], ps_x[:, 1, :], ACT.Copy).then_inc(x2T_done, 1)
                if ts.has(-1):
                    t, p = ts.at(-1)
                    ge(act, o_mm, t - 1)
                    for r in range(2):
                        act.wait_ge(turned_p, 2 * t + 1 + r)
                        act.activation(pT[p][:, r, :, :], ps_p[:, r, :, :], ACT.Copy).then_inc(pT_done, 1)
                if ts.has(0):
                    t, p = ts.at(0)
                    for r in range(2):
                        act.wait_ge(sub_done, 2 * t + 1 + r)
                        act.activation(pr[p][:, r, :, :], pr[p][:, r, :, :], ACT.Exp, scale=D0 ** -0.5).then_inc(exp_done, 1)
                if ts.has(-2):
                    t, p = ts.at(-2)
                    act.wait_ge(top_done, t + 1)
                    act.activation(ex[p][:, :], lg[p][:, :], ACT.Exp, bias=nm0[:, :]).then_inc(rexp_done, 1)
                if ts.has(2):
                    t, p = ts.at(2)
                    act.wait_ge(qk_mm, t + 1)
                    ge(act, qm_done, t - 1)
                    ge(act, s_mm, 2 * t - 2)
                    act.activation(qT[p][:, :, :], ps_q[:, 0, :], ACT.Identity, bias=bq[:, :]).then_inc(qk_done, 1)
                    act.activation(kT[p][:, :, :], ps_q[:, 1, :], ACT.Identity, bias=bk[:, :]).then_inc(qk_done, 1)
                if ts.has(3):
                    t, p = ts.at(3)
                    act.wait_ge(turned_x, t + 1)
                    ge(act, qk_mm, t - 1)
                    act.activation(xT[p][:, :], ps_x[:, 0, :], ACT.Copy).then_inc(xT_done, 1)
            turns(act, NT, 2, 4, turn)

        @block.gpsimd
        def _(g):
            g.wait_ge(w_in, 160)
            half = cst[:, C_HALF:C_HALF + 1]
            mask = cst[:, C_MASK:C_MASK + 8]
            steps = Steps(g, g_step)

            def turn(ts):
                steps.turn(ts, NT, {"eps": (4, 1), "eps2": (-1, 1)})
                if ts.has(1):
                    t, p = ts.at(1)
                    g.wait_ge(qk_done, 2 * t + 1)
                    ge(g, s_mm, 2 * t - 2)
                    g.tensor_tensor(qm[p][:, :, :, :], qT[p][:, :, :].unsqueeze(2).broadcast_to([P, 2, 8, S]),
                                    mask.unsqueeze(1).unsqueeze(3).broadcast_to([P, 2, 8, S]), ALU.mult).then_inc(qm_done, 1)
                if ts.has(4):
                    t, p = ts.at(4)
                    g.wait_ge(mv_done, t + 1)
                    ge(g, xln_done, t - 1)
                    alone(g, passed)
                    steps.did("eps", g.tensor_scalar(rstd[p][:, :], mv[p][:, 1:2], EPS, None, ALU.add))
                    g.tensor_tensor(rstd[p][:, :], rstd[p][:, :], half, ALU.pow).then_inc(rs_done, 1)
                if ts.has(0):
                    t, p = ts.at(0)
                    g.wait_ge(rc_done, t + 1)
                    g.tensor_tensor(pr[p][:, :, :, :], pr[p][:, :, :, :],
                                    rc[p][:, :].rearrange("p (r c) -> p r c", r=2).unsqueeze(3).broadcast_to([P, 2, 8, S]),
                                    ALU.mult).then_inc(pr_done, 1)
                if ts.has(-1):
                    t, p = ts.at(-1)
                    g.wait_ge(mv2_done, t + 1)
                    ge(g, x2_done, t - 1)
                    alone(g, passed)
                    steps.did("eps2", g.tensor_scalar(rstd2[p][:, :], mv2[p][:, 1:2], EPS, None, ALU.add))
                    g.tensor_tensor(rstd2[p][:, :], rstd2[p][:, :], half, ALU.pow).then_inc(rs2_done, 1)
                if ts.has(-2):
                    t, p = ts.at(-2)
                    g.wait_ge(idx_done, t + 1)
                    for k in range(2):
                        alone(g, passed)
                        g.indirect_dma_start(xbuf, bass.IndirectOffsetOnAxis(ap=idx[p][:, k:k + 1], axis=0), x2[p][:, :], None
                                             ).then_inc(sc[p], 16)
                    g.tensor_copy(mid(idx_all, t), idx[p][:, :]).then_inc(idx_kept, 1)

            turns(g, NT, 2, 4, turn)
            for p in range(2):
                g.wait_ge(sc[p], 32 * (NT // 2))

        @block.vector
        def _(v):
            v.wait_ge(w_in, 160)
            v.wait_ge(x_ld, 16 * (NT // XG))
            for p in range(2):
                v.memset(vb[p][:, :, :, :, :], 0.0)
            v.memset(carry[0][:, :, :], 0.0)
            v.tensor_copy(tri[:, :], cst[:, C_TRI:C_TRI + P]).then_inc(setup, 1)
            v.tensor_copy(ones[:, :], cst[:, C_ONES:C_ONES + P]).then_inc(setup, 1)
            v.wait_ge(setup, 2)
            iota = cst[:, C_IOTA:C_IOTA + E]
            base = cst[:, C_BASE:C_BASE + E]
            drop = cst[:, C_DROP:C_DROP + 1]
            even, odd = cst[:, C_EVEN:C_EVEN + 1], cst[:, C_ODD:C_ODD + 1]
            steps = Steps(v, v_step)

            def turn(ts):
                steps.turn(ts, NT, {"max": (0, 2), "sum": (0, 1), "top": (-2, 6), "od": (-1, 1), "rank": (-2, 9),
                                    "st2": (-1, 1), "st": (4, 1)})
                if ts.has(0):
                    t, p = ts.at(0)
                    ge(v, turned_p, 2 * t - 2)
                    for r in range(2):
                        v.wait_ge(s_mm, 2 * t + 1 + r)
                        m = mx[p][:, 8 * r:8 * r + 8]
                        steps.did("max", v.tensor_reduce(m, ps_s[:, r, :, :], AX.X, ALU.max))
                        v.tensor_tensor(pr[p][:, r, :, :], ps_s[:, r, :, :], m.unsqueeze(2).broadcast_to([P, 8, S]),
                                        ALU.subtract).then_inc(sub_done, 1)
                if ts.has(-2):
                    t, p = ts.at(-2)
                    v.wait_ge(lg_mm, t + 1)
                    ge(v, rexp_done, t)
                    steps.did("top", v.tensor_copy(lg[p][:, 0:16], ps_v[:, 256:272]))
                    alone(v, passed)
                    steps.did("top", v.max(lg[p][:, 16:24], lg[p][:, 0:16]))
                    v.tensor_scalar(nm0[:, :], lg[p][:, 16:17], -1.0, None, ALU.mult).then_inc(top_done, 1)
                    steps.did("top", v.max_index(i8[:, :], lg[p][:, 16:24], lg[p][:, 0:16]))
                    steps.did("top", v.tensor_copy(idf[:, :], i8[:, 0:2]))
                    v.tensor_tensor(oh[p][:, :, :], iota.unsqueeze(1).broadcast_to([P, 2, E]),
                                    idf[:, :].unsqueeze(2).broadcast_to([P, 2, E]), ALU.is_equal).then_inc(oh_done, 1)
                if ts.has(-1):
                    t, p = ts.at(-1)
                    v.wait_ge(o_mm, t + 1)
                    ge(v, ao_mm, t - 1)
                    steps.did("od", v.tensor_scalar(od[:, :, :], ps_o[:, 0:2, S:2 * S], odd, None, ALU.mult))
                    v.scalar_tensor_tensor(oT[p][:, :, :], ps_o[:, 0:2, 0:S], even, od[:, :, :], ALU.mult, ALU.add).then_inc(oT_done, 1)
                if ts.has(-2):
                    t, p = ts.at(-2)
                    v.wait_ge(rexp_done, t + 1)
                    steps.did("top", v.reduce_sum(z[:, :], ex[p][:, 0:16], AX.X))
                    steps.did("top", v.reciprocal(z[:, :], z[:, :]))
                if ts.has(-2):
                    t, p = ts.at(-2)
                    v.wait_ge(rk_mm, t + 1)
                    v.wait_ge(oh_done, t + 1)
                    ge(v, rk_done, t)
                    steps.did("rank", v.tensor_tensor(rk[:, :, :], ps_v[:, 272:304].rearrange("p (k e) -> p k e", k=2), carry[p][:, :, :], ALU.add))
                    v.tensor_tensor(carry[1 - p][:, :, :], ps_v[:, 304:336].rearrange("p (k e) -> p k e", k=2), carry[p][:, :, :],
                                    ALU.add).then_inc(rk_done, 1)
                    steps.did("rank", v.tensor_scalar(cl[:, :, :], rk[:, :, :], float(CAP), None, ALU.min))
                    steps.did("rank", v.tensor_tensor(slot[:, :], cl[:, 0, :], cl[:, 1, :], ALU.add))
                    steps.did("rank", v.tensor_tensor(slot[:, :], slot[:, :], base, ALU.add))
                    v.tensor_tensor(mm[:, 0:2, :], oh[p][:, :, :], rk[:, :, :], ALU.mult)
                    steps.did("rank", v.tensor_tensor(mm[:, 2:4, :], oh[p][:, :, :], slot[:, :].unsqueeze(1).broadcast_to([P, 2, E]), ALU.mult))
                    steps.did("rank", v.reduce_sum(red[:, :], mm[:, :, :], AX.X))
                    steps.did("rank", v.tensor_scalar(kp[:, :], red[:, 0:2], float(CAP), None, ALU.is_lt))
                    steps.did("rank", v.scalar_tensor_tensor(wk2[:, :], ex[p][:, 16:18], z[:, :], kp[:, :], ALU.mult, ALU.mult))
                    v.tensor_copy(mid(w_all, t), wk2[:, :])
                    steps.did("rank", v.scalar_tensor_tensor(pos[:, :], red[:, 2:4], drop, kp[:, :], ALU.subtract, ALU.mult))
                    ge(v, sc[p], ts.lap(-2) * 32)
                    ge(v, idx_kept, t - 1)
                    v.tensor_scalar(idx[p][:, :], pos[:, :], drop, None, ALU.add).then_inc(idx_done, 1)
                if ts.has(1):
                    t, p = ts.at(1)
                    v.wait_ge(v_mm, t + 1)
                    ge(v, o_mm, t - 1)
                    for jx in range(2):
                        rows = slice(64 * jx, 64 * jx + 64)
                        ins = v.tensor_tensor(
                            vb[p][rows, :, :, 2 * jx:2 * jx + 2, :].rearrange("p b g h d -> p b g (h d)"),
                            ps_v[rows, 0:256].rearrange("p (b g c) -> p b g c", b=2, g=4)[:, :, :, 16 * jx:16 * jx + 16],
                            bv[rows, :].rearrange("p (g c) -> p g c", g=4)[:, :, 16 * jx:16 * jx + 16].unsqueeze(1).broadcast_to([64, 2, 4, 16]),
                            ALU.add)
                    ins.then_inc(vb_done, 1)
                if ts.has(0):
                    t, p = ts.at(0)
                    v.wait_ge(exp_done, 2 * t + 2)
                    ge(v, pr_done, t - 1)
                    steps.did("sum", v.reduce_sum(sm[p][:, :], pr[p][:, :, :, :].rearrange("p r c k -> p (r c) k"), AX.X))
                    v.reciprocal(rc[p][:, :], sm[p][:, :]).then_inc(rc_done, 1)
                if ts.has(-1):
                    t, p = ts.at(-1)
                    v.wait_ge(ao_mm, t + 1)
                    v.tensor_tensor(mid(x_all, t), ps_o[:, 2, :], mid(x_all, t), ALU.add).then_inc(x1_done, 1)
                    v.wait_ge(x1_done, t + 1)
                    alone(v, passed)
                    steps.did("st2", v.bn_stats(stat2[p][:, :], mid(x_all, t)))
                    alone(v, passed)
                    v.bn_aggr(mv2[p][:, :], stat2[p][:, :]).then_inc(mv2_done, 1)
                if ts.has(4):
                    t, p = ts.at(4)
                    alone(v, passed)
                    steps.did("st", v.bn_stats(stat[p][:, :], mid(x_all, t)))
                    alone(v, passed)
                    v.bn_aggr(mv[p][:, :], stat[p][:, :]).then_inc(mv_done, 1)
                if ts.has(4):
                    t, p = ts.at(4)
                    v.wait_ge(rs_done, t + 1)
                    ge(v, turned_x, t - 1)
                    v.tensor_scalar(xln[p][:, :], mid(x_all, t), mv[p][:, 0:1], rstd[p][:, :], ALU.subtract, ALU.mult).then_inc(xln_done, 1)
                    v.wait_ge(xln_done, t + 1)
                    v.tensor_tensor(mid(x_all, t), mid(x_all, t), bo[:, :], ALU.add)
                if ts.has(-1):
                    t, p = ts.at(-1)
                    v.wait_ge(rs2_done, t + 1)
                    ge(v, turned_x2, t - 1)
                    ge(v, sc[p], ts.lap(-1) * 32)
                    v.tensor_scalar(x2[p][:, :], mid(x_all, t), mv2[p][:, 0:1], rstd2[p][:, :], ALU.subtract, ALU.mult).then_inc(x2_done, 1)
            turns(v, NT, 2, 4, turn)
            v.wait_ge(rk_done, NT)
            v.tensor_copy(counts[:, :, :], carry[NT % 2][:, :, :])


def phase2(nc, NT, wg, wd_in, keep, xbuf, ybuf):
    NS = slot_tiles(NT * P)
    cst, counts, idx_all = keep["cst"], keep["counts"], keep["idx_all"]
    U = 4
    with ExitStack() as ctx:
        def sb(name, shape, dt=F32):
            return ctx.enter_context(nc.sbuf_tensor(name, shape, dt))

        def sem(name):
            return ctx.enter_context(nc.semaphore(name))

        ident = cst[:, C_ID:C_ID + P]
        gu = sb("p2_gu", [D, E * 2 * P])
        dn = sb("p2_dn", [P, E * D])
        zeros = sb("p2_zeros", [P, D])
        n2, nn = sb("p2_n2", [P, 2, E]), sb("p2_nn", [P, E])
        ni, nsh = sb("p2_ni", [P, E], I32), sb("p2_nsh", [P, E], I32)
        nt, end, tail = sb("p2_nt", [P, E]), sb("p2_end", [P, E]), sb("p2_tail", [P, E], I32)
        past, spent = sb("p2_past", [P, NS, E]), sb("p2_spent", [P, NS, E])
        ef, sf, rf = sb("p2_ef", [P, NS]), sb("p2_sf", [P, NS]), sb("p2_rf", [P, NS])
        row_in, who = (sb(f"p2_{n}", [P, NS], I32) for n in ("row_in", "who"))
        shift, jump = sb("p2_shift", [P, E + 1]), sb("p2_jump", [P, E + 1])
        slot_f, moved = sb("p2_slotf", [P, NT * 2]), sb("p2_moved", [P, NT * 2])
        behind = sb("p2_behind", [P, NT * 2, E + 1])
        xe = [sb(f"p2_xe{i}", [P, D]) for i in range(U)]
        xT = [sb(f"p2_xT{i}", [D, P]) for i in range(2)]
        sg = [sb(f"p2_sg{i}", [P, P]) for i in range(2)]
        hh = [sb(f"p2_h{i}", [P, P]) for i in range(2)]
        hT = [sb(f"p2_hT{i}", [P, P]) for i in range(2)]
        ye = [sb(f"p2_ye{i}", [P, D]) for i in range(U)]
        ps_x, ps_g, ps_h, ps_y = ([ctx.enter_context(nc.psum_tensor(f"p2_{n}{i}", [P, 512], F32)) for i in range(2)]
                                  for n in ("psx", "psg", "psh", "psy"))

        zeroed, w_in, tabled, tails = sem("zeroed"), sem("w2_in"), sem("tabled"), sem("tails")
        x_ld = [sem(f"xe_ld{i}") for i in range(U)]
        y_st = [sem(f"ye_st{i}") for i in range(U)]
        x_mm, xT_done, g_mm, sg_done, h_done, h_mm, hT_done, y_mm, y_done = (
            sem(n) for n in ("x_mm", "xT2_done", "g_mm", "sg_done", "h_done", "h_mm", "hT_done", "y_mm", "y_done"))
        v_step = sem("v_step2")
        passed = sem("passed")
        block = ctx.enter_context(nc.Block())

        @block.sync
        def _(sp):
            sp.wait_ge(zeroed, 1)
            sp.dma_start(xbuf[ZERO:ZERO + P, :], zeros[:, :]).then_inc(tails, 16)
            sp.dma_start(ybuf[NS * P:NS * P + P, :], zeros[:, :]).then_inc(tails, 16)
            sp.wait_ge(tabled, 1)
            with sp.Fori(0, E) as e:
                r = sp.value_load(tail[0:1, bass.ds(e, 1)], min_val=0, max_val=ZERO - P)
                sp.dma_start(xbuf[bass.ds(r, P), :], zeros[:, :]).then_inc(tails, 16)
            sp.wait_ge(tails, 16 * (E + 2))

            def turn(ts):
                if ts.has(2):
                    t, p = ts.at(2)
                    ge(sp, x_mm, t - U + 1)
                    r = sp.value_load(row_in[0:1, t:t + 1] if isinstance(t, int) else row_in[0:1, bass.ds(t, 1)], min_val=0, max_val=ZERO)
                    sp.dma_start(xe[p][:, :], xbuf[bass.ds(r, P), :]).then_inc(x_ld[p], 16)
                if ts.has(-3):
                    t, p = ts.at(-3)
                    sp.wait_ge(y_done, t + 1)
                    sp.dma_start(one(ybuf[0:NS * P, :].rearrange("(t p) d -> t p d", p=P), t), ye[p][:, :]).then_inc(y_st[p], 16)
            turns(sp, NS, 3, 2, turn, U)
            for p in range(U):
                sp.wait_ge(y_st[p], 16 * ((NS - p + U - 1) // U))

        @block.gpsimd
        def _(g):
            g.memset(zeros[:, :], 0.0).then_inc(zeroed, 1)

        @block.tensor
        def _(pe):
            pe.wait_ge(w_in, 48)
            pe.wait_ge(tabled, 1)

            def turn(ts):
                if ts.has(1):
                    t, p = ts.at(1)
                    pe.wait_ge(x_ld[p], (ts.lap(1) + 1) * 16)
                    ge(pe, xT_done, t - 1)
                    pe.transpose(ps_x[p % 2][:, 0:P], xe[p][:, :], ident).then_inc(x_mm, 1)
                if ts.has(0):
                    t, p = ts.at(0)
                    pe.wait_ge(xT_done, t + 1)
                    ge(pe, h_done, t - 1)
                    alone(pe, passed)
                    e = pe.value_load(who[0:1, t:t + 1] if isinstance(t, int) else who[0:1, bass.ds(t, 1)], min_val=0, max_val=E - 1)
                    pe.matmul(ps_g[p % 2][:, 0:2 * P], xT[p % 2][:, :], gu[:, bass.ds(e * (2 * P), 2 * P)],
                              start=True, stop=True).then_inc(g_mm, 1)
                if ts.has(-1):
                    t, p = ts.at(-1)
                    pe.wait_ge(h_done, t + 1)
                    ge(pe, hT_done, t - 1)
                    pe.transpose(ps_h[p % 2][:, 0:P], hh[p % 2][:, :], ident).then_inc(h_mm, 1)
                if ts.has(-2):
                    t, p = ts.at(-2)
                    pe.wait_ge(hT_done, t + 1)
                    ge(pe, y_done, t - 1)
                    alone(pe, passed)
                    e = pe.value_load(who[0:1, t:t + 1] if isinstance(t, int) else who[0:1, bass.ds(t, 1)], min_val=0, max_val=E - 1)
                    pe.matmul(ps_y[p % 2][:, 0:D], hT[p % 2][:, :], dn[:, bass.ds(e * D, D)], start=True, stop=True).then_inc(y_mm, 1)
            turns(pe, NS, 3, 2, turn, U)

        @block.scalar
        def _(act):
            act.dma_start(gu[:, :].rearrange("d (e h) -> d e h", e=E)[:, :, 0:P], wg[0]).then_inc(w_in, 16)
            act.dma_start(gu[:, :].rearrange("d (e h) -> d e h", e=E)[:, :, P:2 * P], wg[1]).then_inc(w_in, 16)
            act.dma_start(dn[:, :].rearrange("h (e d) -> h e d", e=E), wd_in).then_inc(w_in, 16)

            def turn(ts):
                if ts.has(1):
                    t, p = ts.at(1)
                    act.wait_ge(x_mm, t + 1)
                    ge(act, g_mm, t - 1)
                    act.activation(xT[p % 2][:, :], ps_x[p % 2][:, 0:P], ACT.Copy).then_inc(xT_done, 1)
                if ts.has(0):
                    t, p = ts.at(0)
                    act.wait_ge(g_mm, t + 1)
                    ge(act, h_done, t - 1)
                    act.activation(sg[p % 2][:, :], ps_g[p % 2][:, 0:P], ACT.Silu).then_inc(sg_done, 1)
            turns(act, NS, 3, 2, turn, U)

        @block.vector
        def _(v):
            done = [0]

            def step(ins):
                ins.then_inc(v_step, 1)
                done[0] += 1
                v.wait_ge(v_step, done[0])

            step(v.tensor_scalar(n2[:, :, :], counts[:, :, :], float(CAP), None, ALU.min))
            step(v.tensor_tensor(nn[:, :], n2[:, 0, :], n2[:, 1, :], ALU.add))
            v.tensor_tensor(tail[:, :], nn[:, :], cst[:, C_BASE:C_BASE + E], ALU.add)
            step(v.tensor_scalar(ni[:, :], nn[:, :], float(P - 1), None, ALU.add))
            step(v.tensor_single_scalar(nsh[:, :], ni[:, :], 7, ALU.logical_shift_right))
            step(v.tensor_copy(nt[:, :], nsh[:, :]))
            step(v.tensor_tensor_scan(end[:, :], cst[:, C_ONES:C_ONES + E], nt[:, :], 0.0, ALU.mult, ALU.add))
            jota = cst[:, C_JOTA:C_JOTA + NS]
            step(v.tensor_tensor(past[:, :, :], jota.unsqueeze(2).broadcast_to([P, NS, E]),
                                 end[:, :].unsqueeze(1).broadcast_to([P, NS, E]), ALU.is_ge))
            step(v.tensor_tensor(spent[:, :, :], past[:, :, :], nt[:, :].unsqueeze(1).broadcast_to([P, NS, E]), ALU.mult))
            step(v.reduce_sum(ef[:, :], past[:, :, :], AX.X))
            step(v.reduce_sum(sf[:, :], spent[:, :, :], AX.X))
            step(v.tensor_tensor(sf[:, :], jota, sf[:, :], ALU.subtract))
            step(v.tensor_scalar(sf[:, :], sf[:, :], float(P), None, ALU.mult))
            step(v.scalar_tensor_tensor(rf[:, :], ef[:, :], float(REG), sf[:, :], ALU.mult, ALU.add))
            step(v.tensor_scalar(row_in[:, :], rf[:, :], float(ZERO), None, ALU.min))
            v.tensor_scalar(who[:, :], ef[:, :], float(E - 1), None, ALU.min).then_inc(tabled, 1)
            base = cst[:, C_BASE:C_BASE + E + 1]
            v.memset(shift[:, E:E + 1], float(NS * P - ZERO - P))
            step(v.tensor_tensor(nt[:, :], end[:, :], nt[:, :], ALU.subtract))
            step(v.scalar_tensor_tensor(shift[:, 0:E], nt[:, :], float(P), base[:, 0:E], ALU.mult, ALU.subtract))
            step(v.tensor_copy(jump[:, 0:1], shift[:, 0:1]))
            step(v.tensor_tensor(jump[:, 1:E + 1], shift[:, 1:E + 1], shift[:, 0:E], ALU.subtract))
            step(v.tensor_copy(slot_f[:, :], idx_all[:, :, :]))
            step(v.tensor_tensor(behind[:, :, :], slot_f[:, :].unsqueeze(2).broadcast_to([P, NT * 2, E + 1]),
                                 base.unsqueeze(1).broadcast_to([P, NT * 2, E + 1]), ALU.is_ge))
            step(v.tensor_tensor(behind[:, :, :], behind[:, :, :], jump[:, :].unsqueeze(1).broadcast_to([P, NT * 2, E + 1]), ALU.mult))
            step(v.reduce_sum(moved[:, :], behind[:, :, :], AX.X))
            v.tensor_tensor(idx_all[:, :, :], slot_f[:, :], moved[:, :], ALU.add)

            def turn(ts):
                if ts.has(0):
                    t, p = ts.at(0)
                    v.wait_ge(sg_done, t + 1)
                    ge(v, h_mm, t - 1)
                    v.tensor_tensor(hh[p % 2][:, :], ps_g[p % 2][:, P:2 * P], sg[p % 2][:, :], ALU.mult).then_inc(h_done, 1)
                if ts.has(-1):
                    t, p = ts.at(-1)
                    v.wait_ge(h_mm, t + 1)
                    ge(v, y_mm, t - 1)
                    v.tensor_copy(hT[p % 2][:, :], ps_h[p % 2][:, 0:P]).then_inc(hT_done, 1)
                if ts.has(-2):
                    t, p = ts.at(-2)
                    v.wait_ge(y_mm, t + 1)
                    ge(v, y_st[p], ts.lap(-2) * 16)
                    v.tensor_copy(ye[p][:, :], ps_y[p % 2][:, 0:D]).then_inc(y_done, 1)
            turns(v, NS, 3, 2, turn, U)


def phase3(nc, NT, ctxT_in, w, keep, ybuf):
    cst, x_all, idx_all, w_all = keep["cst"], keep["x_all"], keep["idx_all"], keep["w_all"]
    HP = H1 // 2
    with ExitStack() as ctx:
        def sb(name, shape, dt=F32):
            return ctx.enter_context(nc.sbuf_tensor(name, shape, dt))

        def sem(name):
            return ctx.enter_context(nc.semaphore(name))

        ident = cst[:, C_ID:C_ID + P]
        wq, wk, wv = (sb(f"p3_{n}", [D, H1 * D1]) for n in ("wq", "wk", "wv"))
        wo_raw, wo = sb("p3_wor", [P, HP, D]), sb("p3_wo", [P, HP, D])
        bq, bk = sb("p3_bq", [P, HP]), sb("p3_bk", [P, HP])
        bv, bo = sb("p3_bv", [P, HP * D1]), sb("p3_bo", [P, D])
        cT = [sb(f"p3_cT{i}", [D, P]) for i in range(2)]
        idx = [sb(f"p3_idx{i}", [P, 2], I32) for i in range(2)]
        gy = [[sb(f"p3_gy{i}{k}", [P, D]) for k in range(2)] for i in range(2)]
        stat, mv, rstd = ([sb(f"p3_{n}{i}", [P, k]) for i in range(2)] for n, k in (("st", 6), ("mv", 2), ("rs", 1)))
        xln = [sb(f"p3_xln{i}", [P, D]) for i in range(2)]
        xT = [sb(f"p3_xT{i}", [D, P]) for i in range(2)]
        qT = [sb(f"p3_qT{i}", [P, HP, 2, S]) for i in range(2)]
        kb = [sb(f"p3_kb{i}", [P, HP, 2, 2, S]) for i in range(2)]
        vd = [sb(f"p3_vd{i}", [P, 2, HP, D1]) for i in range(2)]
        vb = [sb(f"p3_vb{i}", [P, 2, HP, 2, D1]) for i in range(2)]
        pr = [sb(f"p3_pr{i}", [P, 2, HP, S]) for i in range(2)]
        mx, sm = ([sb(f"p3_{n}{i}", [P, 2, HP]) for i in range(2)] for n in ("mx", "sm"))
        rc = [sb(f"p3_rc{i}", [P, 2 * HP, 2]) for i in range(2)]
        oT = [sb(f"p3_oT{i}", [P, HP, 2, S]) for i in range(2)]

        ps_r = ctx.enter_context(nc.psum_tensor("p3_r", [P, 2, 512], F32))
        ps_s = ctx.enter_context(nc.psum_tensor("p3_s", [P, 2, HP, S], F32))
        ps_o = ctx.enter_context(nc.psum_tensor("p3_o", [P, 2, HP, S], F32))
        ps_x = ctx.enter_context(nc.psum_tensor("p3_x", [P, 512], F32))
        ps_w = ctx.enter_context(nc.psum_tensor("p3_w", [P, 512], F32))

        w_in, setup = sem("w3_in"), sem("setup3")
        c_ld = [sem(f"c3_ld{i}") for i in range(2)]
        idx_done = sem("idx3_done")
        got = [sem(f"got{i}") for i in range(2)]
        mixed, x2_done, mv_done, rs_done, xln_done = (sem(n) for n in ("mixed", "x2r_done", "mv3_done", "rs3_done", "xln3_done"))
        turned_x, xT_done, q_mm, q_done, k_mm, k_done, v_mm, vd_done, vb_done = (
            sem(n) for n in ("turned3_x", "xT3_done", "q3_mm", "q3_done", "k3_mm", "k3_done", "v3_mm", "vd_done", "vb3_done"))
        s_mm, sub_done, exp_done, rc_done, o_mm, oT_done, ao_mm, x3_done = (
            sem(n) for n in ("s3_mm", "sub3_done", "exp3_done", "rc3_done", "o3_mm", "oT3_done", "ao3_mm", "x3_done"))
        v_step, g_step = sem("v_step3"), sem("g_step3")
        passed = sem("passed")
        block = ctx.enter_context(nc.Block())

        @block.sync
        def _(sp):
            for dst, src in ((wq[:, :], w["wq"]), (wk[:, :], w["wk"]),
                             (bq[:, :], w["bq"]), (bk[:, :], w["bk"]),
                             (wv[:, :].rearrange("p (x c d) -> p x c d", x=2, c=HP)[:, 0], w["wv"].rearrange("p (c x d) -> p x c d", x=2, c=HP)[:, 0]),
                             (wv[:, :].rearrange("p (x c d) -> p x c d", x=2, c=HP)[:, 1], w["wv"].rearrange("p (c x d) -> p x c d", x=2, c=HP)[:, 1]),
                             (bv[0:64, :].rearrange("p (c d) -> p c d", c=HP), spread(w["bv"].rearrange("(c x d) -> x c d", x=2, c=HP)[0], 64)),
                             (bv[64:128, :].rearrange("p (c d) -> p c d", c=HP), spread(w["bv"].rearrange("(c x d) -> x c d", x=2, c=HP)[1], 64)),
                             (wo_raw[:, :, :], w["wo"].rearrange("(c p) n -> p c n", p=P)), (bo[:, :], spread(w["bo"]))):
                sp.dma_start(dst, src).then_inc(w_in, 16)

            def turn(ts):
                if ts.has(2):
                    t, p = ts.at(2)
                    ge(sp, v_mm, 2 * t - 2)
                    sp.dma_start(cT[p][:, :], one(ctxT_in, t)).then_inc(c_ld[p], 16)
            turns(sp, NT, 2, 4, turn)

        @block.tensor
        def _(pe):
            pe.wait_ge(w_in, 160)
            pe.wait_ge(setup, 1)

            def turn(ts):
                if ts.has(0):
                    t, p = ts.at(0)
                    pe.wait_ge(k_done, 2 * t + 2)
                    pe.wait_ge(q_done, 2 * t + 2)
                    for b in range(2):
                        ge(pe, sub_done, 2 * t - 1 + b)
                        for c in range(HP):
                            last = pe.matmul(ps_s[:, b, c, :], kb[p][:, c, b, :, :], qT[p][:, c, b, :], start=True, stop=True)
                        last.then_inc(s_mm, 1)
                if ts.has(-1):
                    t, p = ts.at(-1)
                    pe.wait_ge(vb_done, t + 1)
                    pe.wait_ge(exp_done, 2 * t + 2)
                    for b in range(2):
                        ge(pe, oT_done, 2 * t - 1 + b)
                        for c in range(HP):
                            last = pe.matmul(ps_o[:, b, c, :], vb[p][:, b, c, :, :], pr[p][:, b, c, :], start=True, stop=True)
                        last.then_inc(o_mm, 1)
                if ts.has(1):
                    t, p = ts.at(1)
                    pe.wait_ge(xT_done, t + 1)
                    pe.wait_ge(c_ld[p], (ts.lap(1) + 1) * 16)
                    for h in range(2):
                        ge(pe, vd_done, 2 * t - 1 + h)
                        for c in range(4):
                            last = pe.matmul(ps_r[:, h, P * c:P * c + P], wq[:, P * (4 * h + c):P * (4 * h + c + 1)], xT[p][:, :], start=True, stop=True)
                        last.then_inc(q_mm, 1)
                    for h in range(2):
                        pe.wait_ge(q_done, 2 * t + 1 + h)
                        for c in range(4):
                            last = pe.matmul(ps_r[:, h, P * c:P * c + P], wk[:, P * (4 * h + c):P * (4 * h + c + 1)], cT[p][:, :], start=True, stop=True)
                        last.then_inc(k_mm, 1)
                    for b in range(2):
                        pe.wait_ge(k_done, 2 * t + 1 + b)
                        for x in range(2):
                            last = pe.matmul(ps_r[64 * x:64 * x + 64, b, :], cT[p][:, S * b:S * b + S], wv[:, 512 * x:512 * x + 512], start=True, stop=True)
                        last.then_inc(v_mm, 1)
                if ts.has(2):
                    t, p = ts.at(2)
                    pe.wait_ge(xln_done, t + 1)
                    ge(pe, xT_done, t)
                    pe.transpose(ps_x[:, 0:P], xln[p][:, :], ident).then_inc(turned_x, 1)
                if ts.has(-1):
                    t, p = ts.at(-1)
                    pe.wait_ge(oT_done, 2 * t + 2)
                    ge(pe, x3_done, t)
                    for c in range(HP):
                        last = pe.matmul(ps_w[:, 0:D], oT[p][:, c, :, :], wo[:, c, :], start=(c == 0), stop=(c == HP - 1))
                    last.then_inc(ao_mm, 1)
            turns(pe, NT, 2, 4, turn)

        @block.scalar
        def _(act):
            act.wait_ge(w_in, 160)
            act.wait_ge(setup, 1)

            def turn(ts):
                for b in range(2):
                    if ts.has(0):
                        t, p = ts.at(0)
                        act.wait_ge(sub_done, 2 * t + 1 + b)
                        act.activation(pr[p][:, b, :, :], pr[p][:, b, :, :], ACT.Exp).then_inc(exp_done, 1)
                    if ts.has(-1):
                        t, p = ts.at(-1)
                        act.wait_ge(o_mm, 2 * t + 1 + b)
                        ge(act, ao_mm, t - 1)
                        act.activation(oT[p][:, :, b, :], ps_o[:, b, :, :], ACT.Copy).then_inc(oT_done, 1)
                if ts.has(1):
                    t, p = ts.at(1)
                    ge(act, s_mm, 2 * t - 2)
                    for h in range(2):
                        act.wait_ge(q_mm, 2 * t + 1 + h)
                        for c in range(4):
                            last = act.activation(qT[p][:, 4 * h + c, :, :], ps_r[:, h, P * c:P * c + P], ACT.Identity, bias=bq[:, 4 * h + c:4 * h + c + 1])
                        last.then_inc(q_done, 1)
                    for h in range(2):
                        act.wait_ge(k_mm, 2 * t + 1 + h)
                        for c in range(4):
                            for x in range(2):
                                rows = slice(64 * x, 64 * x + 64)
                                last = act.activation(kb[p][rows, 4 * h + c, :, x, :], ps_r[rows, h, P * c:P * c + P].rearrange("p (b s) -> p b s", b=2), ACT.Identity,
                                                      bias=bk[rows, 4 * h + c:4 * h + c + 1])
                        last.then_inc(k_done, 1)
                if ts.has(2):
                    t, p = ts.at(2)
                    act.wait_ge(turned_x, t + 1)
                    ge(act, q_mm, 2 * t - 2)
                    act.activation(xT[p][:, :], ps_x[:, 0:P], ACT.Copy).then_inc(xT_done, 1)
            turns(act, NT, 2, 4, turn)

        @block.gpsimd
        def _(g):
            g.wait_ge(setup, 1)
            half = cst[:, C_HALF:C_HALF + 1]
            steps = Steps(g, g_step)

            def turn(ts):
                steps.turn(ts, NT, {"eps": (3, 1), "idx": (4, 1)})
                if ts.has(4):
                    t, p = ts.at(4)
                    ge(g, mixed, t - 1)
                    steps.did("idx", g.tensor_copy(idx[p][:, :], mid(idx_all, t)))
                    for k in range(2):
                        alone(g, passed)
                        g.indirect_dma_start(gy[p][k][:, :], None, ybuf, bass.IndirectOffsetOnAxis(ap=idx[p][:, k:k + 1], axis=0)
                                             ).then_inc(got[p], 16)
                if ts.has(3):
                    t, p = ts.at(3)
                    g.wait_ge(mv_done, t + 1)
                    ge(g, xln_done, t - 1)
                    alone(g, passed)
                    steps.did("eps", g.tensor_scalar(rstd[p][:, :], mv[p][:, 1:2], EPS, None, ALU.add))
                    g.tensor_tensor(rstd[p][:, :], rstd[p][:, :], half, ALU.pow).then_inc(rs_done, 1)
                if ts.has(0):
                    t, p = ts.at(0)
                    g.wait_ge(rc_done, t + 1)
                    g.wait_ge(vd_done, 2 * t + 2)
                    ge(g, o_mm, 2 * t - 2)
                    g.tensor_tensor(vb[p][:, :, :, :, :].rearrange("p b c x d -> p (b c) x d"),
                                    vd[p][:, :, :, :].rearrange("p b c d -> p (b c) d").unsqueeze(2).broadcast_to([P, 2 * HP, 2, D1]),
                                    rc[p][:, :, :].unsqueeze(3).broadcast_to([P, 2 * HP, 2, D1]), ALU.mult).then_inc(vb_done, 1)
            turns(g, NT, 2, 4, turn)

        @block.vector
        def _(v):
            for p in range(2):
                v.memset(kb[p][:, :, :, :, :], 0.0)
                v.memset(rc[p][:, :, :], 0.0)
            v.wait_ge(w_in, 160)
            v.tensor_scalar(wo[:, :, :], wo_raw[:, :, :], D1 ** -0.5, None, ALU.mult).then_inc(setup, 1)
            steps = Steps(v, v_step)

            def turn(ts):
                steps.turn(ts, NT, {"max": (0, 2), "sum": (0, 1), "mix": (3, 3)})
                if ts.has(0):
                    t, p = ts.at(0)
                    ge(v, o_mm, 2 * t - 2)
                    for b in range(2):
                        v.wait_ge(s_mm, 2 * t + 1 + b)
                        steps.did("max", v.tensor_reduce(mx[p][:, b, :], ps_s[:, b, :, :], AX.X, ALU.max))
                        v.tensor_tensor(pr[p][:, b, :, :], ps_s[:, b, :, :], mx[p][:, b, :].unsqueeze(2).broadcast_to([P, HP, S]),
                                        ALU.subtract).then_inc(sub_done, 1)
                if ts.has(3):
                    t, p = ts.at(3)
                    v.wait_ge(got[p], (ts.lap(3) + 1) * 32)
                    wt = mid(w_all, t)
                    steps.did("mix", v.scalar_tensor_tensor(mid(x_all, t), gy[p][0][:, :], wt[:, 0:1], mid(x_all, t), ALU.mult, ALU.add))
                    v.scalar_tensor_tensor(mid(x_all, t), gy[p][1][:, :], wt[:, 1:2], mid(x_all, t), ALU.mult, ALU.add).then_inc(mixed, 1)
                    v.wait_ge(mixed, t + 1)
                    alone(v, passed)
                    steps.did("mix", v.bn_stats(stat[p][:, :], mid(x_all, t)))
                    alone(v, passed)
                    v.bn_aggr(mv[p][:, :], stat[p][:, :]).then_inc(mv_done, 1)
                if ts.has(0):
                    t, p = ts.at(0)
                    ge(v, vb_done, t - 1)
                    v.wait_ge(exp_done, 2 * t + 2)
                    steps.did("sum", v.reduce_sum(sm[p][:, :, :], pr[p][:, :, :, :], AX.X))
                    for x in range(2):
                        rows = slice(64 * x, 64 * x + 64)
                        last = v.reciprocal(rc[p][rows, :, x], sm[p][rows, :, :].rearrange("p b c -> p (b c)"))
                    last.then_inc(rc_done, 1)
                if ts.has(3):
                    t, p = ts.at(3)
                    v.wait_ge(rs_done, t + 1)
                    ge(v, turned_x, t - 1)
                    v.tensor_scalar(xln[p][:, :], mid(x_all, t), mv[p][:, 0:1], rstd[p][:, :], ALU.subtract, ALU.mult).then_inc(xln_done, 1)
                    v.wait_ge(xln_done, t + 1)
                    steps.did("mix", v.tensor_tensor(mid(x_all, t), mid(x_all, t), bo[:, :], ALU.add))
                if ts.has(1):
                    t, p = ts.at(1)
                    ge(v, vb_done, t - 1)
                    for b in range(2):
                        v.wait_ge(v_mm, 2 * t + 1 + b)
                        v.tensor_tensor(vd[p][:, b, :, :], ps_r[:, b, :], bv[:, :], ALU.add).then_inc(vd_done, 1)
                if ts.has(-1):
                    t, p = ts.at(-1)
                    v.wait_ge(ao_mm, t + 1)
                    v.tensor_tensor(mid(x_all, t), ps_w[:, 0:D], mid(x_all, t), ALU.add).then_inc(x3_done, 1)
            turns(v, NT, 2, 4, turn)


def phase4(nc, NT, w1T, w2T, keep, out):
    cst, x_all = keep["cst"], keep["x_all"]
    FC = FF // P
    with ExitStack() as ctx:
        def sb(name, shape, dt=F32):
            return ctx.enter_context(nc.sbuf_tensor(name, shape, dt))

        def sem(name):
            return ctx.enter_context(nc.semaphore(name))

        ones = cst[:, C_ONES:C_ONES + P]
        idb = sb("p4_idb", [P, P], BF16)
        wf, wr = [sb(f"p4_wf{i}", [P, FF]) for i in range(2)], sb("p4_wr", [P, FF])
        wi = [sb(f"p4_wi{i}", [P, FF], BF16) for i in range(2)]
        wsum = sb("p4_wsum", [P, 2])
        ws, wrs = sb("p4_ws", [P, 2]), sb("p4_wrs", [P, 2])
        stat, mv, rstd, am, qs, ds, am2, qs2, ds2 = ([sb(f"p4_{n}{i}", [P, k]) for i in range(2)] for n, k in (
            ("st", 6), ("mv", 2), ("rs", 1), ("am", 1), ("qs", 1), ("ds", 1), ("am2", 1), ("qs2", 1), ("ds2", 1)))
        xln, xf = ([sb(f"p4_{n}{i}", [P, D]) for i in range(2)] for n in ("xln", "xf"))
        xi, xiT = ([sb(f"p4_{n}{i}", [P, D], BF16) for i in range(2)] for n in ("xi", "xiT"))
        h, hf = ([sb(f"p4_{n}{i}", [P, FF]) for i in range(2)] for n in ("h", "hf"))
        hi, hiT = ([sb(f"p4_{n}{i}", [P, FC, P], BF16) for i in range(2)] for n in ("hi", "hiT"))
        y = [sb(f"p4_y{i}", [P, D]) for i in range(2)]
        ps_x = [ctx.enter_context(nc.psum_tensor(f"p4_psx{i}", [P, 1024], BF16)) for i in range(2)]
        ps_t = [ctx.enter_context(nc.psum_tensor(f"p4_pst{i}", [P, 1024], BF16)) for i in range(2)]
        ps_h = [ctx.enter_context(nc.psum_tensor(f"p4_psh{i}", [P, 512], F32)) for i in range(2)]
        ps_y = [ctx.enter_context(nc.psum_tensor(f"p4_psy{i}", [P, 512], F32)) for i in range(2)]

        w_in, summed, w_mm, setup = sem("w4_in"), sem("summed"), sem("w4_mm"), sem("setup4")
        mv_done, rs_done, xi_done, x_mm, xiT_done, h_mm, h_done, hi_done, t_mm, hiT_done, y_mm, y_done = (
            sem(n) for n in ("mv4_done", "rs4_done", "xi_done", "x4_mm", "xiT_done", "h4_mm", "h4_done", "hi_done", "t4_mm", "hiT_done", "y4_mm", "y4_done"))
        st = [sem(f"out_st{i}") for i in range(2)]
        v_step, g_step, s_step = sem("v_step4"), sem("g_step4"), sem("s_step4")
        passed = sem("passed")
        block = ctx.enter_context(nc.Block())

        @block.sync
        def _(sp):
            sp.dma_start(wf[0][:, :], w1T).then_inc(w_in, 16)
            sp.dma_start(wf[1][:, :].rearrange("p (c d) -> p c d", c=FC), w2T.rearrange("(c p) d -> p c d", p=P)).then_inc(w_in, 16)

            def turn(ts):
                if ts.has(-3):
                    t, p = ts.at(-3)
                    sp.wait_ge(y_done, t + 1)
                    sp.dma_start(one(out, t), y[p][:, :]).then_inc(st[p], 16)
            turns(sp, NT, 3, 2, turn)
            for p in range(2):
                sp.wait_ge(st[p], 16 * (NT // 2))

        @block.tensor
        def _(pe):
            pe.wait_ge(summed, 1)
            pe.matmul(ps_y[0][:, 0:2], ones, wsum[:, :], start=True, stop=True).then_inc(w_mm, 1)
            pe.wait_ge(setup, 1)

            def turn(ts):
                if ts.has(1):
                    t, p = ts.at(1)
                    pe.wait_ge(xi_done, t + 1)
                    ge(pe, xiT_done, t - 1)
                    pe.transpose(ps_x[p][:, 0:P], xi[p][:, :], idb[:, :]).then_inc(x_mm, 1)
                if ts.has(0):
                    t, p = ts.at(0)
                    pe.wait_ge(xiT_done, t + 1)
                    ge(pe, h_done, t - 1)
                    pe.matmul(ps_h[p][:, :], xiT[p][:, :], wi[0][:, :], start=True, stop=True).then_inc(h_mm, 1)
                if ts.has(-1):
                    t, p = ts.at(-1)
                    pe.wait_ge(hi_done, t + 1)
                    ge(pe, hiT_done, t - 1)
                    for c in range(FC):
                        last = pe.transpose(ps_t[p][:, P * c:P * c + P], hi[p][:, c, :], idb[:, :])
                    last.then_inc(t_mm, 1)
                if ts.has(-2):
                    t, p = ts.at(-2)
                    pe.wait_ge(hiT_done, t + 1)
                    ge(pe, y_done, t - 1)
                    for c in range(FC):
                        last = pe.matmul(ps_y[p][:, 0:D], hiT[p][:, c, :], wi[1][:, P * c:P * c + P], start=(c == 0), stop=(c == FC - 1))
                    last.then_inc(y_mm, 1)
            turns(pe, NT, 3, 2, turn)

        @block.scalar
        def _(act):
            act.wait_ge(setup, 1)

            def turn(ts):
                if ts.has(1):
                    t, p = ts.at(1)
                    act.wait_ge(x_mm, t + 1)
                    ge(act, h_mm, t - 1)
                    act.activation(xiT[p][:, :], ps_x[p][:, 0:P], ACT.Copy).then_inc(xiT_done, 1)
                if ts.has(0):
                    t, p = ts.at(0)
                    act.wait_ge(h_mm, t + 1)
                    ge(act, hi_done, t - 1)
                    act.activation(h[p][:, :], ps_h[p][:, :], ACT.Gelu, scale=ds[p][:, :]).then_inc(h_done, 1)
                if ts.has(-1):
                    t, p = ts.at(-1)
                    act.wait_ge(t_mm, t + 1)
                    ge(act, y_mm, t - 1)
                    act.activation(hiT[p][:, :, :], ps_t[p][:, 0:FF], ACT.Copy).then_inc(hiT_done, 1)
            turns(act, NT, 3, 2, turn)

        @block.gpsimd
        def _(g):
            g.wait_ge(setup, 1)
            half = cst[:, C_HALF:C_HALF + 1]
            steps = Steps(g, g_step)

            def turn(ts):
                steps.turn(ts, NT, {"eps": (2, 1)})
                if ts.has(2):
                    t, p = ts.at(2)
                    g.wait_ge(mv_done, t + 1)
                    ge(g, xi_done, t - 1)
                    alone(g, passed)
                    steps.did("eps", g.tensor_scalar(rstd[p][:, :], mv[p][:, 1:2], EPS, None, ALU.add))
                    g.tensor_tensor(rstd[p][:, :], rstd[p][:, :], half, ALU.pow).then_inc(rs_done, 1)
            turns(g, NT, 3, 2, turn)

        @block.vector
        def _(v):
            done = [0]

            def step(ins):
                ins.then_inc(s_step, 1)
                done[0] += 1
                v.wait_ge(s_step, done[0])

            v.wait_ge(w_in, 32)
            v.tensor_copy(idb[:, :], cst[:, C_ID:C_ID + P])
            for i in range(2):
                ins = v.tensor_reduce(wsum[:, i:i + 1], wf[i][:, :], AX.X, ALU.add, apply_absolute_value=True)
            ins.then_inc(summed, 1)
            v.wait_ge(w_mm, 1)
            step(v.tensor_scalar(ws[:, :], ps_y[0][:, 0:2], 1.0 / (FF * D), EPS, ALU.mult, ALU.max))
            step(v.reciprocal(wrs[:, :], ws[:, :]))
            for i in range(2):
                step(v.tensor_scalar(wr[:, :], wf[i][:, :], wrs[:, i:i + 1], MAGIC, ALU.mult, ALU.add))
                step(v.tensor_scalar(wr[:, :], wr[:, :], -MAGIC, 1.0, ALU.add, ALU.min))
                ins = v.tensor_scalar(wi[i][:, :], wr[:, :], -1.0, None, ALU.max)
                if i == 0:
                    step(ins)
            ins.then_inc(setup, 1)
            steps = Steps(v, v_step)

            def turn(ts):
                steps.turn(ts, NT, {"st": (2, 6), "h": (-1, 4)})
                if ts.has(-1):
                    t, p = ts.at(-1)
                    v.wait_ge(h_done, t + 1)
                    ge(v, y_done, t - 1)
                    steps.did("h", v.tensor_reduce(am2[p][:, :], h[p][:, :], AX.X, ALU.max, apply_absolute_value=True))
                    steps.did("h", v.tensor_scalar(am2[p][:, :], am2[p][:, :], EPS, 1.0 / 127.0, ALU.max, ALU.mult))
                    v.tensor_scalar(ds2[p][:, :], am2[p][:, :], ws[:, 1:2], None, ALU.mult)
                    steps.did("h", v.reciprocal(qs2[p][:, :], am2[p][:, :]))
                    steps.did("h", v.tensor_scalar(hf[p][:, :], h[p][:, :], qs2[p][:, :], MAGIC, ALU.mult, ALU.add))
                    ge(v, t_mm, t - 1)
                    v.tensor_scalar(hi[p][:, :, :], hf[p][:, :], -MAGIC, None, ALU.add).then_inc(hi_done, 1)
                if ts.has(2):
                    t, p = ts.at(2)
                    alone(v, passed)
                    steps.did("st", v.bn_stats(stat[p][:, :], mid(x_all, t)))
                    alone(v, passed)
                    v.bn_aggr(mv[p][:, :], stat[p][:, :]).then_inc(mv_done, 1)
                if ts.has(-2):
                    t, p = ts.at(-2)
                    v.wait_ge(y_mm, t + 1)
                    ge(v, st[p], ts.lap(-2) * 16)
                    v.scalar_tensor_tensor(y[p][:, :], ps_y[p][:, 0:D], ds2[p][:, :], mid(x_all, t), ALU.mult, ALU.add).then_inc(y_done, 1)
                if ts.has(2):
                    t, p = ts.at(2)
                    v.wait_ge(rs_done, t + 1)
                    steps.did("st", v.tensor_scalar(xln[p][:, :], mid(x_all, t), mv[p][:, 0:1], rstd[p][:, :], ALU.subtract, ALU.mult))
                    steps.did("st", v.tensor_reduce(am[p][:, :], xln[p][:, :], AX.X, ALU.max, apply_absolute_value=True))
                    steps.did("st", v.tensor_scalar(am[p][:, :], am[p][:, :], EPS, 1.0 / 127.0, ALU.max, ALU.mult))
                    ge(v, h_done, t - 1)
                    v.tensor_scalar(ds[p][:, :], am[p][:, :], ws[:, 0:1], None, ALU.mult)
                    steps.did("st", v.reciprocal(qs[p][:, :], am[p][:, :]))
                    steps.did("st", v.tensor_scalar(xf[p][:, :], xln[p][:, :], qs[p][:, :], MAGIC, ALU.mult, ALU.add))
                    ge(v, x_mm, t - 1)
                    v.tensor_scalar(xi[p][:, :], xf[p][:, :], -MAGIC, None, ALU.add).then_inc(xi_done, 1)
            turns(v, NT, 3, 2, turn)


def program(nc, NT, a, out):
    xbuf = nc.dram_tensor("slots_in", [ZERO + 2 * P, D], F32).ap()
    ybuf = nc.dram_tensor("slots_out", [(slot_tiles(NT * P) + 1) * P, D], F32).ap()
    with ExitStack() as ctx:
        def sb(name, shape, dt=F32):
            return ctx.enter_context(nc.sbuf_tensor(name, shape, dt))

        keep = dict(x_all=sb("x_all", [P, NT, D]), idx_all=sb("idx_all", [P, NT, 2], I32), w_all=sb("w_all", [P, NT, 2]),
                    counts=sb("counts", [P, 2, E]), cst=sb("cst", [P, N_CONST]))
        names = dict(wq="Wq", wk="Wk", wv="Wv", wo="Wo", bq="bq", bk="bk", bv="bv", bo="bo")
        w0 = {k: a["L0_xattn_" + n] for k, n in names.items()} | {"wr": a["L0_ffn_router_w"]}
        w1 = {k: a["L1_xattn_" + n] for k, n in names.items()}
        phase1(nc, NT, a["x"], a["ctx_twice"], a["constants"], w0, keep, xbuf)
        phase2(nc, NT, (a["L0_ffn_gate_w"], a["L0_ffn_up_w"]), a["L0_ffn_down_w"], keep, xbuf, ybuf)
        phase3(nc, NT, a["ctx_turned"], w1, keep, ybuf)
        phase4(nc, NT, a["L1_ffn_w1"], a["L1_ffn_w2"], keep, out)


def kernel(x, ctx_1024, **weights):
    import numpy as np
    import concourse.bacc as bacc
    from concourse.bass_utils import run_bass_kernel_spmd

    batch, s, d = x.shape
    nt = batch * s // P
    ctx_t = np.asarray(ctx_1024).reshape(nt, 2, s, d).transpose(0, 3, 1, 2)
    laid = {
        "x": np.asarray(x).reshape(batch * s, d),
        "ctx_turned": ctx_t.reshape(nt, d, 2 * s),
        "ctx_twice": np.broadcast_to(ctx_t[:, :, :, None, :], (nt, d, 2, 2, s)),
        "constants": constants(batch * s),
    }
    for name, v in weights.items():
        laid[name] = np.asarray(v)
    for name in ("L0_ffn_gate_w", "L0_ffn_up_w", "L0_ffn_down_w"):
        laid[name] = laid[name].transpose(1, 0, 2)
    for name in ("L1_ffn_w1", "L1_ffn_w2"):
        laid[name] = laid[name].T
    for name in ("L1_xattn_bq", "L1_xattn_bk"):
        laid[name] = laid[name].reshape(H1 // 2, P).T
    laid = {k: np.ascontiguousarray(v) for k, v in laid.items()}
    nc = bacc.Bacc("TRN2", target_bir_lowering=False, num_devices=1)
    a = {k: nc.dram_tensor(f"in_{k}", v.shape, mybir.dt.from_np(v.dtype), kind="ExternalInput").ap() for k, v in laid.items()}
    out = nc.dram_tensor("out_x", [nt, P, d], F32, kind="ExternalOutput").ap()
    program(nc, nt, a, out)
    r = run_bass_kernel_spmd(nc, [{f"in_{k}": v for k, v in laid.items()}], core_ids=[0])
    return r.results[0]["out_x"].reshape(batch, s, d)
```

```python
from contextlib import ExitStack

import concourse.bass as bass
from concourse import mybir

F32 = mybir.dt.float32
BF16 = mybir.dt.bfloat16
I32 = mybir.dt.int32
U32 = mybir.dt.uint32
ALU = mybir.AluOpType
ACT = mybir.ActivationFunctionType
AX = mybir.AxisListType

P = 128
S = 64
D = 128
E = 16
CAP = 640
REG = 2 * CAP
H0, D0 = 16, 8
H1, D1 = 16, 64
ZERO = E * REG
FF = 512
EPS = 1e-5
MAGIC = 12582912.0

C_ID, C_TRI, C_ONES = 0, 128, 256
C_MASK = 384
C_EVEN, C_ODD = 392, 393
C_IOTA = 394
C_BASE = 410
C_DROP = 427
C_HALF = 428
C_PART, C_PART128 = 429, 430
N_CONST = 512


def slot_tiles(tokens):
    return (2 * tokens + E * (P - 1)) // P + 1


def constants():
    import numpy as np

    c = np.zeros((P, N_CONST), np.float32)
    part = np.arange(P)
    c[:, C_ID:C_ID + P] = np.eye(P)
    c[:, C_TRI:C_TRI + P] = part[:, None] < part[None, :]
    c[:, C_ONES:C_ONES + P] = 1.0
    c[:, C_MASK:C_MASK + 8] = (part[:, None] % 64) // D0 == np.arange(8)[None, :]
    c[:, C_EVEN] = (part // D0) % 2 == 0
    c[:, C_ODD] = (part // D0) % 2 == 1
    c[:, C_IOTA:C_IOTA + E] = np.arange(E)
    c[:, C_BASE:C_BASE + E + 1] = np.arange(E + 1) * REG
    c[:, C_DROP] = ZERO + part
    c[:, C_HALF] = -0.5
    c[:, C_PART] = part
    c[:, C_PART128] = P * part
    return c


def ge(eng, sem, value):
    if isinstance(value, int) and value <= 0:
        return
    eng.wait_ge(sem, value)


def alone(eng, passed):
    eng.sem_inc(passed, 1)


class Tiles:

    def __init__(self, total, reg, const, unroll):
        self.total, self.reg, self.const, self.unroll = total, reg, const, unroll

    def at(self, off):
        k = self.const + off
        return (k if self.reg is None else self.reg * self.unroll + k), k % self.unroll

    def lap(self, off):
        k = (self.const + off) // self.unroll
        return k if self.reg is None else self.reg + k

    def has(self, off):
        return self.reg is not None or 0 <= self.const + off < self.total

    def full(self, off):
        return self.has(off) and (self.const + off) % self.unroll == self.unroll - 1


def turns(eng, total, back, ahead, body, unroll=2):
    first = back + 4
    steady = max(0, (total - ahead - first) // unroll)
    for n in range(-ahead, first if steady else total + back):
        body(Tiles(total, None, n, unroll))
    if steady:
        with eng.Fori(0, steady) as i:
            for k in range(unroll):
                body(Tiles(total, i, first + k, unroll))
        for n in range(first + unroll * steady, total + back):
            body(Tiles(total, None, n, unroll))


class Steps:

    def __init__(self, eng, sem):
        self.eng, self.sem, self.before, self.k = eng, sem, 0, 0

    def turn(self, ts, total, kinds, grouped={}):
        u = ts.unroll
        if ts.reg is None:
            self.before = sum(c * max(0, min(total, ts.const + off)) for off, c in kinds.values())
            self.before += sum(c * (max(0, min(total, ts.const + off)) // u) for off, c in grouped.values())
        else:
            self.before = sum(c * (ts.const + off) for off, c in kinds.values()) + ts.reg * (u * sum(c for _, c in kinds.values()))
            if grouped:
                self.before = self.before + sum(c * ((ts.const + off) // u) for off, c in grouped.values()) + ts.reg * sum(c for _, c in grouped.values())
        self.k = 0

    def did(self, kind, ins):
        ins.then_inc(self.sem, 1)
        self.k += 1
        self.eng.wait_ge(self.sem, self.before + self.k)


def cols(vec):
    return vec.rearrange("(p a) -> p a", a=1)


def mid1(ap, t):
    return ap[:, t:t + 1] if isinstance(t, int) else ap[:, bass.ds(t, 1)]


def spread(vec, n=P):
    return vec.partition_broadcast(n)


def one(ap, t):
    if isinstance(t, int):
        return ap[t]
    return ap[bass.ds(t, 1)].squeeze(0)


def mid(ap, t):
    if isinstance(t, int):
        return ap[:, t]
    return ap[:, bass.ds(t, 1)].squeeze(1)


def group(ap, g, n):
    if isinstance(g, int):
        return ap[:, n * g:n * g + n]
    return ap[:, bass.ds(g * n, n)]


def phase1(nc, NT, x_in, ctx_dup, consts_in, w, keep, xbuf, ybuf, later):
    x_all, idx_all, w_all, counts = keep["x_all"], keep["idx_all"], keep["w_all"], keep["counts"]
    G = 4
    NG = NT // G
    with ExitStack() as ctx:
        def sb(name, shape, dt=F32):
            return ctx.enter_context(nc.sbuf_tensor(name, shape, dt))

        def sem(name):
            return ctx.enter_context(nc.semaphore(name))

        cst = keep["cst"]
        ident = cst[:, C_ID:C_ID + P]
        wq, wk, wv, wo = (sb(f"p1_{n}", [D, D]) for n in ("wq", "wk", "wv", "wo"))
        wr = sb("p1_wr", [D, E])
        bq, bk = sb("p1_bq", [P, 1]), sb("p1_bk", [P, 1])
        bqm = sb("p1_bqm", [P, 8])
        bv, bo = sb("p1_bv", [P, D]), sb("p1_bo", [P, D])
        tri, ones = sb("p1_tri", [P, P], BF16), sb("p1_ones", [P, P], BF16)

        cT = [sb(f"p1_cT{i}", [D, 2, 2, S]) for i in range(G)]
        stat, mv_all, rstd_all = sb("p1_st", [P, NT, 6]), sb("p1_mv", [P, NT, 2]), sb("p1_rs", [P, NT])
        stat2, mv2, rstd2 = sb("p1_st2", [P, 6]), sb("p1_mv2", [P, G, 2]), sb("p1_rs2", [P, G])
        xln = [sb(f"p1_xln{i}", [P, D]) for i in range(2)]
        xT = [sb(f"p1_xT{i}", [D, P]) for i in range(2)]
        kb = [sb(f"p1_kb{i}", [P, 2, 2, S]) for i in range(2)]
        qm = [sb(f"p1_qm{i}", [P, 2, 8, S]) for i in range(2)]
        pr = [sb(f"p1_pr{i}", [P, 2, 4, 2, S]) for i in range(2)]
        mx, sm, rc = ([sb(f"p1_{n}{i}", [P, 16]) for i in range(2)] for n in ("mx", "sm", "rc"))
        pT = [sb(f"p1_pT{i}", [P, 2, 4, P]) for i in range(2)]
        vb = [sb(f"p1_vb{i}", [P, 2, 4, 2, 2 * D0]) for i in range(2)]
        od = sb("p1_od", [P, 2, S])
        oT = [sb(f"p1_oT{i}", [P, 2, S]) for i in range(2)]
        x2 = [sb(f"p1_x2{i}", [P, D]) for i in range(G)]
        x2_kept = [sb(f"p1_x2k{i}", [P, D]) for i in range(G)]
        x2T = [sb(f"p1_x2T{i}", [D, P]) for i in range(2)]
        lg, ex = sb("p1_lg", [P, G, 24]), sb("p1_ex", [P, G, 24])
        i8, idf = sb("p1_i8", [P, G, 8], U32), sb("p1_idf", [P, G, 2])
        z = sb("p1_z", [P, G])
        oh = sb("p1_oh", [P, G, 2, E], BF16)
        carry = sb("p1_carry", [P, 2, E])
        rk, cl, slot = sb("p1_rk", [P, G, 2, E]), sb("p1_cl", [P, G, E]), sb("p1_slot", [P, G, E])
        mm, red = sb("p1_mm", [P, 2, G, 2, E]), sb("p1_red", [P, 2, G, 2])
        kp, pos = sb("p1_kp", [P, G, 2]), sb("p1_pos", [P, G, 2])
        idx = [sb(f"p1_idx{i}", [P, 2], I32) for i in range(G)]

        ps_s = ctx.enter_context(nc.psum_tensor("ps_s", [P, 2, 4, 2, S], F32))
        ps_p = ctx.enter_context(nc.psum_tensor("ps_p", [P, 2, 4, P], F32))
        ps_x = ctx.enter_context(nc.psum_tensor("ps_x", [P, 4, P], F32))
        ps_q = ctx.enter_context(nc.psum_tensor("ps_q", [P, 4, P], F32))
        ps_v = ctx.enter_context(nc.psum_tensor("ps_v", [P, 512], F32))
        ps_o = ctx.enter_context(nc.psum_tensor("ps_o", [P, 4, P], F32))
        LG, RK, CT = 256, 320, 448

        zeros = sb("p1_zeros", [P, D])
        w_in, cst_in, later_in, zero_st = sem("w_in"), sem("cst_in"), sem("later_in"), sem("zero_st"); x_ld = [sem(f"x_ld{i}") for i in range(NG)]; c_ld = [sem(f"c_ld{i}") for i in range(G)]
        setup = sem("setup")
        mv_done, rs_done, xln_done, bo_done = sem("mv_done"), sem("rs_done"), sem("xln_done"), sem("bo_done")
        turned_x, xT_done = sem("turned_x"), sem("xT_done")
        qk_mm, k_done, qm_done = sem("qk_mm"), sem("k_done"), sem("qm_done")
        v_mm, vb_done = sem("v_mm"), sem("vb_done")
        s_mm, sub_done, exp_done = sem("s_mm"), sem("sub_done"), sem("exp_done")
        rc_done, pr_done, turned_p, pT_done = sem("rc_done"), sem("pr_done"), sem("turned_p"), sem("pT_done")
        o_mm, oT_done, ao_mm, x1_done = sem("o_mm"), sem("oT_done"), sem("ao_mm"), sem("x1_done")
        mv2_done, rs2_done, x2_done = sem("mv2_done"), sem("rs2_done"), sem("x2_done")
        turned_x2, x2T_done, lg_mm, lg_read, top_done = sem("turned_x2"), sem("x2T_done"), sem("lg_mm"), sem("lg_read"), sem("top_done")
        rexp_done, oh_done, rk_mm, rk_done = sem("rexp_done"), sem("oh_done"), sem("rk_mm"), sem("rk_done")
        idx_done, kept = sem("idx_done"), sem("kept")
        sc = [sem(f"scattered{i}") for i in range(G)]
        v_step, g_step, start_step, rs_step = sem("v_step"), sem("g_step"), sem("start_step"), sem("rs_step")
        passed = sem("passed")
        block = ctx.enter_context(nc.Block())

        xg = x_in.rearrange("(g t p) d -> g p t d", t=G, p=P)
        X2, LOG, RANK, KEEP, SCAT = -5, -6, -7, -8, -11
        BACK, AHEAD = 11, 4

        @block.sync
        def _(sp):
            sp.dma_start(cst[:, :], consts_in).then_inc(cst_in, 16)
            for g in range(NG):
                sp.dma_start(x_all[:, g * G:(g + 1) * G, :], xg[g]).then_inc(x_ld[g], 16)
            sp.wait_ge(setup, 3)
            sp.dma_start(xbuf[0:ZERO, :].rearrange("(e r) d -> r e d", e=E)[0:P], zeros[:, :].unsqueeze(1).broadcast_to([P, E, D])).then_inc(zero_st, 16)
            sp.dma_start(xbuf[ZERO:ZERO + P, :], zeros[:, :]).then_inc(zero_st, 16)
            sp.dma_start(ybuf[slot_tiles(NT * P) * P:, :], zeros[:, :]).then_inc(zero_st, 16)

            def turn(ts):
                if ts.reg is None and ts.const == 2:
                    for dst, src in later:
                        sp.dma_start(dst, src).then_inc(later_in, 16)
                if ts.has(3):
                    t, p = ts.at(3)
                    ge(sp, v_mm, t - G + 1)
                    sp.dma_start(cT[p][:, :, :, :], one(ctx_dup, t)).then_inc(c_ld[p], 16)
            turns(sp, NT, BACK, AHEAD, turn, G)
            sp.wait_ge(later_in, 16 * len(later))

        @block.tensor
        def _(pe):
            pe.wait_ge(w_in, 192)
            pe.wait_ge(cst_in, 16)
            pe.wait_ge(setup, 3)

            def turn(ts):
                if ts.has(0):
                    t, p = ts.at(0)
                    p %= 2
                    pe.wait_ge(k_done, t + 1)
                    pe.wait_ge(qm_done, t + 1)
                    for b in range(2):
                        ge(pe, sub_done, 2 * t - 1 + b)
                        for j in range(4):
                            last = pe.matmul(ps_s[:, b, j, :, :], qm[p][:, b, 2 * j:2 * j + 2, :], kb[p][:, b, :, :], start=True, stop=True)
                        last.then_inc(s_mm, 1)
                if ts.has(LOG):
                    t, p = ts.at(LOG)
                    pe.wait_ge(x2_done, t + 1)
                    pe.wait_ge(xT_done, (t + 3 - LOG) if not isinstance(t, int) else min(t + 3 - LOG, NT))
                    pe.transpose(ps_x[:, 1, :], x2[p][:, :], ident).then_inc(turned_x2, 1)
                if ts.has(-1):
                    t, p = ts.at(-1)
                    p %= 2
                    pe.wait_ge(pr_done, t + 1)
                    for b in range(2):
                        ge(pe, pT_done, 2 * t - 1 + b)
                        for j in range(4):
                            last = pe.transpose(ps_p[:, b, j, :], pr[p][:, b, j, :, :], ident)
                        last.then_inc(turned_p, 1)
                if ts.has(LOG):
                    t, p = ts.at(LOG)
                    pe.wait_ge(x2T_done, t + 1)
                    pe.wait_ge(vb_done, (t + 1 - LOG) if not isinstance(t, int) else min(t + 1 - LOG, NT))
                    if ts.full(LOG - 1):
                        ge(pe, lg_read, ts.lap(LOG - 1) + 1)
                    if ts.full(RANK - 1):
                        ge(pe, rk_done, ts.lap(RANK - 1) + 1)
                    k = (ts.const + LOG) % G
                    pe.matmul(ps_v[:, LG + 16 * k:LG + 16 * k + 16], x2T[p % 2][:, :], wr[:, :], start=True, stop=True).then_inc(lg_mm, 1)
                if ts.full(RANK):
                    g = ts.lap(RANK)
                    pe.wait_ge(oh_done, g + 1)
                    pe.wait_ge(lg_read, g + 1)
                    pe.wait_ge(vb_done, (g * G + G - RANK) if not isinstance(g, int) else min(g * G + G - RANK, NT))
                    pe.matmul(ps_v[:, RK:RK + G * 32], tri[:, :], oh[:, :, :, :], start=True, stop=False)
                    for k in range(1, G):
                        pe.matmul(ps_v[:, RK + 32 * k:RK + G * 32], ones[:, :], oh[:, 0:G - k, :, :], start=False, stop=(k == G - 1))
                    for k in range(G):
                        last = pe.matmul(ps_v[:, CT:CT + 32], ones[:, :], oh[:, k, :, :], start=(k == 0), stop=(k == G - 1))
                    last.then_inc(rk_mm, 1)
                if ts.has(-1):
                    t, p = ts.at(-1)
                    p %= 2
                    ge(pe, x1_done, t)
                    for b in range(2):
                        pe.wait_ge(pT_done, 2 * t + 1 + b)
                        for j in range(4):
                            last = pe.matmul(ps_o[32 * j:32 * j + 32, b, :], vb[p][:, b, j, :, :], pT[p][:, b, j, :], start=True, stop=True)
                    last.then_inc(o_mm, 1)
                if ts.has(2):
                    t, p = ts.at(2)
                    pe.wait_ge(xT_done, t + 1)
                    ge(pe, k_done, t)
                    ge(pe, qm_done, t)
                    pe.wait_ge(c_ld[p], (ts.lap(2) + 1) * 16)
                    pe.matmul(ps_q[:, 0, :], wq[:, :], xT[p % 2][:, :], start=True, stop=True)
                    pe.matmul(ps_q[:, 1, :], wk[:, :], cT[p][:, :, 0, :], start=True, stop=True).then_inc(qk_mm, 1)
                if ts.has(1):
                    t, p = ts.at(1)
                    ge(pe, vb_done, t)
                    if ts.full(LOG):
                        ge(pe, lg_read, ts.lap(LOG) + 1)
                    if ts.full(RANK):
                        ge(pe, rk_done, ts.lap(RANK) + 1)
                    for b in range(2):
                        last = pe.matmul(ps_v[:, 128 * b:128 * b + 128], cT[p][:, b, :, :], wv[:, :], start=True, stop=True)
                    last.then_inc(v_mm, 1)
                if ts.has(-1):
                    t, p = ts.at(-1)
                    pe.wait_ge(oT_done, t + 1)
                    pe.matmul(ps_o[:, 2, :], oT[p % 2][:, :, :], wo[:, :], start=True, stop=True).then_inc(ao_mm, 1)
                if ts.has(3):
                    t, p = ts.at(3)
                    pe.wait_ge(xln_done, t + 1)
                    ge(pe, x2T_done, t - 3 + LOG + 1)
                    pe.transpose(ps_x[:, 0, :], xln[p % 2][:, :], ident).then_inc(turned_x, 1)
            turns(pe, NT, BACK, AHEAD, turn, G)

        @block.scalar
        def _(act):
            act.wait_ge(w_in, 192)
            act.wait_ge(cst_in, 16)
            act.wait_ge(setup, 3)
            mask = cst[:, C_MASK:C_MASK + 8]

            def turn(ts):
                if ts.has(LOG):
                    t, p = ts.at(LOG)
                    act.wait_ge(turned_x2, t + 1)
                    ge(act, lg_mm, t - 1)
                    act.activation(x2T[p % 2][:, :], ps_x[:, 1, :], ACT.Copy).then_inc(x2T_done, 1)
                if ts.has(-1):
                    t, p = ts.at(-1)
                    ge(act, o_mm, t - 1)
                    for r in range(2):
                        act.wait_ge(turned_p, 2 * t + 1 + r)
                        act.activation(pT[p % 2][:, r, :, :], ps_p[:, r, :, :], ACT.Copy).then_inc(pT_done, 1)
                if ts.has(0):
                    t, p = ts.at(0)
                    p %= 2
                    for r in range(2):
                        act.wait_ge(sub_done, 2 * t + 1 + r)
                        act.activation(pr[p][:, r, :, :, :], pr[p][:, r, :, :, :], ACT.Exp, scale=D0 ** -0.5).then_inc(exp_done, 1)
                if ts.has(2):
                    t, p = ts.at(2)
                    p %= 2
                    act.wait_ge(qk_mm, t + 1)
                    ge(act, s_mm, 2 * t - 2)
                    for r in range(2):
                        rows = slice(64 * r, 64 * r + 64)
                        last = act.activation(kb[p][rows, :, r, :], ps_q[rows, 1, :].rearrange("p (b s) -> p b s", b=2), ACT.Identity, bias=bk[rows, :])
                    last.then_inc(k_done, 1)
                    for j in range(8):
                        last = act.activation(qm[p][:, :, j, :], ps_q[:, 0, :].rearrange("p (b s) -> p b s", b=2), ACT.Identity,
                                              bias=bqm[:, j:j + 1], scale=mask[:, j:j + 1])
                    last.then_inc(qm_done, 1)
                if ts.full(LOG):
                    act.wait_ge(top_done, ts.lap(LOG) + 1)
                    act.activation(ex[:, :, :], ex[:, :, :], ACT.Exp).then_inc(rexp_done, 1)
                if ts.has(3):
                    t, p = ts.at(3)
                    act.wait_ge(turned_x, t + 1)
                    ge(act, qk_mm, t - 1)
                    act.activation(xT[p % 2][:, :], ps_x[:, 0, :], ACT.Copy).then_inc(xT_done, 1)
            turns(act, NT, BACK, AHEAD, turn, G)

        @block.gpsimd
        def _(g):
            for dst, src in ((wq, w["wq"]), (wk, w["wk"]), (wv, w["wv"]), (wr, w["wr"]),
                             (bq, cols(w["bq"])), (bk, cols(w["bk"])), (bv, spread(w["bv"])), (bo, spread(w["bo"]))):
                g.dma_start(dst[:, :], src).then_inc(w_in, 16)
            for j in range(4):
                g.dma_start(wo[32 * j:32 * j + 32, :], w["wo"].rearrange("(r j c) n -> j r c n", r=2, j=4)[j]).then_inc(w_in, 16)
            g.wait_ge(w_in, 192)
            g.wait_ge(cst_in, 16)
            half = cst[:, C_HALF:C_HALF + 1]
            steps = Steps(g, g_step)
            g.wait_ge(mv_done, 1)
            g.tensor_scalar(rstd_all[:, :], mv_all[:, :, 1], EPS, None, ALU.add).then_inc(rs_step, 1)
            g.wait_ge(rs_step, 1)
            g.wait_ge(zero_st, 48)
            g.tensor_tensor(rstd_all[:, :], rstd_all[:, :], half.broadcast_to([P, NT]), ALU.pow).then_inc(rs_done, 1)

            def turn(ts):
                steps.turn(ts, NT, {"idx": (SCAT, 1)}, {"eps2": (-2, 1)})
                if ts.full(-2):
                    q = ts.lap(-2)
                    g.wait_ge(mv2_done, q * G + G)
                    ge(g, x2_done, q * G)
                    alone(g, passed)
                    steps.did("eps2", g.tensor_scalar(rstd2[:, :], mv2[:, :, 1], EPS, None, ALU.add))
                    g.tensor_tensor(rstd2[:, :], rstd2[:, :], half.broadcast_to([P, G]), ALU.pow).then_inc(rs2_done, 1)
                if ts.has(3):
                    t, p = ts.at(3)
                    g.wait_ge(xln_done, t + 1)
                    alone(g, passed)
                    g.tensor_tensor(mid(x_all, t), mid(x_all, t), bo[:, :], ALU.add).then_inc(bo_done, 1)
                if ts.has(KEEP):
                    t, p = ts.at(KEEP)
                    g.wait_ge(x2_done, t + 1)
                    ge(g, sc[p], ts.lap(KEEP) * 32)
                    alone(g, passed)
                    g.tensor_copy(x2_kept[p][:, :], x2[p][:, :]).then_inc(kept, 1)
                if ts.has(SCAT):
                    t, p = ts.at(SCAT)
                    g.wait_ge(idx_done, ts.lap(SCAT) + 1)
                    g.wait_ge(kept, t + 1)
                    ge(g, sc[p], ts.lap(SCAT) * 32)
                    steps.did("idx", g.tensor_copy(idx[p][:, :], mid(idx_all, t)))
                    for k in range(2):
                        alone(g, passed)
                        g.indirect_dma_start(xbuf, bass.IndirectOffsetOnAxis(ap=idx[p][:, k:k + 1], axis=0), x2_kept[p][:, :], None,
                                             bounds_check=ZERO - 1, oob_is_err=False).then_inc(sc[p], 16)
                if ts.has(0):
                    t, p = ts.at(0)
                    p %= 2
                    g.wait_ge(rc_done, t + 1)
                    probs = pr[p][:, :, :, :, :].rearrange("p b j r k -> p (b j r) k")
                    g.tensor_tensor(probs, probs,
                                    rc[p][:, :].unsqueeze(2).broadcast_to([P, 16, S]), ALU.mult).then_inc(pr_done, 1)
            turns(g, NT, BACK, AHEAD, turn, G)
            for p in range(G):
                g.wait_ge(sc[p], 32 * (NT // G))

        @block.vector
        def _(v):
            for g in range(NG):
                v.wait_ge(x_ld[g], 16)
                for t in range(G * g, G * g + G):
                    last = v.bn_stats(stat[:, t, :], x_all[:, t, :])
                last.then_inc(start_step, 1)
            v.wait_ge(start_step, NG)
            for t in range(NT):
                last = v.bn_aggr(mv_all[:, t, :], stat[:, t, :])
            last.then_inc(mv_done, 1)
            for p in range(2):
                v.memset(vb[p][:, :, :, :, :], 0.0)
                v.memset(kb[p][:, :, :, :], 0.0)
            v.memset(carry[:, :, :], 0.0)
            v.memset(zeros[:, :], 0.0)
            v.wait_ge(w_in, 192)
            v.wait_ge(cst_in, 16)
            mask = cst[:, C_MASK:C_MASK + 8]
            v.tensor_scalar(bqm[:, :], mask, bq[:, :], None, ALU.mult).then_inc(setup, 1)
            v.tensor_copy(tri[:, :], cst[:, C_TRI:C_TRI + P]).then_inc(setup, 1)
            v.tensor_copy(ones[:, :], cst[:, C_ONES:C_ONES + P]).then_inc(setup, 1)
            v.wait_ge(setup, 3)
            v.wait_ge(rs_done, 1)
            iota = cst[:, C_IOTA:C_IOTA + E]
            base = cst[:, C_BASE:C_BASE + E]
            drop = cst[:, C_DROP:C_DROP + 1]
            even, odd = cst[:, C_EVEN:C_EVEN + 1], cst[:, C_ODD:C_ODD + 1]
            steps = Steps(v, v_step)

            def turn(ts):
                steps.turn(ts, NT, {"max": (0, 2), "od": (-1, 1), "sum": (0, 1), "st2": (-1, 1)}, {"top": (LOG, 3), "rank": (RANK, 8)})
                if ts.has(0):
                    t, p = ts.at(0)
                    p %= 2
                    ge(v, turned_p, 2 * t - 2)
                    for r in range(2):
                        v.wait_ge(s_mm, 2 * t + 1 + r)
                        m = mx[p][:, 8 * r:8 * r + 8]
                        scores = ps_s[:, r, :, :, :].rearrange("p j h k -> p (j h) k")
                        steps.did("max", v.tensor_reduce(m, scores, AX.X, ALU.max))
                        v.tensor_tensor(pr[p][:, r, :, :, :].rearrange("p j h k -> p (j h) k"), scores, m.unsqueeze(2).broadcast_to([P, 8, S]),
                                        ALU.subtract).then_inc(sub_done, 1)
                if ts.has(-1):
                    t, p = ts.at(-1)
                    v.wait_ge(o_mm, t + 1)
                    ge(v, ao_mm, t - 1)
                    steps.did("od", v.tensor_scalar(od[:, :, :], ps_o[:, 0:2, S:2 * S], odd, None, ALU.mult))
                    v.scalar_tensor_tensor(oT[p % 2][:, :, :], ps_o[:, 0:2, 0:S], even, od[:, :, :], ALU.mult, ALU.add).then_inc(oT_done, 1)
                if ts.has(X2):
                    t, p = ts.at(X2)
                    v.wait_ge(rs2_done, ts.lap(X2) + 1)
                    ge(v, turned_x2, t - G + 1)
                    ge(v, kept, t - G + 1)
                    v.tensor_scalar(x2[p][:, :], mid(x_all, t), mv2[:, p, 0:1], rstd2[:, p:p + 1], ALU.subtract, ALU.mult).then_inc(x2_done, 1)
                if ts.has(0):
                    t, p = ts.at(0)
                    v.wait_ge(exp_done, 2 * t + 2)
                    ge(v, pr_done, t - 1)
                    steps.did("sum", v.reduce_sum(sm[p % 2][:, :], pr[p % 2][:, :, :, :, :].rearrange("p b j r k -> p (b j r) k"), AX.X))
                    v.reciprocal(rc[p % 2][:, :], sm[p % 2][:, :]).then_inc(rc_done, 1)
                if ts.full(LOG):
                    g = ts.lap(LOG)
                    v.wait_ge(lg_mm, g * G + G)
                    v.tensor_copy(lg[:, :, 0:16], ps_v[:, LG:LG + 16 * G].rearrange("p (g e) -> p g e", g=G)).then_inc(lg_read, 1)
                    v.wait_ge(lg_read, g + 1)
                    for k in range(G):
                        alone(v, passed)
                        last = v.max(lg[:, k, 16:24], lg[:, k, 0:16])
                    steps.did("top", last)
                    v.tensor_tensor(ex[:, :, :], lg[:, :, :], lg[:, :, 16:17].broadcast_to([P, G, 24]), ALU.subtract).then_inc(top_done, 1)
                    for k in range(G):
                        last = v.max_index(i8[:, k, :], lg[:, k, 16:24], lg[:, k, 0:16])
                    steps.did("top", last)
                    steps.did("top", v.tensor_copy(idf[:, :, :], i8[:, :, 0:2]))
                    ge(v, rk_mm, g)
                    v.tensor_tensor(oh[:, :, :, :], iota.unsqueeze(1).unsqueeze(1).broadcast_to([P, G, 2, E]),
                                    idf[:, :, :].unsqueeze(3).broadcast_to([P, G, 2, E]), ALU.is_equal).then_inc(oh_done, 1)
                if ts.full(RANK):
                    g = ts.lap(RANK)
                    v.wait_ge(rexp_done, g + 1)
                    steps.did("rank", v.reduce_sum(z[:, :], ex[:, :, 0:16], AX.X))
                    v.wait_ge(rk_mm, g + 1)
                    ge(v, rk_done, g)
                    steps.did("rank", v.tensor_tensor(rk[:, :, :, :], ps_v[:, RK:RK + 32 * G].rearrange("p (g k e) -> p g k e", g=G, k=2),
                                                      carry[:, :, :].unsqueeze(1).broadcast_to([P, G, 2, E]), ALU.add))
                    v.tensor_tensor(carry[:, :, :], ps_v[:, CT:CT + 32].rearrange("p (k e) -> p k e", k=2), carry[:, :, :], ALU.add).then_inc(rk_done, 1)
                    v.scalar_tensor_tensor(cl[:, :, :], rk[:, :, 1, :], float(CAP), base.unsqueeze(1).broadcast_to([P, G, E]), ALU.min, ALU.add)
                    steps.did("rank", v.reciprocal(z[:, :], z[:, :]))
                    v.tensor_tensor(mm[:, 0, :, :, :], oh[:, :, :, :], rk[:, :, :, :], ALU.mult)
                    steps.did("rank", v.scalar_tensor_tensor(slot[:, :, :], rk[:, :, 0, :], float(CAP), cl[:, :, :], ALU.min, ALU.add))
                    steps.did("rank", v.tensor_tensor(mm[:, 1, :, :, :], oh[:, :, :, :], slot[:, :, :].unsqueeze(2).broadcast_to([P, G, 2, E]), ALU.mult))
                    steps.did("rank", v.reduce_sum(red[:, :, :, :], mm[:, :, :, :, :], AX.X))
                    steps.did("rank", v.tensor_scalar(kp[:, :, :], red[:, 0, :, :], float(CAP), None, ALU.is_lt))
                    v.scalar_tensor_tensor(pos[:, :, :], red[:, 1, :, :], drop, kp[:, :, :], ALU.subtract, ALU.mult)
                    steps.did("rank", v.tensor_tensor(kp[:, :, :], kp[:, :, :], z[:, :].unsqueeze(2).broadcast_to([P, G, 2]), ALU.mult))
                    v.tensor_tensor(group(w_all, g, G), ex[:, :, 16:18], kp[:, :, :], ALU.mult)
                    v.tensor_scalar(group(idx_all, g, G), pos[:, :, :], drop, None, ALU.add).then_inc(idx_done, 1)
                if ts.has(1):
                    t, p = ts.at(1)
                    v.wait_ge(v_mm, t + 1)
                    ge(v, o_mm, t - 1)
                    for r in range(2):
                        rows = slice(64 * r, 64 * r + 64)
                        ins = v.tensor_tensor(
                            vb[p % 2][rows, :, :, r, :],
                            ps_v[rows, 0:256].rearrange("p (b r j c) -> p b r j c", b=2, r=2, j=4)[:, :, r, :, :],
                            bv[rows, :].rearrange("p (r j c) -> p r j c", r=2, j=4)[:, r, :, :].unsqueeze(1).broadcast_to([64, 2, 4, 16]),
                            ALU.add)
                    ins.then_inc(vb_done, 1)
                if ts.has(4):
                    t, p = ts.at(4)
                    ge(v, turned_x, t - 1)
                    v.tensor_scalar(xln[p % 2][:, :], mid(x_all, t), mid(mv_all, t)[:, 0:1], mid1(rstd_all, t), ALU.subtract, ALU.mult).then_inc(xln_done, 1)
                if ts.has(-1):
                    t, p = ts.at(-1)
                    v.wait_ge(ao_mm, t + 1)
                    v.wait_ge(bo_done, t + 1)
                    v.tensor_tensor(mid(x_all, t), ps_o[:, 2, :], mid(x_all, t), ALU.add).then_inc(x1_done, 1)
                    v.wait_ge(x1_done, t + 1)
                    alone(v, passed)
                    steps.did("st2", v.bn_stats(stat2[:, :], mid(x_all, t)))
                    alone(v, passed)
                    v.bn_aggr(mv2[:, p, :], stat2[:, :]).then_inc(mv2_done, 1)
            turns(v, NT, BACK, AHEAD, turn, G)
            v.wait_ge(rk_done, NG)
            v.tensor_copy(counts[:, :, :], carry[:, :, :])


def phase2(nc, NT, keep, xbuf, ybuf):
    NS = slot_tiles(NT * P)
    cst, counts, idx_all = keep["cst"], keep["counts"], keep["idx_all"]
    gu, dn = keep["gu"], keep["dn"]
    U = 8
    X = E + 1
    with ExitStack() as ctx:
        def sb(name, shape, dt=F32):
            return ctx.enter_context(nc.sbuf_tensor(name, shape, dt))

        def sem(name):
            return ctx.enter_context(nc.semaphore(name))

        ident = cst[:, C_ID:C_ID + P]
        n2, nn = sb("p2_n2", [P, 2, E]), sb("p2_nn", [P, E])
        ni, nsh = sb("p2_ni", [P, E], I32), sb("p2_nsh", [P, E], I32)
        nt, end = sb("p2_nt", [P, E]), sb("p2_end", [P, E])
        lim, jump = sb("p2_lim", [P, X]), sb("p2_jump", [P, 3, E])
        past, taken, at = sb("p2_past", [P, E]), sb("p2_taken", [P, 3, E]), sb("p2_at", [P, 4])
        table = sb("p2_table", [1, 2, P], I32)
        edge, shift = sb("p2_edge", [P, 2 * X]), sb("p2_shift", [P, 2 * X])
        first, off, gap = sb("p2_first", [P, X]), sb("p2_off", [P, X]), sb("p2_gap", [P, X])
        slot_f, moved = sb("p2_slotf", [P, NT * 2]), sb("p2_moved", [P, NT * 2])
        behind = sb("p2_behind", [P, NT * 2, 2 * X])
        xe = [sb(f"p2_xe{i}", [P, D]) for i in range(U)]
        xT = [sb(f"p2_xT{i}", [D, P]) for i in range(4)]
        sg = [sb(f"p2_sg{i}", [P, P]) for i in range(2)]
        hh = [sb(f"p2_h{i}", [P, P]) for i in range(4)]
        hT = [sb(f"p2_hT{i}", [P, P]) for i in range(4)]
        ye = [sb(f"p2_ye{i}", [P, D]) for i in range(U)]
        ps_x, ps_g, ps_h, ps_y = ([ctx.enter_context(nc.psum_tensor(f"p2_{n}{i}", [P, 512], F32)) for i in range(2)]
                                  for n in ("psx", "psg", "psh", "psy"))

        listed, list_mm, tabled = sem("listed"), sem("list_mm"), sem("tabled")
        x_ld = [sem(f"xe_ld{i}") for i in range(U)]
        y_st = [sem(f"ye_st{i}") for i in range(U)]
        x_mm, xT_done, g_mm, sg_done, h_done, h_mm, hT_done, y_mm, y_done = (
            sem(n) for n in ("x_mm", "xT2_done", "g_mm", "sg_done", "h_done", "h_mm", "hT_done", "y_mm", "y_done"))
        v_step = sem("v_step2")
        passed = sem("passed")
        block = ctx.enter_context(nc.Block())
        LOAD, TX, HID, TH, DOWN, OUT = 5, 2, -1, -2, -4, -5
        BACK, AHEAD = 6, 5

        def entry(k, t):
            return table[0:1, k, t:t + 1] if isinstance(t, int) else table[0:1, k, bass.ds(t, 1)]

        @block.sync
        def _(sp):
            sp.wait_ge(tabled, 1)

            def turn(ts):
                if ts.has(LOAD):
                    t, p = ts.at(LOAD)
                    ge(sp, x_mm, t - U + 1)
                    r = sp.value_load(entry(0, t), min_val=0, max_val=ZERO)
                    sp.dma_start(xe[p][:, :], xbuf[bass.ds(r, P), :]).then_inc(x_ld[p], 16)
                if ts.has(OUT - 1):
                    t, p = ts.at(OUT - 1)
                    sp.wait_ge(y_done, t + 1)
                    sp.dma_start(one(ybuf[0:NS * P, :].rearrange("(t p) d -> t p d", p=P), t), ye[p][:, :]).then_inc(y_st[p], 16)
            turns(sp, NS, BACK, AHEAD, turn, U)
            for p in range(U):
                sp.wait_ge(y_st[p], 16 * ((NS - p + U - 1) // U))

        @block.tensor
        def _(pe):
            pe.wait_ge(listed, 1)
            for k in range(2):
                last = pe.matmul(ps_g[0][0:1, P * k:P * k + P], at[:, k:k + 1], ident, start=True, stop=True)
            last.then_inc(list_mm, 1)
            pe.wait_ge(tabled, 1)

            def turn(ts):
                if ts.has(0):
                    t, p = ts.at(0)
                    pe.wait_ge(xT_done, t + 1)
                    ge(pe, h_done, t - 1)
                    alone(pe, passed)
                    e = pe.value_load(entry(1, t), min_val=0, max_val=E - 1)
                    pe.matmul(ps_g[p % 2][:, 0:2 * P], xT[p % 4][:, :], gu[:, bass.ds(e * (2 * P), 2 * P)],
                              start=True, stop=True).then_inc(g_mm, 1)
                if ts.has(TX):
                    t, p = ts.at(TX)
                    pe.wait_ge(x_ld[p], (ts.lap(TX) + 1) * 16)
                    ge(pe, xT_done, t - 1)
                    pe.transpose(ps_x[p % 2][:, 0:P], xe[p][:, :], ident).then_inc(x_mm, 1)
                if ts.has(TH):
                    t, p = ts.at(TH)
                    pe.wait_ge(h_done, t + 1)
                    ge(pe, hT_done, t - 1)
                    pe.transpose(ps_h[p % 2][:, 0:P], hh[p % 4][:, :], ident).then_inc(h_mm, 1)
                if ts.has(DOWN):
                    t, p = ts.at(DOWN)
                    pe.wait_ge(hT_done, t + 1)
                    ge(pe, y_done, t - 1)
                    alone(pe, passed)
                    e = pe.value_load(entry(1, t), min_val=0, max_val=E - 1)
                    pe.matmul(ps_y[p % 2][:, 0:D], hT[p % 4][:, :], dn[:, bass.ds(e * D, D)], start=True, stop=True).then_inc(y_mm, 1)
            turns(pe, NS, BACK, AHEAD, turn, U)

        @block.scalar
        def _(act):
            def turn(ts):
                if ts.has(OUT):
                    t, p = ts.at(OUT)
                    act.wait_ge(y_mm, t + 1)
                    ge(act, y_st[p], ts.lap(OUT) * 16)
                    act.activation(ye[p][:, :], ps_y[p % 2][:, 0:D], ACT.Copy).then_inc(y_done, 1)
                if ts.has(0):
                    t, p = ts.at(0)
                    act.wait_ge(g_mm, t + 1)
                    ge(act, h_done, t - 1)
                    act.activation(sg[p % 2][:, :], ps_g[p % 2][:, 0:P], ACT.Silu).then_inc(sg_done, 1)
                if ts.has(TX):
                    t, p = ts.at(TX)
                    act.wait_ge(x_mm, t + 1)
                    ge(act, g_mm, t - 3)
                    act.activation(xT[p % 4][:, :], ps_x[p % 2][:, 0:P], ACT.Copy).then_inc(xT_done, 1)
            turns(act, NS, BACK, AHEAD, turn, U)

        @block.vector
        def _(v):
            done = [0]

            def step(ins):
                ins.then_inc(v_step, 1)
                done[0] += 1
                v.wait_ge(v_step, done[0])

            base = cst[:, C_BASE:C_BASE + X]
            step(v.tensor_scalar(n2[:, :, :], counts[:, :, :], float(CAP), None, ALU.min))
            step(v.tensor_tensor(nn[:, :], n2[:, 0, :], n2[:, 1, :], ALU.add))
            step(v.tensor_scalar(ni[:, :], nn[:, :], float(P - 1), None, ALU.add))
            v.tensor_copy(lim[:, E:X], base[:, E:X])
            step(v.tensor_single_scalar(nsh[:, :], ni[:, :], 7, ALU.logical_shift_right))
            v.tensor_scalar(gap[:, 0:E], nn[:, :], -float(P), 0.0, ALU.add, ALU.max)
            step(v.tensor_copy(nt[:, :], nsh[:, :]))
            v.tensor_tensor(lim[:, 0:E], gap[:, 0:E], base[:, 0:E], ALU.add)
            step(v.tensor_tensor_scan(end[:, :], cst[:, C_ONES:C_ONES + E], nt[:, :], 0.0, ALU.mult, ALU.add))
            v.tensor_scalar(past[:, :], end[:, :], cst[:, C_PART:C_PART + 1], None, ALU.is_le)
            v.tensor_scalar(jump[:, 0, :], nt[:, :], -float(P), float(REG), ALU.mult, ALU.add)
            v.tensor_copy(jump[:, 1, :], cst[:, C_ONES:C_ONES + E])
            step(v.tensor_tensor(jump[:, 2, :], lim[:, 1:X], lim[:, 0:E], ALU.subtract))
            step(v.tensor_tensor(taken[:, :, :], jump[:, :, :], past[:, :].unsqueeze(1).broadcast_to([P, 3, E]), ALU.mult))
            step(v.reduce_sum(at[:, 0:3], taken[:, :, :], AX.X))
            v.tensor_tensor(at[:, 2:3], at[:, 2:3], lim[:, 0:1], ALU.add)
            v.tensor_scalar(at[:, 1:2], at[:, 1:2], float(E - 1), None, ALU.min)
            step(v.tensor_scalar(at[:, 0:1], at[:, 0:1], cst[:, C_PART128:C_PART128 + 1], None, ALU.add))
            v.tensor_tensor(at[:, 0:1], at[:, 0:1], at[:, 2:3], ALU.min).then_inc(listed, 1)
            v.wait_ge(list_mm, 1)
            v.tensor_copy(table[0:1, :, :], ps_g[0][0:1, 0:2 * P].rearrange("p (k t) -> p k t", k=2)).then_inc(tabled, 1)

            def remap(n):
                if n == 0:
                    v.tensor_copy(edge[:, 0:X], base)
                    v.memset(first[:, E:X], float(NS))
                    v.memset(off[:, E:X], 0.0)
                    step(v.tensor_tensor(first[:, 0:E], end[:, :], nt[:, :], ALU.subtract))
                    step(v.scalar_tensor_tensor(edge[:, X:X + E], nt[:, :], float(P), base[:, 0:E], ALU.mult, ALU.add))
                    v.tensor_copy(edge[:, X + E:], base[:, E:X])
                    step(v.tensor_scalar(edge[:, X:X + E], edge[:, X:X + E], -float(P), None, ALU.add))
                    step(v.tensor_tensor(off[:, 0:E], edge[:, X:X + E], lim[:, 0:E], ALU.subtract))
                    step(v.tensor_scalar(off[:, 0:E], off[:, 0:E], 0.0, None, ALU.max))
                    step(v.scalar_tensor_tensor(gap[:, :], first[:, :], float(P), base, ALU.mult, ALU.subtract))
                if n == 1:
                    v.tensor_copy(shift[:, X:], off[:, :])
                    v.tensor_copy(shift[:, 0:1], gap[:, 0:1])
                    step(v.tensor_tensor(shift[:, 1:X], gap[:, 1:X], gap[:, 0:E], ALU.subtract))
                    step(v.tensor_tensor(shift[:, 1:X], shift[:, 1:X], off[:, 0:E], ALU.subtract))
                    step(v.tensor_copy(slot_f[:, :], idx_all[:, :, :]))
                if n in (2, 3, 4, 5):
                    part = slice(NT // 2 * (n - 2), NT // 2 * (n - 1))
                    where = behind[:, part, :]
                    wide = [P, NT // 2, 2 * X]
                    step(v.tensor_tensor(where, slot_f[:, part].unsqueeze(2).broadcast_to(wide), edge[:, :].unsqueeze(1).broadcast_to(wide), ALU.is_ge))
                    step(v.tensor_tensor(where, where, shift[:, :].unsqueeze(1).broadcast_to(wide), ALU.mult))
                    step(v.reduce_sum(moved[:, part], where, AX.X))
                if n == 6:
                    v.tensor_tensor(idx_all[:, :, :], slot_f[:, :], moved[:, :], ALU.add)

            def turn(ts):
                if ts.has(HID):
                    t, p = ts.at(HID)
                    v.wait_ge(sg_done, t + 1)
                    ge(v, h_mm, t - 3)
                    v.tensor_tensor(hh[p % 4][:, :], ps_g[p % 2][:, P:2 * P], sg[p % 2][:, :], ALU.mult).then_inc(h_done, 1)
                if ts.has(TH - 1):
                    t, p = ts.at(TH - 1)
                    v.wait_ge(h_mm, t + 1)
                    ge(v, y_mm, t - 3)
                    v.tensor_copy(hT[p % 4][:, :], ps_h[p % 2][:, 0:P]).then_inc(hT_done, 1)
                if ts.reg is None and 0 <= ts.const < 7:
                    remap(ts.const)
            turns(v, NS, BACK, AHEAD, turn, U)


def phase3(nc, NT, ctxT_in, keep, ybuf):
    cst, x_all, idx_all, w_all = keep["cst"], keep["x_all"], keep["idx_all"], keep["w_all"]
    HP = H1 // 2
    with ExitStack() as ctx:
        def sb(name, shape, dt=F32):
            return ctx.enter_context(nc.sbuf_tensor(name, shape, dt))

        def sem(name):
            return ctx.enter_context(nc.semaphore(name))

        ident = cst[:, C_ID:C_ID + P]
        wq, wk, wv, wo_raw, bq, bk, bv, bo = (keep[n] for n in ("wq", "wk", "wv", "wo", "bq", "bk", "bv", "bo"))
        wo = sb("p3_wo", [P, HP, D])
        cT = [sb(f"p3_cT{i}", [D, P]) for i in range(2)]
        idx = [sb(f"p3_idx{i}", [P, 2], I32) for i in range(2)]
        gy = [[sb(f"p3_gy{i}{k}", [P, D]) for k in range(2)] for i in range(2)]
        stat, mv, rstd = ([sb(f"p3_{n}{i}", [P, k]) for i in range(2)] for n, k in (("st", 6), ("mv", 2), ("rs", 1)))
        xln = [sb(f"p3_xln{i}", [P, D]) for i in range(2)]
        xT = [sb(f"p3_xT{i}", [D, P]) for i in range(2)]
        qT = [sb(f"p3_qT{i}", [P, HP, 2, S]) for i in range(2)]
        kb = [sb(f"p3_kb{i}", [P, HP, 2, 2, S]) for i in range(2)]
        vd = [sb(f"p3_vd{i}", [P, 2, HP, D1]) for i in range(2)]
        vb = [sb(f"p3_vb{i}", [P, 2, HP, 2, D1]) for i in range(2)]
        pr = [sb(f"p3_pr{i}", [P, 2, HP, S]) for i in range(2)]
        mx, sm = ([sb(f"p3_{n}{i}", [P, 2, HP]) for i in range(2)] for n in ("mx", "sm"))
        rc = [sb(f"p3_rc{i}", [P, 2 * HP, 2]) for i in range(2)]
        oT = [sb(f"p3_oT{i}", [P, HP, 2, S]) for i in range(2)]

        ps_r = ctx.enter_context(nc.psum_tensor("p3_r", [P, 2, 512], F32))
        ps_s = ctx.enter_context(nc.psum_tensor("p3_s", [P, 2, HP, S], F32))
        ps_o = ctx.enter_context(nc.psum_tensor("p3_o", [P, 2, HP, S], F32))
        ps_x = ctx.enter_context(nc.psum_tensor("p3_x", [P, 512], F32))
        ps_w = ctx.enter_context(nc.psum_tensor("p3_w", [P, 512], F32))

        setup = sem("setup3")
        c_ld = [sem(f"c3_ld{i}") for i in range(2)]
        idx_done = sem("idx3_done")
        got = [sem(f"got{i}") for i in range(2)]
        mixed, x2_done, mv_done, rs_done, xln_done = (sem(n) for n in ("mixed", "x2r_done", "mv3_done", "rs3_done", "xln3_done"))
        turned_x, xT_done, q_mm, q_done, k_mm, k_done, v_mm, vd_done, vb_done = (
            sem(n) for n in ("turned3_x", "xT3_done", "q3_mm", "q3_done", "k3_mm", "k3_done", "v3_mm", "vd_done", "vb3_done"))
        s_mm, sub_done, exp_done, rc_done, o_mm, oT_done, ao_mm, x3_done = (
            sem(n) for n in ("s3_mm", "sub3_done", "exp3_done", "rc3_done", "o3_mm", "oT3_done", "ao3_mm", "x3_done"))
        v_step, g_step = sem("v_step3"), sem("g_step3")
        passed = sem("passed")
        block = ctx.enter_context(nc.Block())

        @block.sync
        def _(sp):
            def turn(ts):
                if ts.has(2):
                    t, p = ts.at(2)
                    ge(sp, v_mm, 2 * t - 2)
                    sp.dma_start(cT[p][:, :], one(ctxT_in, t)).then_inc(c_ld[p], 16)
            turns(sp, NT, 2, 4, turn)

        @block.tensor
        def _(pe):
            pe.wait_ge(setup, 1)

            def turn(ts):
                if ts.has(0):
                    t, p = ts.at(0)
                    pe.wait_ge(k_done, 2 * t + 2)
                    pe.wait_ge(q_done, 2 * t + 2)
                    for b in range(2):
                        ge(pe, sub_done, 2 * t - 1 + b)
                        for c in range(HP):
                            last = pe.matmul(ps_s[:, b, c, :], kb[p][:, c, b, :, :], qT[p][:, c, b, :], start=True, stop=True)
                        last.then_inc(s_mm, 1)
                if ts.has(-1):
                    t, p = ts.at(-1)
                    pe.wait_ge(vb_done, t + 1)
                    pe.wait_ge(exp_done, 2 * t + 2)
                    for b in range(2):
                        ge(pe, oT_done, 2 * t - 1 + b)
                        for c in range(HP):
                            last = pe.matmul(ps_o[:, b, c, :], vb[p][:, b, c, :, :], pr[p][:, b, c, :], start=True, stop=True)
                        last.then_inc(o_mm, 1)
                if ts.has(1):
                    t, p = ts.at(1)
                    pe.wait_ge(xT_done, t + 1)
                    pe.wait_ge(c_ld[p], (ts.lap(1) + 1) * 16)
                    for h in range(2):
                        ge(pe, vd_done, 2 * t - 1 + h)
                        for c in range(4):
                            last = pe.matmul(ps_r[:, h, P * c:P * c + P], wq[:, P * (4 * h + c):P * (4 * h + c + 1)], xT[p][:, :], start=True, stop=True)
                        last.then_inc(q_mm, 1)
                    for h in range(2):
                        pe.wait_ge(q_done, 2 * t + 1 + h)
                        for c in range(4):
                            last = pe.matmul(ps_r[:, h, P * c:P * c + P], wk[:, P * (4 * h + c):P * (4 * h + c + 1)], cT[p][:, :], start=True, stop=True)
                        last.then_inc(k_mm, 1)
                    for b in range(2):
                        pe.wait_ge(k_done, 2 * t + 1 + b)
                        for x in range(2):
                            last = pe.matmul(ps_r[64 * x:64 * x + 64, b, :], cT[p][:, S * b:S * b + S], wv[:, 512 * x:512 * x + 512], start=True, stop=True)
                        last.then_inc(v_mm, 1)
                if ts.has(2):
                    t, p = ts.at(2)
                    pe.wait_ge(xln_done, t + 1)
                    ge(pe, xT_done, t)
                    pe.transpose(ps_x[:, 0:P], xln[p][:, :], ident).then_inc(turned_x, 1)
                if ts.has(-1):
                    t, p = ts.at(-1)
                    pe.wait_ge(oT_done, 2 * t + 2)
                    ge(pe, x3_done, t)
                    for c in range(HP):
                        last = pe.matmul(ps_w[:, 0:D], oT[p][:, c, :, :], wo[:, c, :], start=(c == 0), stop=(c == HP - 1))
                    last.then_inc(ao_mm, 1)
            turns(pe, NT, 2, 4, turn)

        @block.scalar
        def _(act):
            act.wait_ge(setup, 1)

            def turn(ts):
                for b in range(2):
                    if ts.has(0):
                        t, p = ts.at(0)
                        act.wait_ge(sub_done, 2 * t + 1 + b)
                        act.activation(pr[p][:, b, :, :], pr[p][:, b, :, :], ACT.Exp).then_inc(exp_done, 1)
                    if ts.has(-1):
                        t, p = ts.at(-1)
                        act.wait_ge(o_mm, 2 * t + 1 + b)
                        ge(act, ao_mm, t - 1)
                        act.activation(oT[p][:, :, b, :], ps_o[:, b, :, :], ACT.Copy).then_inc(oT_done, 1)
                if ts.has(1):
                    t, p = ts.at(1)
                    ge(act, s_mm, 2 * t - 2)
                    for h in range(2):
                        act.wait_ge(q_mm, 2 * t + 1 + h)
                        for c in range(4):
                            last = act.activation(qT[p][:, 4 * h + c, :, :], ps_r[:, h, P * c:P * c + P], ACT.Identity, bias=bq[:, 4 * h + c:4 * h + c + 1])
                        last.then_inc(q_done, 1)
                    for h in range(2):
                        act.wait_ge(k_mm, 2 * t + 1 + h)
                        for c in range(4):
                            for x in range(2):
                                rows = slice(64 * x, 64 * x + 64)
                                last = act.activation(kb[p][rows, 4 * h + c, :, x, :], ps_r[rows, h, P * c:P * c + P].rearrange("p (b s) -> p b s", b=2), ACT.Identity,
                                                      bias=bk[rows, 4 * h + c:4 * h + c + 1])
                        last.then_inc(k_done, 1)
                if ts.has(2):
                    t, p = ts.at(2)
                    act.wait_ge(turned_x, t + 1)
                    ge(act, q_mm, 2 * t - 2)
                    act.activation(xT[p][:, :], ps_x[:, 0:P], ACT.Copy).then_inc(xT_done, 1)
            turns(act, NT, 2, 4, turn)

        @block.gpsimd
        def _(g):
            g.wait_ge(setup, 1)
            half = cst[:, C_HALF:C_HALF + 1]
            steps = Steps(g, g_step)

            def turn(ts):
                steps.turn(ts, NT, {"eps": (3, 1), "idx": (4, 1)})
                if ts.has(4):
                    t, p = ts.at(4)
                    ge(g, mixed, t - 1)
                    steps.did("idx", g.tensor_copy(idx[p][:, :], mid(idx_all, t)))
                    for k in range(2):
                        alone(g, passed)
                        g.indirect_dma_start(gy[p][k][:, :], None, ybuf, bass.IndirectOffsetOnAxis(ap=idx[p][:, k:k + 1], axis=0)
                                             ).then_inc(got[p], 16)
                if ts.has(3):
                    t, p = ts.at(3)
                    g.wait_ge(mv_done, t + 1)
                    ge(g, xln_done, t - 1)
                    alone(g, passed)
                    steps.did("eps", g.tensor_scalar(rstd[p][:, :], mv[p][:, 1:2], EPS, None, ALU.add))
                    g.tensor_tensor(rstd[p][:, :], rstd[p][:, :], half, ALU.pow).then_inc(rs_done, 1)
                if ts.has(0):
                    t, p = ts.at(0)
                    g.wait_ge(rc_done, t + 1)
                    g.wait_ge(vd_done, 2 * t + 2)
                    ge(g, o_mm, 2 * t - 2)
                    g.tensor_tensor(vb[p][:, :, :, :, :].rearrange("p b c x d -> p (b c) x d"),
                                    vd[p][:, :, :, :].rearrange("p b c d -> p (b c) d").unsqueeze(2).broadcast_to([P, 2 * HP, 2, D1]),
                                    rc[p][:, :, :].unsqueeze(3).broadcast_to([P, 2 * HP, 2, D1]), ALU.mult).then_inc(vb_done, 1)
            turns(g, NT, 2, 4, turn)

        @block.vector
        def _(v):
            for p in range(2):
                v.memset(kb[p][:, :, :, :, :], 0.0)
                v.memset(rc[p][:, :, :], 0.0)
            v.tensor_scalar(wo[:, :, :], wo_raw[:, :, :], D1 ** -0.5, None, ALU.mult).then_inc(setup, 1)
            steps = Steps(v, v_step)

            def turn(ts):
                steps.turn(ts, NT, {"max": (0, 2), "sum": (0, 1), "mix": (3, 3)})
                if ts.has(0):
                    t, p = ts.at(0)
                    ge(v, o_mm, 2 * t - 2)
                    for b in range(2):
                        v.wait_ge(s_mm, 2 * t + 1 + b)
                        steps.did("max", v.tensor_reduce(mx[p][:, b, :], ps_s[:, b, :, :], AX.X, ALU.max))
                        v.tensor_tensor(pr[p][:, b, :, :], ps_s[:, b, :, :], mx[p][:, b, :].unsqueeze(2).broadcast_to([P, HP, S]),
                                        ALU.subtract).then_inc(sub_done, 1)
                if ts.has(3):
                    t, p = ts.at(3)
                    v.wait_ge(got[p], (ts.lap(3) + 1) * 32)
                    wt = mid(w_all, t)
                    steps.did("mix", v.scalar_tensor_tensor(mid(x_all, t), gy[p][0][:, :], wt[:, 0:1], mid(x_all, t), ALU.mult, ALU.add))
                    v.scalar_tensor_tensor(mid(x_all, t), gy[p][1][:, :], wt[:, 1:2], mid(x_all, t), ALU.mult, ALU.add).then_inc(mixed, 1)
                    v.wait_ge(mixed, t + 1)
                    alone(v, passed)
                    steps.did("mix", v.bn_stats(stat[p][:, :], mid(x_all, t)))
                    alone(v, passed)
                    v.bn_aggr(mv[p][:, :], stat[p][:, :]).then_inc(mv_done, 1)
                if ts.has(0):
                    t, p = ts.at(0)
                    ge(v, vb_done, t - 1)
                    v.wait_ge(exp_done, 2 * t + 2)
                    steps.did("sum", v.reduce_sum(sm[p][:, :, :], pr[p][:, :, :, :], AX.X))
                    for x in range(2):
                        rows = slice(64 * x, 64 * x + 64)
                        last = v.reciprocal(rc[p][rows, :, x], sm[p][rows, :, :].rearrange("p b c -> p (b c)"))
                    last.then_inc(rc_done, 1)
                if ts.has(3):
                    t, p = ts.at(3)
                    v.wait_ge(rs_done, t + 1)
                    ge(v, turned_x, t - 1)
                    v.tensor_scalar(xln[p][:, :], mid(x_all, t), mv[p][:, 0:1], rstd[p][:, :], ALU.subtract, ALU.mult).then_inc(xln_done, 1)
                    v.wait_ge(xln_done, t + 1)
                    steps.did("mix", v.tensor_tensor(mid(x_all, t), mid(x_all, t), bo[:, :], ALU.add))
                if ts.has(1):
                    t, p = ts.at(1)
                    ge(v, vb_done, t - 1)
                    for b in range(2):
                        v.wait_ge(v_mm, 2 * t + 1 + b)
                        v.tensor_tensor(vd[p][:, b, :, :], ps_r[:, b, :], bv[:, :], ALU.add).then_inc(vd_done, 1)
                if ts.has(-1):
                    t, p = ts.at(-1)
                    v.wait_ge(ao_mm, t + 1)
                    v.tensor_tensor(mid(x_all, t), ps_w[:, 0:D], mid(x_all, t), ALU.add).then_inc(x3_done, 1)
            turns(v, NT, 2, 4, turn)


def phase4(nc, NT, w1T, w2T, keep, out):
    cst, x_all = keep["cst"], keep["x_all"]
    FC = FF // P
    with ExitStack() as ctx:
        def sb(name, shape, dt=F32):
            return ctx.enter_context(nc.sbuf_tensor(name, shape, dt))

        def sem(name):
            return ctx.enter_context(nc.semaphore(name))

        ones = cst[:, C_ONES:C_ONES + P]
        idb = sb("p4_idb", [P, P], BF16)
        wf, wr = [sb(f"p4_wf{i}", [P, FF]) for i in range(2)], sb("p4_wr", [P, FF])
        wi = [sb(f"p4_wi{i}", [P, FF], BF16) for i in range(2)]
        wsum = sb("p4_wsum", [P, 2])
        ws, wrs = sb("p4_ws", [P, 2]), sb("p4_wrs", [P, 2])
        stat, mv, rstd, am, qs, ds, am2, qs2, ds2 = ([sb(f"p4_{n}{i}", [P, k]) for i in range(2)] for n, k in (
            ("st", 6), ("mv", 2), ("rs", 1), ("am", 1), ("qs", 1), ("ds", 1), ("am2", 1), ("qs2", 1), ("ds2", 1)))
        xln, xf = ([sb(f"p4_{n}{i}", [P, D]) for i in range(2)] for n in ("xln", "xf"))
        xi, xiT = ([sb(f"p4_{n}{i}", [P, D], BF16) for i in range(2)] for n in ("xi", "xiT"))
        h, hf = ([sb(f"p4_{n}{i}", [P, FF]) for i in range(2)] for n in ("h", "hf"))
        hi, hiT = ([sb(f"p4_{n}{i}", [P, FC, P], BF16) for i in range(2)] for n in ("hi", "hiT"))
        y = [sb(f"p4_y{i}", [P, D]) for i in range(2)]
        ps_x = [ctx.enter_context(nc.psum_tensor(f"p4_psx{i}", [P, 1024], BF16)) for i in range(2)]
        ps_t = [ctx.enter_context(nc.psum_tensor(f"p4_pst{i}", [P, 1024], BF16)) for i in range(2)]
        ps_h = [ctx.enter_context(nc.psum_tensor(f"p4_psh{i}", [P, 512], F32)) for i in range(2)]
        ps_y = [ctx.enter_context(nc.psum_tensor(f"p4_psy{i}", [P, 512], F32)) for i in range(2)]

        w_in, summed, w_mm, setup = sem("w4_in"), sem("summed"), sem("w4_mm"), sem("setup4")
        mv_done, rs_done, xi_done, x_mm, xiT_done, h_mm, h_done, hi_done, t_mm, hiT_done, y_mm, y_done = (
            sem(n) for n in ("mv4_done", "rs4_done", "xi_done", "x4_mm", "xiT_done", "h4_mm", "h4_done", "hi_done", "t4_mm", "hiT_done", "y4_mm", "y4_done"))
        st = [sem(f"out_st{i}") for i in range(2)]
        v_step, g_step, s_step = sem("v_step4"), sem("g_step4"), sem("s_step4")
        passed = sem("passed")
        block = ctx.enter_context(nc.Block())

        @block.sync
        def _(sp):
            sp.dma_start(wf[0][:, :], w1T).then_inc(w_in, 16)
            sp.dma_start(wf[1][:, :].rearrange("p (c d) -> p c d", c=FC), w2T.rearrange("(c p) d -> p c d", p=P)).then_inc(w_in, 16)

            def turn(ts):
                if ts.has(-3):
                    t, p = ts.at(-3)
                    sp.wait_ge(y_done, t + 1)
                    sp.dma_start(one(out, t), y[p][:, :]).then_inc(st[p], 16)
            turns(sp, NT, 3, 2, turn)
            for p in range(2):
                sp.wait_ge(st[p], 16 * (NT // 2))

        @block.tensor
        def _(pe):
            pe.wait_ge(summed, 1)
            pe.matmul(ps_y[0][:, 0:2], ones, wsum[:, :], start=True, stop=True).then_inc(w_mm, 1)
            pe.wait_ge(setup, 1)

            def turn(ts):
                if ts.has(1):
                    t, p = ts.at(1)
                    pe.wait_ge(xi_done, t + 1)
                    ge(pe, xiT_done, t - 1)
                    pe.transpose(ps_x[p][:, 0:P], xi[p][:, :], idb[:, :]).then_inc(x_mm, 1)
                if ts.has(0):
                    t, p = ts.at(0)
                    pe.wait_ge(xiT_done, t + 1)
                    ge(pe, h_done, t - 1)
                    pe.matmul(ps_h[p][:, :], xiT[p][:, :], wi[0][:, :], start=True, stop=True).then_inc(h_mm, 1)
                if ts.has(-1):
                    t, p = ts.at(-1)
                    pe.wait_ge(hi_done, t + 1)
                    ge(pe, hiT_done, t - 1)
                    for c in range(FC):
                        last = pe.transpose(ps_t[p][:, P * c:P * c + P], hi[p][:, c, :], idb[:, :])
                    last.then_inc(t_mm, 1)
                if ts.has(-2):
                    t, p = ts.at(-2)
                    pe.wait_ge(hiT_done, t + 1)
                    ge(pe, y_done, t - 1)
                    for c in range(FC):
                        last = pe.matmul(ps_y[p][:, 0:D], hiT[p][:, c, :], wi[1][:, P * c:P * c + P], start=(c == 0), stop=(c == FC - 1))
                    last.then_inc(y_mm, 1)
            turns(pe, NT, 3, 2, turn)

        @block.scalar
        def _(act):
            act.wait_ge(setup, 1)

            def turn(ts):
                if ts.has(1):
                    t, p = ts.at(1)
                    act.wait_ge(x_mm, t + 1)
                    ge(act, h_mm, t - 1)
                    act.activation(xiT[p][:, :], ps_x[p][:, 0:P], ACT.Copy).then_inc(xiT_done, 1)
                if ts.has(0):
                    t, p = ts.at(0)
                    act.wait_ge(h_mm, t + 1)
                    ge(act, hi_done, t - 1)
                    act.activation(h[p][:, :], ps_h[p][:, :], ACT.Gelu, scale=ds[p][:, :]).then_inc(h_done, 1)
                if ts.has(-1):
                    t, p = ts.at(-1)
                    act.wait_ge(t_mm, t + 1)
                    ge(act, y_mm, t - 1)
                    act.activation(hiT[p][:, :, :], ps_t[p][:, 0:FF], ACT.Copy).then_inc(hiT_done, 1)
            turns(act, NT, 3, 2, turn)

        @block.gpsimd
        def _(g):
            g.wait_ge(setup, 1)
            half = cst[:, C_HALF:C_HALF + 1]
            steps = Steps(g, g_step)

            def turn(ts):
                steps.turn(ts, NT, {"eps": (2, 1)})
                if ts.has(2):
                    t, p = ts.at(2)
                    g.wait_ge(mv_done, t + 1)
                    ge(g, xi_done, t - 1)
                    alone(g, passed)
                    steps.did("eps", g.tensor_scalar(rstd[p][:, :], mv[p][:, 1:2], EPS, None, ALU.add))
                    g.tensor_tensor(rstd[p][:, :], rstd[p][:, :], half, ALU.pow).then_inc(rs_done, 1)
            turns(g, NT, 3, 2, turn)

        @block.vector
        def _(v):
            done = [0]

            def step(ins):
                ins.then_inc(s_step, 1)
                done[0] += 1
                v.wait_ge(s_step, done[0])

            v.wait_ge(w_in, 32)
            v.tensor_copy(idb[:, :], cst[:, C_ID:C_ID + P])
            for i in range(2):
                ins = v.tensor_reduce(wsum[:, i:i + 1], wf[i][:, :], AX.X, ALU.add, apply_absolute_value=True)
            ins.then_inc(summed, 1)
            v.wait_ge(w_mm, 1)
            step(v.tensor_scalar(ws[:, :], ps_y[0][:, 0:2], 1.0 / (FF * D), EPS, ALU.mult, ALU.max))
            step(v.reciprocal(wrs[:, :], ws[:, :]))
            for i in range(2):
                step(v.tensor_scalar(wr[:, :], wf[i][:, :], wrs[:, i:i + 1], MAGIC, ALU.mult, ALU.add))
                step(v.tensor_scalar(wr[:, :], wr[:, :], -MAGIC, 1.0, ALU.add, ALU.min))
                ins = v.tensor_scalar(wi[i][:, :], wr[:, :], -1.0, None, ALU.max)
                if i == 0:
                    step(ins)
            ins.then_inc(setup, 1)
            steps = Steps(v, v_step)

            def turn(ts):
                steps.turn(ts, NT, {"st": (2, 6), "h": (-1, 4)})
                if ts.has(-1):
                    t, p = ts.at(-1)
                    v.wait_ge(h_done, t + 1)
                    ge(v, y_done, t - 1)
                    steps.did("h", v.tensor_reduce(am2[p][:, :], h[p][:, :], AX.X, ALU.max, apply_absolute_value=True))
                    steps.did("h", v.tensor_scalar(am2[p][:, :], am2[p][:, :], EPS, 1.0 / 127.0, ALU.max, ALU.mult))
                    v.tensor_scalar(ds2[p][:, :], am2[p][:, :], ws[:, 1:2], None, ALU.mult)
                    steps.did("h", v.reciprocal(qs2[p][:, :], am2[p][:, :]))
                    steps.did("h", v.tensor_scalar(hf[p][:, :], h[p][:, :], qs2[p][:, :], MAGIC, ALU.mult, ALU.add))
                    ge(v, t_mm, t - 1)
                    v.tensor_scalar(hi[p][:, :, :], hf[p][:, :], -MAGIC, None, ALU.add).then_inc(hi_done, 1)
                if ts.has(2):
                    t, p = ts.at(2)
                    alone(v, passed)
                    steps.did("st", v.bn_stats(stat[p][:, :], mid(x_all, t)))
                    alone(v, passed)
                    v.bn_aggr(mv[p][:, :], stat[p][:, :]).then_inc(mv_done, 1)
                if ts.has(-2):
                    t, p = ts.at(-2)
                    v.wait_ge(y_mm, t + 1)
                    ge(v, st[p], ts.lap(-2) * 16)
                    v.scalar_tensor_tensor(y[p][:, :], ps_y[p][:, 0:D], ds2[p][:, :], mid(x_all, t), ALU.mult, ALU.add).then_inc(y_done, 1)
                if ts.has(2):
                    t, p = ts.at(2)
                    v.wait_ge(rs_done, t + 1)
                    steps.did("st", v.tensor_scalar(xln[p][:, :], mid(x_all, t), mv[p][:, 0:1], rstd[p][:, :], ALU.subtract, ALU.mult))
                    steps.did("st", v.tensor_reduce(am[p][:, :], xln[p][:, :], AX.X, ALU.max, apply_absolute_value=True))
                    steps.did("st", v.tensor_scalar(am[p][:, :], am[p][:, :], EPS, 1.0 / 127.0, ALU.max, ALU.mult))
                    ge(v, h_done, t - 1)
                    v.tensor_scalar(ds[p][:, :], am[p][:, :], ws[:, 0:1], None, ALU.mult)
                    steps.did("st", v.reciprocal(qs[p][:, :], am[p][:, :]))
                    steps.did("st", v.tensor_scalar(xf[p][:, :], xln[p][:, :], qs[p][:, :], MAGIC, ALU.mult, ALU.add))
                    ge(v, x_mm, t - 1)
                    v.tensor_scalar(xi[p][:, :], xf[p][:, :], -MAGIC, None, ALU.add).then_inc(xi_done, 1)
            turns(v, NT, 3, 2, turn)


def program(nc, NT, a, out):
    xbuf = nc.dram_tensor("slots_in", [ZERO + P, D], F32).ap()
    ybuf = nc.dram_tensor("slots_out", [(slot_tiles(NT * P) + 1) * P, D], F32).ap()
    with ExitStack() as ctx:
        def sb(name, shape, dt=F32):
            return ctx.enter_context(nc.sbuf_tensor(name, shape, dt))

        keep = dict(x_all=sb("x_all", [P, NT, D]), idx_all=sb("idx_all", [P, NT, 2], I32), w_all=sb("w_all", [P, NT, 2]),
                    counts=sb("counts", [P, 2, E]), cst=sb("cst", [P, N_CONST]), gu=sb("gu", [D, E * 2 * P]), dn=sb("dn", [P, E * D]),
                    wq=sb("l1_wq", [D, H1 * D1]), wk=sb("l1_wk", [D, H1 * D1]), wv=sb("l1_wv", [D, H1 * D1]), wo=sb("l1_wo", [P, H1 // 2, D]),
                    bq=sb("l1_bq", [P, H1 // 2]), bk=sb("l1_bk", [P, H1 // 2]), bv=sb("l1_bv", [P, H1 * D1 // 2]), bo=sb("l1_bo", [P, D]))
        names = dict(wq="Wq", wk="Wk", wv="Wv", wo="Wo", bq="bq", bk="bk", bv="bv", bo="bo")
        w0 = {k: a["L0_xattn_" + n] for k, n in names.items()} | {"wr": a["L0_ffn_router_w"]}
        w1 = {k: a["L1_xattn_" + n] for k, n in names.items()}
        later = [(keep["gu"][:, :].rearrange("d (e h) -> d e h", e=E)[:, :, 0:P], a["L0_ffn_gate_w"]),
                 (keep["gu"][:, :].rearrange("d (e h) -> d e h", e=E)[:, :, P:2 * P], a["L0_ffn_up_w"]),
                 (keep["dn"][:, :].rearrange("h (e d) -> h e d", e=E), a["L0_ffn_down_w"])]
        HP = H1 // 2
        for n in ("wq", "wk", "bq", "bk"):
            later.append((keep[n][:, :], w1[n]))
        later.append((keep["wo"][:, :, :], w1["wo"].rearrange("(c p) n -> p c n", p=P)))
        later.append((keep["bo"][:, :], spread(w1["bo"])))
        for x in range(2):
            later.append((keep["wv"][:, :].rearrange("p (x c d) -> p x c d", x=2, c=HP)[:, x], w1["wv"].rearrange("p (c x d) -> p x c d", x=2, c=HP)[:, x]))
            later.append((keep["bv"][64 * x:64 * x + 64, :].rearrange("p (c d) -> p c d", c=HP), spread(w1["bv"].rearrange("(c x d) -> x c d", x=2, c=HP)[x], 64)))
        phase1(nc, NT, a["x"], a["ctx_twice"], a["constants"], w0, keep, xbuf, ybuf, later)
        phase2(nc, NT, keep, xbuf, ybuf)
        phase3(nc, NT, a["ctx_turned"], keep, ybuf)
        phase4(nc, NT, a["L1_ffn_w1"], a["L1_ffn_w2"], keep, out)


def kernel(x, ctx_1024, **weights):
    import numpy as np
    import concourse.bacc as bacc
    from concourse.bass_utils import run_bass_kernel_spmd

    batch, s, d = x.shape
    nt = batch * s // P
    ctx_t = np.asarray(ctx_1024).reshape(nt, 2, s, d).transpose(0, 3, 1, 2)
    laid = {
        "x": np.asarray(x).reshape(batch * s, d),
        "ctx_turned": ctx_t.reshape(nt, d, 2 * s),
        "ctx_twice": np.broadcast_to(ctx_t[:, :, :, None, :], (nt, d, 2, 2, s)),
        "constants": constants(),
    }
    for name, v in weights.items():
        laid[name] = np.asarray(v)
    for name in ("L0_ffn_gate_w", "L0_ffn_up_w", "L0_ffn_down_w"):
        laid[name] = laid[name].transpose(1, 0, 2)
    for name in ("L1_ffn_w1", "L1_ffn_w2"):
        laid[name] = laid[name].T
    for name in ("L1_xattn_bq", "L1_xattn_bk"):
        laid[name] = laid[name].reshape(H1 // 2, P).T
    laid = {k: np.ascontiguousarray(v) for k, v in laid.items()}
    nc = bacc.Bacc("TRN2", target_bir_lowering=False, num_devices=1)
    a = {k: nc.dram_tensor(f"in_{k}", v.shape, mybir.dt.from_np(v.dtype), kind="ExternalInput").ap() for k, v in laid.items()}
    out = nc.dram_tensor("out_x", [nt, P, d], F32, kind="ExternalOutput").ap()
    program(nc, nt, a, out)
    r = run_bass_kernel_spmd(nc, [{f"in_{k}": v for k, v in laid.items()}], core_ids=[0])
    return r.results[0]["out_x"].reshape(batch, s, d)
```

```python
from contextlib import ExitStack

import concourse.bass as bass
from concourse import mybir

F32 = mybir.dt.float32
BF16 = mybir.dt.bfloat16
I32 = mybir.dt.int32
U32 = mybir.dt.uint32
ALU = mybir.AluOpType
ACT = mybir.ActivationFunctionType
AX = mybir.AxisListType

P = 128
S = 64
D = 128
E = 16
CAP = 640
REG = 2 * CAP
H0, D0 = 16, 8
H1, D1 = 16, 64
ZERO = E * REG
FF = 512
EPS = 1e-5
X = E + 1
PACK = 6
MAGIC = 12582912.0

C_ID, C_TRI, C_ONES = 0, 128, 256
C_MASK = 384
C_EVEN, C_ODD = 392, 393
C_IOTA = 394
C_BASE = 410
C_DROP = 427
C_HALF = 428
C_PART, C_PART128 = 429, 430
N_CONST = 512


def slot_tiles(tokens):
    return (2 * tokens + E * (P - 1)) // P + 1


def constants():
    import numpy as np

    c = np.zeros((P, N_CONST), np.float32)
    part = np.arange(P)
    c[:, C_ID:C_ID + P] = np.eye(P)
    c[:, C_TRI:C_TRI + P] = part[:, None] < part[None, :]
    c[:, C_ONES:C_ONES + P] = 1.0
    c[:, C_MASK:C_MASK + 8] = (part[:, None] % 64) // D0 == np.arange(8)[None, :]
    c[:, C_EVEN] = (part // D0) % 2 == 0
    c[:, C_ODD] = (part // D0) % 2 == 1
    c[:, C_IOTA:C_IOTA + E] = np.arange(E)
    c[:, C_BASE:C_BASE + E + 1] = np.arange(E + 1) * REG
    c[:, C_DROP] = ZERO + part
    c[:, C_HALF] = -0.5
    c[:, C_PART] = part
    c[:, C_PART128] = P * part
    return c


def ge(eng, sem, value):
    if isinstance(value, int) and value <= 0:
        return
    eng.wait_ge(sem, value)


def alone(eng, passed):
    eng.sem_inc(passed, 1)


class Tiles:

    def __init__(self, total, reg, const, unroll, buffers):
        self.total, self.reg, self.const, self.unroll, self.buffers = total, reg, const, unroll, buffers

    def at(self, off):
        k = self.const + off
        return (k if self.reg is None else self.reg * self.unroll + k), k % self.buffers

    def lap(self, off):
        k = (self.const + off) // self.buffers
        return k if self.reg is None else self.reg * (self.unroll // self.buffers) + k

    def has(self, off):
        return self.reg is not None or 0 <= self.const + off < self.total

    def full(self, off):
        return self.has(off) and (self.const + off) % self.unroll == self.unroll - 1


def turns(eng, total, back, ahead, body, unroll, buffers):
    first = back + 4
    steady = max(0, (total - ahead - first) // unroll)
    for n in range(-ahead, first if steady else total + back):
        body(Tiles(total, None, n, unroll, buffers))
    if steady:
        with eng.Fori(0, steady) as i:
            for k in range(unroll):
                body(Tiles(total, i, first + k, unroll, buffers))
        for n in range(first + unroll * steady, total + back):
            body(Tiles(total, None, n, unroll, buffers))


class Steps:

    def __init__(self, eng, sem):
        self.eng, self.sem, self.before, self.k = eng, sem, 0, 0

    def turn(self, ts, total, kinds, grouped={}):
        u = ts.unroll
        if ts.reg is None:
            self.before = sum(c * max(0, min(total, ts.const + off)) for off, c in kinds.values())
            self.before += sum(c * (max(0, min(total, ts.const + off)) // u) for off, c in grouped.values())
        else:
            self.before = sum(c * (ts.const + off) for off, c in kinds.values()) + ts.reg * (u * sum(c for _, c in kinds.values()))
            if grouped:
                self.before = self.before + sum(c * ((ts.const + off) // u) for off, c in grouped.values()) + ts.reg * sum(c for _, c in grouped.values())
        self.k = 0

    def did(self, kind, ins):
        ins.then_inc(self.sem, 1)
        self.k += 1
        self.eng.wait_ge(self.sem, self.before + self.k)


def cols(vec):
    return vec.rearrange("(p a) -> p a", a=1)


def mid1(ap, t):
    return ap[:, t:t + 1] if isinstance(t, int) else ap[:, bass.ds(t, 1)]


def spread(vec, n=P):
    return vec.partition_broadcast(n)


def one(ap, t):
    if isinstance(t, int):
        return ap[t]
    return ap[bass.ds(t, 1)].squeeze(0)


def mid(ap, t):
    if isinstance(t, int):
        return ap[:, t]
    return ap[:, bass.ds(t, 1)].squeeze(1)


def group(ap, g, n):
    if isinstance(g, int):
        return ap[:, n * g:n * g + n]
    return ap[:, bass.ds(g * n, n)]


def phase1(nc, NT, x_in, ctx_dup, consts_in, w, keep, xbuf, ybuf, later):
    x_all, idx_all, w_all = keep["x_all"], keep["idx_all"], keep["w_all"]
    G = 4
    NG = NT // G
    with ExitStack() as ctx:
        def sb(name, shape, dt=F32):
            return ctx.enter_context(nc.sbuf_tensor(name, shape, dt))

        def sem(name):
            return ctx.enter_context(nc.semaphore(name))

        cst = keep["cst"]
        ident = cst[:, C_ID:C_ID + P]
        wq, wk, wv, wo = (sb(f"p1_{n}", [D, D]) for n in ("wq", "wk", "wv", "wo"))
        wr = sb("p1_wr", [D, E])
        bq, bk = sb("p1_bq", [P, 1]), sb("p1_bk", [P, 1])
        bqm = sb("p1_bqm", [P, 8])
        bv, bo = sb("p1_bv", [P, D]), sb("p1_bo", [P, D])
        tri, ones = sb("p1_tri", [P, P], BF16), sb("p1_ones", [P, P], BF16)

        cT = [sb(f"p1_cT{i}", [D, 2, 2, S]) for i in range(G)]
        stat, mv_all, rstd_all = sb("p1_st", [P, NT, 6]), sb("p1_mv", [P, NT, 2]), sb("p1_rs", [P, NT])
        stat2, mv2, rstd2 = sb("p1_st2", [P, 6]), sb("p1_mv2", [P, G, 2]), sb("p1_rs2", [P, G])
        xln = [sb(f"p1_xln{i}", [P, D]) for i in range(2)]
        xT = [sb(f"p1_xT{i}", [D, P]) for i in range(2)]
        kb = [sb(f"p1_kb{i}", [P, 2, 2, S]) for i in range(2)]
        qm = [sb(f"p1_qm{i}", [P, 2, 8, S]) for i in range(2)]
        pr = [sb(f"p1_pr{i}", [P, 2, 4, 2, S]) for i in range(2)]
        mx, sm, rc = ([sb(f"p1_{n}{i}", [P, 16]) for i in range(2)] for n in ("mx", "sm", "rc"))
        pT = [sb(f"p1_pT{i}", [P, 2, 4, P]) for i in range(2)]
        vb = [sb(f"p1_vb{i}", [P, 2, 4, 2, 2 * D0]) for i in range(2)]
        od = sb("p1_od", [P, 2, S])
        oT = [sb(f"p1_oT{i}", [P, 2, S]) for i in range(2)]
        x2 = [sb(f"p1_x2{i}", [P, D]) for i in range(G)]
        x2_kept = [sb(f"p1_x2k{i}", [P, D]) for i in range(G)]
        x2T = [sb(f"p1_x2T{i}", [D, P]) for i in range(2)]
        lg, ex = sb("p1_lg", [P, G, 24]), sb("p1_ex", [P, G, 24])
        i8, idf = sb("p1_i8", [P, G, 8], U32), sb("p1_idf", [P, G, 2])
        z = sb("p1_z", [P, G])
        oh = sb("p1_oh", [P, G, 2, E], BF16)
        carry = sb("p1_carry", [P, 2, E])
        rk, cl, slot = sb("p1_rk", [P, G, 2, E]), sb("p1_cl", [P, G, E]), sb("p1_slot", [P, G, E])
        mm, red = sb("p1_mm", [P, 2, G, 2, E]), sb("p1_red", [P, 2, G, 2])
        kp, kz, pos = sb("p1_kp", [P, G, 2]), sb("p1_kz", [P, G, 2]), sb("p1_pos", [P, G, 2])
        idx = [sb(f"p1_idx{i}", [P, 2], I32) for i in range(G)]

        ps_s = ctx.enter_context(nc.psum_tensor("ps_s", [P, 2, 4, 2, S], F32))
        ps_p = ctx.enter_context(nc.psum_tensor("ps_p", [P, 2, 4, P], F32))
        ps_x = ctx.enter_context(nc.psum_tensor("ps_x", [P, 4, P], F32))
        ps_q = ctx.enter_context(nc.psum_tensor("ps_q", [P, 4, P], F32))
        ps_v = ctx.enter_context(nc.psum_tensor("ps_v", [P, 512], F32))
        ps_o = ctx.enter_context(nc.psum_tensor("ps_o", [P, 4, P], F32))
        LG, RK, CT = 256, 320, 448

        zeros = sb("p1_zeros", [P, D])
        w_in, cst_in, later_in, zero_st = sem("w_in"), sem("cst_in"), sem("later_in"), sem("zero_st")
        x_ld, c_ld = [sem(f"x_ld{i}") for i in range(NG)], [sem(f"c_ld{i}") for i in range(G)]
        setup = sem("setup")
        mv_done, rs_done, xln_done, bo_done = sem("mv_done"), sem("rs_done"), sem("xln_done"), sem("bo_done")
        turned_x, xT_done = sem("turned_x"), sem("xT_done")
        qk_mm, k_done, qm_done = sem("qk_mm"), sem("k_done"), sem("qm_done")
        v_mm, vb_done = sem("v_mm"), sem("vb_done")
        s_mm, sub_done, exp_done = sem("s_mm"), sem("sub_done"), sem("exp_done")
        rc_done, pr_done, turned_p, pT_done = sem("rc_done"), sem("pr_done"), sem("turned_p"), sem("pT_done")
        o_mm, oT_done, ao_mm, x1_done = sem("o_mm"), sem("oT_done"), sem("ao_mm"), sem("x1_done")
        mv2_done, rs2_done, x2_done = sem("mv2_done"), sem("rs2_done"), sem("x2_done")
        turned_x2, x2T_done, lg_mm, lg_read, top_done = sem("turned_x2"), sem("x2T_done"), sem("lg_mm"), sem("lg_read"), sem("top_done")
        rexp_done, oh_done, rk_mm, rk_done = sem("rexp_done"), sem("oh_done"), sem("rk_mm"), sem("rk_done")
        max_done, st2_done, sm_done, od_done = sem("max_done"), sem("st2_done"), sem("sm_done"), sem("od_done")
        idx_done, kept, top_step, rank_step = sem("idx_done"), sem("kept"), sem("top_step"), sem("rank_step")
        sc = [sem(f"scattered{i}") for i in range(G)]
        g_step, start_step, rs_step = sem("g_step"), sem("start_step"), sem("rs_step")
        passed = sem("passed")
        n2, nn = sb("p2_n2", [P, 2, E]), sb("p2_nn", [P, E])
        ni, nsh = sb("p2_ni", [P, E], I32), sb("p2_nsh", [P, E], I32)
        nt, end, lim = keep["nt"], keep["end"], keep["lim"]
        gap, jump = sb("p2_gap", [P, E]), sb("p2_jump", [P, 3, E])
        past, taken, at = sb("p2_past", [P, E]), sb("p2_taken", [P, 3, E]), sb("p2_at", [P, 4])
        table = keep["table"]
        who, word = sb("p2_who", [1, P + PACK]), sb("p2_word", [1, P])
        listed, list_mm, tabled, t_step = sem("listed"), sem("list_mm"), sem("tabled"), sem("t_step")
        block = ctx.enter_context(nc.Block())

        xg = x_in.rearrange("(g t p) d -> g p t d", t=G, p=P)
        X2, LOG, RANK, KEEP, SCAT = -5, -6, -7, -8, -10
        BACK, AHEAD = 10, 4

        @block.sync
        def _(sp):
            sp.dma_start(cst[:, :], consts_in).then_inc(cst_in, 16)
            for g in range(NG):
                sp.dma_start(x_all[:, g * G:(g + 1) * G, :], xg[g]).then_inc(x_ld[g], 16)
            sp.wait_ge(setup, 3)
            sp.dma_start(xbuf[0:ZERO, :].rearrange("(e r) d -> r e d", e=E)[0:P], zeros[:, :].unsqueeze(1).broadcast_to([P, E, D])).then_inc(zero_st, 16)
            sp.dma_start(xbuf[ZERO:ZERO + P, :], zeros[:, :]).then_inc(zero_st, 16)
            sp.dma_start(ybuf[slot_tiles(NT * P) * P:, :], zeros[:, :]).then_inc(zero_st, 16)

            def turn(ts):
                if ts.reg is None and ts.const == 2:
                    for dst, src in later:
                        sp.dma_start(dst, src).then_inc(later_in, 16)
                if ts.has(3):
                    t, p = ts.at(3)
                    ge(sp, v_mm, t - G + 1)
                    sp.dma_start(cT[p][:, :, :, :], one(ctx_dup, t)).then_inc(c_ld[p], 16)
            turns(sp, NT, BACK, AHEAD, turn, G, G)
            sp.wait_ge(later_in, 16 * len(later))

        @block.tensor
        def _(pe):
            pe.wait_ge(w_in, 192)
            pe.wait_ge(cst_in, 16)
            pe.wait_ge(setup, 3)

            def turn(ts):
                if ts.has(0):
                    t, p = ts.at(0)
                    p %= 2
                    pe.wait_ge(k_done, t + 1)
                    pe.wait_ge(qm_done, t + 1)
                    for b in range(2):
                        ge(pe, sub_done, 2 * t - 1 + b)
                        for j in range(4):
                            last = pe.matmul(ps_s[:, b, j, :, :], qm[p][:, b, 2 * j:2 * j + 2, :], kb[p][:, b, :, :], start=True, stop=True)
                        last.then_inc(s_mm, 1)
                if ts.has(-1):
                    t, p = ts.at(-1)
                    p %= 2
                    for b in range(2):
                        pe.wait_ge(pr_done, 2 * t + 1 + b)
                        ge(pe, pT_done, 2 * t - 1 + b)
                        for j in range(4):
                            last = pe.transpose(ps_p[:, b, j, :], pr[p][:, b, j, :, :], ident)
                        last.then_inc(turned_p, 1)
                if ts.has(LOG):
                    t, p = ts.at(LOG)
                    pe.wait_ge(x2_done, t + 1)
                    pe.wait_ge(xT_done, (t + 3 - LOG) if not isinstance(t, int) else min(t + 3 - LOG, NT))
                    pe.transpose(ps_x[:, 1, :], x2[p][:, :], ident).then_inc(turned_x2, 1)
                if ts.has(-1):
                    t, p = ts.at(-1)
                    p %= 2
                    ge(pe, x1_done, t)
                    for b in range(2):
                        pe.wait_ge(pT_done, 2 * t + 1 + b)
                        for j in range(4):
                            last = pe.matmul(ps_o[32 * j:32 * j + 32, b, :], vb[p][:, b, j, :, :], pT[p][:, b, j, :], start=True, stop=True)
                    last.then_inc(o_mm, 1)
                if ts.has(LOG):
                    t, p = ts.at(LOG)
                    pe.wait_ge(x2T_done, t + 1)
                    pe.wait_ge(vb_done, (t + 1 - LOG) if not isinstance(t, int) else min(t + 1 - LOG, NT))
                    if ts.full(LOG - 1):
                        ge(pe, lg_read, ts.lap(LOG - 1) + 1)
                    if ts.full(RANK - 1):
                        ge(pe, rk_done, ts.lap(RANK - 1) + 1)
                    k = (ts.const + LOG) % G
                    pe.matmul(ps_v[:, LG + 16 * k:LG + 16 * k + 16], x2T[p % 2][:, :], wr[:, :], start=True, stop=True).then_inc(lg_mm, 1)
                if ts.full(RANK):
                    g = ts.lap(RANK)
                    pe.wait_ge(oh_done, g + 1)
                    pe.wait_ge(lg_read, g + 1)
                    pe.wait_ge(vb_done, (g * G + G - RANK) if not isinstance(g, int) else min(g * G + G - RANK, NT))
                    pe.matmul(ps_v[:, RK:RK + G * 32], tri[:, :], oh[:, :, :, :], start=True, stop=False)
                    for k in range(1, G):
                        pe.matmul(ps_v[:, RK + 32 * k:RK + G * 32], ones[:, :], oh[:, 0:G - k, :, :], start=False, stop=(k == G - 1))
                    for k in range(G):
                        last = pe.matmul(ps_v[:, CT:CT + 32], ones[:, :], oh[:, k, :, :], start=(k == 0), stop=(k == G - 1))
                    last.then_inc(rk_mm, 1)
                if ts.has(2):
                    t, p = ts.at(2)
                    pe.wait_ge(xT_done, t + 1)
                    ge(pe, k_done, t)
                    ge(pe, qm_done, t)
                    pe.wait_ge(c_ld[p], (ts.lap(2) + 1) * 16)
                    pe.matmul(ps_q[:, 0, :], wq[:, :], xT[p % 2][:, :], start=True, stop=True)
                    pe.matmul(ps_q[:, 1, :], wk[:, :], cT[p][:, :, 0, :], start=True, stop=True).then_inc(qk_mm, 1)
                if ts.has(1):
                    t, p = ts.at(1)
                    ge(pe, vb_done, t)
                    if ts.full(LOG):
                        ge(pe, lg_read, ts.lap(LOG) + 1)
                    if ts.full(RANK):
                        ge(pe, rk_done, ts.lap(RANK) + 1)
                    for b in range(2):
                        last = pe.matmul(ps_v[:, 128 * b:128 * b + 128], cT[p][:, b, :, :], wv[:, :], start=True, stop=True)
                    last.then_inc(v_mm, 1)
                if ts.has(-1):
                    t, p = ts.at(-1)
                    pe.wait_ge(oT_done, t + 1)
                    pe.matmul(ps_o[:, 2, :], oT[p % 2][:, :, :], wo[:, :], start=True, stop=True).then_inc(ao_mm, 1)
                if ts.has(3):
                    t, p = ts.at(3)
                    pe.wait_ge(xln_done, t + 1)
                    ge(pe, x2T_done, t - 3 + LOG + 1)
                    pe.transpose(ps_x[:, 0, :], xln[p % 2][:, :], ident).then_inc(turned_x, 1)
            turns(pe, NT, BACK, AHEAD, turn, G, G)
            pe.wait_ge(listed, 1)
            for k in range(2):
                last = pe.matmul(ps_q[0:1, k, :], at[:, k:k + 1], ident, start=True, stop=True)
            last.then_inc(list_mm, 1)

        @block.scalar
        def _(act):
            for dst, src in ((wq, w["wq"]), (wk, w["wk"]), (wv, w["wv"]), (wr, w["wr"]),
                             (bq, cols(w["bq"])), (bk, cols(w["bk"])), (bv, spread(w["bv"])), (bo, spread(w["bo"]))):
                act.dma_start(dst[:, :], src).then_inc(w_in, 16)
            for j in range(4):
                act.dma_start(wo[32 * j:32 * j + 32, :], w["wo"].rearrange("(r j c) n -> j r c n", r=2, j=4)[j]).then_inc(w_in, 16)
            act.wait_ge(w_in, 192)
            act.wait_ge(cst_in, 16)
            act.wait_ge(setup, 3)
            mask = cst[:, C_MASK:C_MASK + 8]

            def turn(ts):
                if ts.has(-1):
                    t, p = ts.at(-1)
                    ge(act, o_mm, t - 1)
                    for r in range(2):
                        act.wait_ge(turned_p, 2 * t + 1 + r)
                        act.activation(pT[p % 2][:, r, :, :], ps_p[:, r, :, :], ACT.Copy).then_inc(pT_done, 1)
                if ts.has(LOG):
                    t, p = ts.at(LOG)
                    act.wait_ge(turned_x2, t + 1)
                    ge(act, lg_mm, t - 1)
                    act.activation(x2T[p % 2][:, :], ps_x[:, 1, :], ACT.Copy).then_inc(x2T_done, 1)
                if ts.has(0):
                    t, p = ts.at(0)
                    p %= 2
                    for r in range(2):
                        act.wait_ge(sub_done, 2 * t + 1 + r)
                        act.activation(pr[p][:, r, :, :, :], pr[p][:, r, :, :, :], ACT.Exp, scale=D0 ** -0.5).then_inc(exp_done, 1)
                if ts.has(2):
                    t, p = ts.at(2)
                    p %= 2
                    act.wait_ge(qk_mm, t + 1)
                    ge(act, s_mm, 2 * t - 2)
                    for r in range(2):
                        rows = slice(64 * r, 64 * r + 64)
                        last = act.activation(kb[p][rows, :, r, :], ps_q[rows, 1, :].rearrange("p (b s) -> p b s", b=2), ACT.Identity, bias=bk[rows, :])
                    last.then_inc(k_done, 1)
                    for j in range(8):
                        last = act.activation(qm[p][:, :, j, :], ps_q[:, 0, :].rearrange("p (b s) -> p b s", b=2), ACT.Identity,
                                              bias=bqm[:, j:j + 1], scale=mask[:, j:j + 1])
                    last.then_inc(qm_done, 1)
                if ts.full(LOG):
                    act.wait_ge(top_done, ts.lap(LOG) + 1)
                    act.activation(ex[:, :, :], ex[:, :, :], ACT.Exp).then_inc(rexp_done, 1)
                if ts.has(KEEP):
                    t, p = ts.at(KEEP)
                    act.wait_ge(x2_done, t + 1)
                    ge(act, sc[p], ts.lap(KEEP) * 32)
                    act.activation(x2_kept[p][:, :], x2[p][:, :], ACT.Copy).then_inc(kept, 1)
                if ts.has(3):
                    t, p = ts.at(3)
                    act.wait_ge(turned_x, t + 1)
                    ge(act, qk_mm, t - 1)
                    act.activation(xT[p % 2][:, :], ps_x[:, 0, :], ACT.Copy).then_inc(xT_done, 1)
            turns(act, NT, BACK, AHEAD, turn, G, G)

        @block.gpsimd
        def _(g):
            g.wait_ge(w_in, 192)
            g.wait_ge(cst_in, 16)
            half = cst[:, C_HALF:C_HALF + 1]
            steps = Steps(g, g_step)
            for q in range(NG):
                rs = rstd_all[:, G * q:G * q + G]
                g.wait_ge(mv_done, q + 1)
                g.tensor_scalar(rs, mv_all[:, G * q:G * q + G, 1], EPS, None, ALU.add).then_inc(rs_step, 1)
                g.wait_ge(rs_step, q + 1)
                g.tensor_tensor(rs, rs, half.broadcast_to([P, G]), ALU.pow).then_inc(rs_done, 1)

            def turn(ts):
                steps.turn(ts, NT, {"idx": (SCAT, 1)}, {"eps2": (-2, 1)})
                if ts.full(-2):
                    q = ts.lap(-2)
                    g.wait_ge(mv2_done, q * G + G)
                    ge(g, x2_done, q * G)
                    alone(g, passed)
                    steps.did("eps2", g.tensor_scalar(rstd2[:, :], mv2[:, :, 1], EPS, None, ALU.add))
                    g.tensor_tensor(rstd2[:, :], rstd2[:, :], half.broadcast_to([P, G]), ALU.pow).then_inc(rs2_done, 1)
                if ts.has(3):
                    t, p = ts.at(3)
                    g.wait_ge(xln_done, t + 1)
                    alone(g, passed)
                    g.tensor_tensor(mid(x_all, t), mid(x_all, t), bo[:, :], ALU.add).then_inc(bo_done, 1)
                if ts.has(0):
                    t, p = ts.at(0)
                    p %= 2
                    for b in range(2):
                        g.wait_ge(rc_done, 2 * t + 1 + b)
                        probs = pr[p][:, b, :, :, :].rearrange("p j r k -> p (j r) k")
                        g.tensor_tensor(probs, probs, rc[p][:, 8 * b:8 * b + 8].unsqueeze(2).broadcast_to([P, 8, S]), ALU.mult).then_inc(pr_done, 1)
                if ts.has(SCAT):
                    t, p = ts.at(SCAT)
                    g.wait_ge(idx_done, ts.lap(SCAT) + 1)
                    g.wait_ge(kept, t + 1)
                    if ts.reg is None:
                        g.wait_ge(zero_st, 48)
                    ge(g, sc[p], ts.lap(SCAT) * 32)
                    steps.did("idx", g.tensor_copy(idx[p][:, :], mid(idx_all, t)))
                    for k in range(2):
                        alone(g, passed)
                        g.indirect_dma_start(xbuf, bass.IndirectOffsetOnAxis(ap=idx[p][:, k:k + 1], axis=0), x2_kept[p][:, :], None,
                                             bounds_check=ZERO - 1, oob_is_err=False).then_inc(sc[p], 16)
            turns(g, NT, BACK, AHEAD, turn, G, G)
            for p in range(G):
                g.wait_ge(sc[p], 32 * (NT // G))

        @block.vector
        def _(v):
            for g in range(NG):
                v.wait_ge(x_ld[g], 16)
                for t in range(G * g, G * g + G):
                    last = v.bn_stats(stat[:, t, :], x_all[:, t, :])
                last.then_inc(start_step, 1)
                v.wait_ge(start_step, g + 1)
                for t in range(G * g, G * g + G):
                    last = v.bn_aggr(mv_all[:, t, :], stat[:, t, :])
                last.then_inc(mv_done, 1)
            for p in range(2):
                v.memset(vb[p][:, :, :, :, :], 0.0)
                v.memset(kb[p][:, :, :, :], 0.0)
            v.memset(carry[:, :, :], 0.0)
            v.memset(zeros[:, :], 0.0)
            v.wait_ge(w_in, 192)
            v.wait_ge(cst_in, 16)
            mask = cst[:, C_MASK:C_MASK + 8]
            v.tensor_scalar(bqm[:, :], mask, bq[:, :], None, ALU.mult).then_inc(setup, 1)
            v.tensor_copy(tri[:, :], cst[:, C_TRI:C_TRI + P]).then_inc(setup, 1)
            v.tensor_copy(ones[:, :], cst[:, C_ONES:C_ONES + P]).then_inc(setup, 1)
            v.wait_ge(setup, 3)
            iota = cst[:, C_IOTA:C_IOTA + E]
            base = cst[:, C_BASE:C_BASE + E]
            drop = cst[:, C_DROP:C_DROP + 1]
            even, odd = cst[:, C_EVEN:C_EVEN + 1], cst[:, C_ODD:C_ODD + 1]

            def top(ts, part):
                if not ts.full(LOG):
                    return
                g = ts.lap(LOG)
                if part == 0:
                    v.wait_ge(lg_mm, g * G + G)
                    ge(v, rexp_done, g)
                    v.tensor_copy(lg[:, :, 0:16], ps_v[:, LG:LG + 16 * G].rearrange("p (g e) -> p g e", g=G)).then_inc(lg_read, 1)
                if part == 1:
                    v.wait_ge(lg_read, g + 1)
                    for k in range(G):
                        alone(v, passed)
                        last = v.max(lg[:, k, 16:24], lg[:, k, 0:16])
                    last.then_inc(top_step, 1)
                if part == 2:
                    v.wait_ge(top_step, g * 3 + 1)
                    v.tensor_tensor(ex[:, :, :], lg[:, :, :], lg[:, :, 16:17].broadcast_to([P, G, 24]), ALU.subtract).then_inc(top_done, 1)
                    for k in range(G):
                        last = v.max_index(i8[:, k, :], lg[:, k, 16:24], lg[:, k, 0:16])
                    last.then_inc(top_step, 1)
                if part == 3:
                    v.wait_ge(top_step, g * 3 + 2)
                    v.tensor_copy(idf[:, :, :], i8[:, :, 0:2]).then_inc(top_step, 1)
                if part == 4:
                    v.wait_ge(top_step, g * 3 + 3)
                    ge(v, rk_mm, g)
                    v.tensor_tensor(oh[:, :, :, :], iota.unsqueeze(1).unsqueeze(1).broadcast_to([P, G, 2, E]),
                                    idf[:, :, :].unsqueeze(3).broadcast_to([P, G, 2, E]), ALU.is_equal).then_inc(oh_done, 1)

            def rank(ts, part):
                if not ts.full(RANK):
                    return
                g = ts.lap(RANK)
                if part == 0:
                    v.wait_ge(rexp_done, g + 1)
                    v.reduce_sum(z[:, :], ex[:, :, 0:16], AX.X).then_inc(rank_step, 1)
                if part == 1:
                    v.wait_ge(rk_mm, g + 1)
                    ge(v, rk_done, g)
                    v.tensor_tensor(rk[:, :, :, :], ps_v[:, RK:RK + 32 * G].rearrange("p (g k e) -> p g k e", g=G, k=2),
                                    carry[:, :, :].unsqueeze(1).broadcast_to([P, G, 2, E]), ALU.add).then_inc(rank_step, 1)
                if part == 2:
                    v.wait_ge(rank_step, g * 8 + 2)
                    v.tensor_tensor(carry[:, :, :], ps_v[:, CT:CT + 32].rearrange("p (k e) -> p k e", k=2), carry[:, :, :], ALU.add).then_inc(rk_done, 1)
                    v.scalar_tensor_tensor(cl[:, :, :], rk[:, :, 1, :], float(CAP), base.unsqueeze(1).broadcast_to([P, G, E]), ALU.min, ALU.add)
                    v.reciprocal(z[:, :], z[:, :]).then_inc(rank_step, 1)
                if part == 3:
                    v.wait_ge(rank_step, g * 8 + 3)
                    v.tensor_tensor(mm[:, 0, :, :, :], oh[:, :, :, :], rk[:, :, :, :], ALU.mult)
                    v.scalar_tensor_tensor(slot[:, :, :], rk[:, :, 0, :], float(CAP), cl[:, :, :], ALU.min, ALU.add).then_inc(rank_step, 1)
                if part == 4:
                    v.wait_ge(rank_step, g * 8 + 4)
                    v.tensor_tensor(mm[:, 1, :, :, :], oh[:, :, :, :], slot[:, :, :].unsqueeze(2).broadcast_to([P, G, 2, E]), ALU.mult).then_inc(rank_step, 1)
                if part == 5:
                    v.wait_ge(rank_step, g * 8 + 5)
                    v.reduce_sum(red[:, :, :, :], mm[:, :, :, :, :], AX.X).then_inc(rank_step, 1)
                if part == 6:
                    v.wait_ge(rank_step, g * 8 + 6)
                    v.tensor_scalar(kp[:, :, :], red[:, 0, :, :], float(CAP), None, ALU.is_lt).then_inc(rank_step, 1)
                if part == 7:
                    v.wait_ge(rank_step, g * 8 + 7)
                    v.scalar_tensor_tensor(pos[:, :, :], red[:, 1, :, :], drop, kp[:, :, :], ALU.subtract, ALU.mult)
                    v.tensor_tensor(kz[:, :, :], kp[:, :, :], z[:, :].unsqueeze(2).broadcast_to([P, G, 2]), ALU.mult).then_inc(rank_step, 1)
                if part == 8:
                    v.wait_ge(rank_step, g * 8 + 8)
                    v.tensor_tensor(group(w_all, g, G), ex[:, :, 16:18], kz[:, :, :], ALU.mult)
                    v.tensor_scalar(group(idx_all, g, G), pos[:, :, :], drop, None, ALU.add).then_inc(idx_done, 1)

            def sums(ts, b):
                if ts.has(0):
                    t, p = ts.at(0)
                    v.wait_ge(exp_done, 2 * t + 1 + b)
                    ge(v, pr_done, 2 * t - 3 + b)
                    v.reduce_sum(sm[p % 2][:, 8 * b:8 * b + 8], pr[p % 2][:, b, :, :, :].rearrange("p j r k -> p (j r) k"), AX.X).then_inc(sm_done, 1)

            def inverses(ts, b):
                if ts.has(0):
                    t, p = ts.at(0)
                    v.wait_ge(sm_done, 2 * t + 1 + b)
                    v.reciprocal(rc[p % 2][:, 8 * b:8 * b + 8], sm[p % 2][:, 8 * b:8 * b + 8]).then_inc(rc_done, 1)

            def statistics(ts):
                if ts.has(-2):
                    t, p = ts.at(-2)
                    v.wait_ge(st2_done, t + 1)
                    ge(v, x2_done, t - G + 1)
                    alone(v, passed)
                    v.bn_aggr(mv2[:, p, :], stat2[:, :]).then_inc(mv2_done, 1)

            def turn(ts):
                if ts.has(-2) and not ts.has(0):
                    statistics(ts)
                if ts.has(0):
                    t, p = ts.at(0)
                    p %= 2
                    ge(v, turned_p, 2 * t - 2)
                    for r in range(2):
                        v.wait_ge(s_mm, 2 * t + 1 + r)
                        m = mx[p][:, 8 * r:8 * r + 8]
                        scores = ps_s[:, r, :, :, :].rearrange("p j h k -> p (j h) k")
                        v.tensor_reduce(m, scores, AX.X, ALU.max).then_inc(max_done, 1)
                        if r == 0:
                            statistics(ts)
                        v.wait_ge(max_done, 2 * t + 1 + r)
                        v.tensor_tensor(pr[p][:, r, :, :, :].rearrange("p j h k -> p (j h) k"), scores, m.unsqueeze(2).broadcast_to([P, 8, S]),
                                        ALU.subtract).then_inc(sub_done, 1)
                sums(ts, 0)
                if ts.has(-1):
                    t, p = ts.at(-1)
                    v.wait_ge(o_mm, t + 1)
                    ge(v, ao_mm, t - 1)
                    v.tensor_scalar(od[:, :, :], ps_o[:, 0:2, S:2 * S], odd, None, ALU.mult).then_inc(od_done, 1)
                inverses(ts, 0)
                rank(ts, 0)
                top(ts, 0)
                if ts.has(-1):
                    t, p = ts.at(-1)
                    v.wait_ge(od_done, t + 1)
                    v.scalar_tensor_tensor(oT[p % 2][:, :, :], ps_o[:, 0:2, 0:S], even, od[:, :, :], ALU.mult, ALU.add).then_inc(oT_done, 1)
                rank(ts, 1)
                top(ts, 1)
                rank(ts, 2)
                top(ts, 2)
                sums(ts, 1)
                rank(ts, 3)
                top(ts, 3)
                inverses(ts, 1)
                if ts.has(X2):
                    t, p = ts.at(X2)
                    v.wait_ge(rs2_done, ts.lap(X2) + 1)
                    ge(v, turned_x2, t - G + 1)
                    ge(v, kept, t - G + 1)
                    v.tensor_scalar(x2[p][:, :], mid(x_all, t), mv2[:, p, 0:1], rstd2[:, p:p + 1], ALU.subtract, ALU.mult).then_inc(x2_done, 1)
                rank(ts, 4)
                top(ts, 4)
                if ts.has(1):
                    t, p = ts.at(1)
                    v.wait_ge(v_mm, t + 1)
                    ge(v, o_mm, t - 1)
                    for r in range(2):
                        rows = slice(64 * r, 64 * r + 64)
                        ins = v.tensor_tensor(
                            vb[p % 2][rows, :, :, r, :],
                            ps_v[rows, 0:256].rearrange("p (b r j c) -> p b r j c", b=2, r=2, j=4)[:, :, r, :, :],
                            bv[rows, :].rearrange("p (r j c) -> p r j c", r=2, j=4)[:, r, :, :].unsqueeze(1).broadcast_to([64, 2, 4, 16]),
                            ALU.add)
                    ins.then_inc(vb_done, 1)
                rank(ts, 5)
                rank(ts, 6)
                if ts.has(-1):
                    t, p = ts.at(-1)
                    v.wait_ge(ao_mm, t + 1)
                    v.wait_ge(bo_done, t + 1)
                    v.tensor_tensor(mid(x_all, t), ps_o[:, 2, :], mid(x_all, t), ALU.add).then_inc(x1_done, 1)
                if ts.has(4):
                    t, p = ts.at(4)
                    v.wait_ge(rs_done, ts.lap(4) + 1)
                    ge(v, turned_x, t - 1)
                    v.tensor_scalar(xln[p % 2][:, :], mid(x_all, t), mid(mv_all, t)[:, 0:1], mid1(rstd_all, t), ALU.subtract, ALU.mult).then_inc(xln_done, 1)
                rank(ts, 7)
                if ts.has(-1):
                    t, p = ts.at(-1)
                    ge(v, mv2_done, t)
                    v.wait_ge(x1_done, t + 1)
                    alone(v, passed)
                    v.bn_stats(stat2[:, :], mid(x_all, t)).then_inc(st2_done, 1)
                rank(ts, 8)
            turns(v, NT, BACK, AHEAD, turn, G, G)
            v.wait_ge(rk_done, NG)
            done = [0]

            def step(ins):
                ins.then_inc(t_step, 1)
                done[0] += 1
                v.wait_ge(t_step, done[0])

            base = cst[:, C_BASE:C_BASE + X]
            step(v.tensor_scalar(n2[:, :, :], carry[:, :, :], float(CAP), None, ALU.min))
            step(v.tensor_tensor(nn[:, :], n2[:, 0, :], n2[:, 1, :], ALU.add))
            step(v.tensor_scalar(ni[:, :], nn[:, :], float(P - 1), None, ALU.add))
            v.tensor_copy(lim[:, E:X], base[:, E:X])
            step(v.tensor_single_scalar(nsh[:, :], ni[:, :], 7, ALU.logical_shift_right))
            v.tensor_scalar(gap[:, 0:E], nn[:, :], -float(P), 0.0, ALU.add, ALU.max)
            step(v.tensor_copy(nt[:, :], nsh[:, :]))
            v.tensor_tensor(lim[:, 0:E], gap[:, 0:E], base[:, 0:E], ALU.add)
            step(v.tensor_tensor_scan(end[:, :], cst[:, C_ONES:C_ONES + E], nt[:, :], 0.0, ALU.mult, ALU.add))
            v.tensor_scalar(past[:, :], end[:, :], cst[:, C_PART:C_PART + 1], None, ALU.is_le)
            v.tensor_scalar(jump[:, 0, :], nt[:, :], -float(P), float(REG), ALU.mult, ALU.add)
            v.tensor_copy(jump[:, 1, :], cst[:, C_ONES:C_ONES + E])
            step(v.tensor_tensor(jump[:, 2, :], lim[:, 1:X], lim[:, 0:E], ALU.subtract))
            step(v.tensor_tensor(taken[:, :, :], jump[:, :, :], past[:, :].unsqueeze(1).broadcast_to([P, 3, E]), ALU.mult))
            step(v.reduce_sum(at[:, 0:3], taken[:, :, :], AX.X))
            v.tensor_tensor(at[:, 2:3], at[:, 2:3], lim[:, 0:1], ALU.add)
            v.tensor_scalar(at[:, 1:2], at[:, 1:2], float(E - 1), None, ALU.min)
            step(v.tensor_scalar(at[:, 0:1], at[:, 0:1], cst[:, C_PART128:C_PART128 + 1], None, ALU.add))
            v.tensor_tensor(at[:, 0:1], at[:, 0:1], at[:, 2:3], ALU.min).then_inc(listed, 1)
            v.wait_ge(list_mm, 1)
            v.memset(who[:, P:], 0.0)
            v.tensor_copy(table[0:1, 0, :], ps_q[0:1, 0, :]).then_inc(tabled, 1)
            step(v.tensor_copy(who[:, 0:P], ps_q[0:1, 1, :]))
            last = who[:, PACK - 1:PACK - 1 + P]
            for k in reversed(range(PACK - 1)):
                ins = v.scalar_tensor_tensor(word[:, :] if k else table[0:1, 1, :], last, float(E), who[:, k:k + P], ALU.mult, ALU.add)
                last = word[:, :]
                if k:
                    step(ins)
            ins.then_inc(tabled, 1)


def phase2(nc, NT, keep, xbuf, ybuf):
    NS = slot_tiles(NT * P)
    cst, idx_all = keep["cst"], keep["idx_all"]
    gu, dn = keep["gu"], keep["dn"]
    U, R = 16, 8
    with ExitStack() as ctx:
        def sb(name, shape, dt=F32):
            return ctx.enter_context(nc.sbuf_tensor(name, shape, dt))

        def sem(name):
            return ctx.enter_context(nc.semaphore(name))

        ident = cst[:, C_ID:C_ID + P]
        nt, end, lim, table = (keep[n] for n in ("nt", "end", "lim", "table"))
        edge, shift = sb("p2_edge", [P, 2 * X]), sb("p2_shift", [P, 2 * X])
        first, off, gap = sb("p2_first", [P, X]), sb("p2_off", [P, X]), sb("p2_gap2", [P, X])
        slot_f, moved = sb("p2_slotf", [P, NT * 2]), sb("p2_moved", [P, NT * 2])
        behind = sb("p2_behind", [P, NT * 2, 2 * X])
        xe = [sb(f"p2_xe{i}", [P, D]) for i in range(R)]
        xT = [sb(f"p2_xT{i}", [D, P]) for i in range(4)]
        sg = [sb(f"p2_sg{i}", [P, P]) for i in range(2)]
        hh = [sb(f"p2_h{i}", [P, P]) for i in range(4)]
        hT = [sb(f"p2_hT{i}", [P, P]) for i in range(4)]
        ye = [sb(f"p2_ye{i}", [P, D]) for i in range(R)]
        ps_x, ps_g, ps_h, ps_y = ([ctx.enter_context(nc.psum_tensor(f"p2_{n}{i}", [P, 512], F32)) for i in range(2)]
                                  for n in ("psx", "psg", "psh", "psy"))

        x_ld = [sem(f"xe_ld{i}") for i in range(R)]
        y_st = [sem(f"ye_st{i}") for i in range(R)]
        x_mm, xT_done, g_mm, sg_done, h_done, h_mm, hT_done, y_mm, y_done = (
            sem(n) for n in ("x_mm", "xT2_done", "g_mm", "sg_done", "h_done", "h_mm", "hT_done", "y_mm", "y_done"))
        v_step = sem("v_step2")
        passed = sem("passed")
        block = ctx.enter_context(nc.Block())
        LOAD, TX, HID, TH, DOWN, OUT = 7, 2, -1, -2, -4, -5
        BACK, AHEAD = 6, 7
        row_known, word_known = {}, {}

        def rows(ts):
            looped, at = ts.reg is not None, ts.const + LOAD
            if (looped, at) not in row_known:
                n = R if looped else min(4, NS - at)
                where = bass.ds(ts.reg * U + at, n) if looped else slice(at, at + n)
                _, got = nc.values_load_multi_w_load_instructions(table[0:1, 0, where], engines=[mybir.EngineType.SP], min_val=0, max_val=ZERO)
                row_known.update({(looped, at + i): value for i, value in enumerate(got)})
            return row_known[looped, at]

        def expert(ts, o):
            looped, at = ts.reg is not None, ts.const + o
            if (looped, at) not in word_known:
                start = ts.const + DOWN if looped else at
                for i in range(0, U - DOWN if looped else 1, PACK):
                    where = bass.ds(ts.reg * U + start + i, 1) if looped else slice(start, start + 1)
                    alone(nc.tensor, passed)
                    word = nc.tensor.value_load(table[0:1, 1, where], min_val=0, max_val=E ** PACK - 1)
                    word_known.update({(looped, start + i + j): (word, j) for j in range(PACK)})
            word, j = word_known[looped, at]
            return (word >> (4 * j)) & (E - 1) if j else word & (E - 1)

        @block.sync
        def _(sp):
            def turn(ts):
                if ts.has(LOAD):
                    t, p = ts.at(LOAD)
                    ge(sp, x_mm, t - R + 1)
                    sp.dma_start(xe[p][:, :], xbuf[bass.ds(rows(ts), P), :]).then_inc(x_ld[p], 16)
            turns(sp, NS, BACK, AHEAD, turn, U, R)

        @block.gpsimd
        def _(g):
            for p in range(2):
                g.memset(keep["kb"][p][:, :, :, :, :], 0.0)
                g.memset(keep["rc"][p][:, :, :], 0.0)
            g.tensor_scalar(keep["wo"][:, :, :], keep["wo_raw"][:, :, :], D1 ** -0.5, None, ALU.mult)

        @block.tensor
        def _(pe):
            def turn(ts):
                if ts.has(0):
                    t, p = ts.at(0)
                    pe.wait_ge(xT_done, t + 1)
                    ge(pe, h_done, t - 1)
                    e = expert(ts, 0)
                    pe.matmul(ps_g[p % 2][:, 0:2 * P], xT[p % 4][:, :], gu[:, bass.ds(e * (2 * P), 2 * P)],
                              start=True, stop=True).then_inc(g_mm, 1)
                if ts.has(TX):
                    t, p = ts.at(TX)
                    pe.wait_ge(x_ld[p], (ts.lap(TX) + 1) * 16)
                    ge(pe, xT_done, t - 1)
                    pe.transpose(ps_x[p % 2][:, 0:P], xe[p][:, :], ident).then_inc(x_mm, 1)
                if ts.has(TH):
                    t, p = ts.at(TH)
                    pe.wait_ge(h_done, t + 1)
                    ge(pe, hT_done, t - 1)
                    pe.transpose(ps_h[p % 2][:, 0:P], hh[p % 4][:, :], ident).then_inc(h_mm, 1)
                if ts.has(DOWN):
                    t, p = ts.at(DOWN)
                    pe.wait_ge(hT_done, t + 1)
                    ge(pe, y_done, t - 1)
                    e = expert(ts, DOWN)
                    pe.matmul(ps_y[p % 2][:, 0:D], hT[p % 4][:, :], dn[:, bass.ds(e * D, D)], start=True, stop=True).then_inc(y_mm, 1)
            turns(pe, NS, BACK, AHEAD, turn, U, R)

        @block.scalar
        def _(act):
            def turn(ts):
                if ts.has(OUT):
                    t, p = ts.at(OUT)
                    act.wait_ge(y_mm, t + 1)
                    ge(act, y_st[p], ts.lap(OUT) * 16)
                    act.activation(ye[p][:, :], ps_y[p % 2][:, 0:D], ACT.Copy).then_inc(y_done, 1)
                if ts.has(OUT - 1):
                    t, p = ts.at(OUT - 1)
                    act.wait_ge(y_done, t + 1)
                    act.dma_start(one(ybuf[0:NS * P, :].rearrange("(t p) d -> t p d", p=P), t), ye[p][:, :]).then_inc(y_st[p], 16)
                if ts.has(0):
                    t, p = ts.at(0)
                    act.wait_ge(g_mm, t + 1)
                    ge(act, h_done, t - 1)
                    act.activation(sg[p % 2][:, :], ps_g[p % 2][:, 0:P], ACT.Silu).then_inc(sg_done, 1)
                if ts.has(TX):
                    t, p = ts.at(TX)
                    act.wait_ge(x_mm, t + 1)
                    ge(act, g_mm, t - 3)
                    act.activation(xT[p % 4][:, :], ps_x[p % 2][:, 0:P], ACT.Copy).then_inc(xT_done, 1)
            turns(act, NS, BACK, AHEAD, turn, U, R)
            for p in range(R):
                act.wait_ge(y_st[p], 16 * ((NS - p + R - 1) // R))

        @block.vector
        def _(v):
            done = [0]

            def step(ins):
                ins.then_inc(v_step, 1)
                done[0] += 1
                v.wait_ge(v_step, done[0])

            base = cst[:, C_BASE:C_BASE + X]

            def remap(n):
                if n == 0:
                    v.tensor_copy(edge[:, 0:X], base)
                    v.memset(first[:, E:X], float(NS))
                    v.memset(off[:, E:X], 0.0)
                    step(v.tensor_tensor(first[:, 0:E], end[:, :], nt[:, :], ALU.subtract))
                    step(v.scalar_tensor_tensor(edge[:, X:X + E], nt[:, :], float(P), base[:, 0:E], ALU.mult, ALU.add))
                    v.tensor_copy(edge[:, X + E:], base[:, E:X])
                    step(v.tensor_scalar(edge[:, X:X + E], edge[:, X:X + E], -float(P), None, ALU.add))
                    step(v.tensor_tensor(off[:, 0:E], edge[:, X:X + E], lim[:, 0:E], ALU.subtract))
                    step(v.tensor_scalar(off[:, 0:E], off[:, 0:E], 0.0, None, ALU.max))
                    step(v.scalar_tensor_tensor(gap[:, :], first[:, :], float(P), base, ALU.mult, ALU.subtract))
                if n == 1:
                    v.tensor_copy(shift[:, X:], off[:, :])
                    v.tensor_copy(shift[:, 0:1], gap[:, 0:1])
                    step(v.tensor_tensor(shift[:, 1:X], gap[:, 1:X], gap[:, 0:E], ALU.subtract))
                    step(v.tensor_tensor(shift[:, 1:X], shift[:, 1:X], off[:, 0:E], ALU.subtract))
                    step(v.tensor_copy(slot_f[:, :], idx_all[:, :, :]))
                if n in (2, 3, 4, 5):
                    part = slice(NT // 2 * (n - 2), NT // 2 * (n - 1))
                    where = behind[:, part, :]
                    wide = [P, NT // 2, 2 * X]
                    step(v.tensor_tensor(where, slot_f[:, part].unsqueeze(2).broadcast_to(wide), edge[:, :].unsqueeze(1).broadcast_to(wide), ALU.is_ge))
                    step(v.tensor_tensor(where, where, shift[:, :].unsqueeze(1).broadcast_to(wide), ALU.mult))
                    step(v.reduce_sum(moved[:, part], where, AX.X))
                if n == 6:
                    v.tensor_tensor(idx_all[:, :, :], slot_f[:, :], moved[:, :], ALU.add)

            def turn(ts):
                if ts.has(HID):
                    t, p = ts.at(HID)
                    v.wait_ge(sg_done, t + 1)
                    ge(v, h_mm, t - 3)
                    v.tensor_tensor(hh[p % 4][:, :], ps_g[p % 2][:, P:2 * P], sg[p % 2][:, :], ALU.mult).then_inc(h_done, 1)
                if ts.has(TH - 1):
                    t, p = ts.at(TH - 1)
                    v.wait_ge(h_mm, t + 1)
                    ge(v, y_mm, t - 3)
                    v.tensor_copy(hT[p % 4][:, :], ps_h[p % 2][:, 0:P]).then_inc(hT_done, 1)
                if ts.reg is None and 0 <= ts.const < 7:
                    remap(ts.const)
            turns(v, NS, BACK, AHEAD, turn, U, R)


def phase3(nc, NT, ctxT_in, keep, ybuf, out):
    cst, x_all, idx_all, w_all = keep["cst"], keep["x_all"], keep["idx_all"], keep["w_all"]
    HP = H1 // 2
    FC = FF // P
    XI, HID, HI, RES = -2, -3, -4, -5
    U = 4
    BACK, AHEAD = 6, 4
    with ExitStack() as ctx:
        def sb(name, shape, dt=F32):
            return ctx.enter_context(nc.sbuf_tensor(name, shape, dt))

        def sem(name):
            return ctx.enter_context(nc.semaphore(name))

        ident = cst[:, C_ID:C_ID + P]
        wq, wk, wv, wo, bq, bk, bv, bo = (keep[n] for n in ("wq", "wk", "wv", "wo", "bq", "bk", "bv", "bo"))
        cT = [sb(f"p3_cT{i}", [D, P]) for i in range(2)]
        idx = [sb(f"p3_idx{i}", [P, 2], I32) for i in range(2)]
        gy = [[sb(f"p3_gy{i}{k}", [P, D]) for k in range(2)] for i in range(2)]
        stat, mv, rstd = ([sb(f"p3_{n}{i}", [P, k]) for i in range(2)] for n, k in (("st", 6), ("mv", 2), ("rs", 1)))
        xln = [sb(f"p3_xln{i}", [P, D]) for i in range(2)]
        xT = [sb(f"p3_xT{i}", [D, P]) for i in range(2)]
        qT = [sb(f"p3_qT{i}", [P, HP, 2, S]) for i in range(2)]
        kb, rc = keep["kb"], keep["rc"]
        vd = [sb(f"p3_vd{i}", [P, 2, HP, D1]) for i in range(2)]
        vb = [sb(f"p3_vb{i}", [P, 2, HP, 2, D1]) for i in range(2)]
        pr = [sb(f"p3_pr{i}", [P, 2, HP, S]) for i in range(2)]
        mx, sm = ([sb(f"p3_{n}{i}", [P, 2, HP]) for i in range(2)] for n in ("mx", "sm"))
        oT = [sb(f"p3_oT{i}", [P, HP, 2, S]) for i in range(2)]
        ones = cst[:, C_ONES:C_ONES + P]
        wf = keep["wf"]
        idb = sb("p4_idb", [P, P], BF16)
        wr = sb("p4_wr", [P, FF])
        wi = [sb(f"p4_wi{i}", [P, FF], BF16) for i in range(2)]
        wsum, ws, wrs = sb("p4_wsum", [P, 2]), sb("p4_ws", [P, 2]), sb("p4_wrs", [P, 2])
        stat4, mv4, rstd4, am, qs, ds, am2, qs2, ds2 = ([sb(f"p4_{n}{i}", [P, k]) for i in range(2)] for n, k in (
            ("st", 6), ("mv", 2), ("rs", 1), ("am", 1), ("qs", 1), ("ds", 1), ("am2", 1), ("qs2", 1), ("ds2", 1)))
        xln4, xf = sb("p4_xln", [P, D]), sb("p4_xf", [P, D])
        xi, xiT = ([sb(f"p4_{n}{i}", [P, D], BF16) for i in range(2)] for n in ("xi", "xiT"))
        hid, hf = [sb(f"p4_h{i}", [P, FF]) for i in range(2)], sb("p4_hf", [P, FF])
        hi, hiT = ([sb(f"p4_{n}{i}", [P, FC, P], BF16) for i in range(2)] for n in ("hi", "hiT"))
        y = [sb(f"p4_y{i}", [P, D]) for i in range(2)]

        ps_r = ctx.enter_context(nc.psum_tensor("p3_r", [P, 2, 512], F32))
        ps_s = ctx.enter_context(nc.psum_tensor("p3_s", [P, 2, HP, S], F32))
        ps_o = ctx.enter_context(nc.psum_tensor("p3_o", [P, 2, HP, S], F32))
        ps_x = ctx.enter_context(nc.psum_tensor("p3_x", [P, 512], F32))
        ps_w = ctx.enter_context(nc.psum_tensor("p3_w", [P, 512], F32))
        ps_xi = ps_x[:, P:P + P // 2].bitcast(BF16)
        ps_hi = ps_r[:, 1, 0:FF // 2].bitcast(BF16)

        c_ld = [sem(f"c3_ld{i}") for i in range(2)]
        got = [sem(f"got{i}") for i in range(2)]
        mixed, mv_done, rs_done, xln_done = (sem(n) for n in ("mixed", "mv3_done", "rs3_done", "xln3_done"))
        turned_x, xT_done, q_mm, q_done, k_mm, k0_done, k1_done, v_mm, vd_done, vb_done = (
            sem(n) for n in ("turned3_x", "xT3_done", "q3_mm", "q3_done", "k3_mm", "k30_done", "k31_done", "v3_mm", "vd_done", "vb3_done"))
        s_mm, sub_done, exp_done, rc_done, o_mm, oT_done, ao_mm, x3_done = (
            sem(n) for n in ("s3_mm", "sub3_done", "exp3_done", "rc3_done", "o3_mm", "oT3_done", "ao3_mm", "x3_done"))
        w_sized, w_mm, w_rounded = sem("w_sized"), sem("w4_mm"), sem("w_rounded")
        mv4_done, rs4_done, qs2_done, bo_done, xi_done, xi_mm, xiT_done, h_mm, h_done, hi_done, hi_mm, hiT_done, y_mm, y_done = (
            sem(n) for n in ("mv4_done", "rs4_done", "qs2_done", "bo3_done", "xi_done", "xi_mm", "xiT_done", "h4_mm", "h4_done", "hi_done", "hi_mm", "hiT_done", "y4_mm", "y4_done"))
        st = [sem(f"out_st{i}") for i in range(2)]
        v_step, g_step, w_step = sem("v_step3"), sem("g_step3"), sem("w_step")
        passed = sem("passed")
        block = ctx.enter_context(nc.Block())

        def upto(t, more):
            return min(t + more, NT) if isinstance(t, int) else t + more

        @block.sync
        def _(sp):
            def turn(ts):
                if ts.has(2):
                    t, p = ts.at(2)
                    ge(sp, v_mm, 2 * t - 2)
                    sp.dma_start(cT[p][:, :], one(ctxT_in, t)).then_inc(c_ld[p], 16)
                if ts.has(RES):
                    t, p = ts.at(RES)
                    sp.wait_ge(y_done, t + 1)
                    sp.dma_start(one(out, t), y[p][:, :]).then_inc(st[p], 16)
            turns(sp, NT, BACK, AHEAD, turn, U, 2)
            for p in range(2):
                sp.wait_ge(st[p], 16 * (NT // 2))

        @block.tensor
        def _(pe):
            pe.wait_ge(w_sized, 1)
            pe.matmul(ps_w[:, 2 * P:2 * P + 2], ones, wsum[:, :], start=True, stop=True).then_inc(w_mm, 1)
            pe.wait_ge(w_rounded, 1)

            def turn(ts):
                if ts.has(0):
                    t, p = ts.at(0)
                    pe.wait_ge(k0_done, 2 * t + 2)
                    pe.wait_ge(k1_done, 2 * t + 2)
                    pe.wait_ge(q_done, 2 * t + 2)
                    for b in range(2):
                        ge(pe, sub_done, 2 * t - 1 + b)
                        for c in range(HP):
                            last = pe.matmul(ps_s[:, b, c, :], kb[p][:, c, b, :, :], qT[p][:, c, b, :], start=True, stop=True)
                        last.then_inc(s_mm, 1)
                def head_outputs(b):
                    if ts.has(-1):
                        t, p = ts.at(-1)
                        if b == 0:
                            pe.wait_ge(vb_done, t + 1)
                        pe.wait_ge(exp_done, 2 * t + 1 + b)
                        ge(pe, oT_done, 2 * t - 1 + b)
                        for c in range(HP):
                            last = pe.matmul(ps_o[:, b, c, :], vb[p][:, b, c, :, :], pr[p][:, b, c, :], start=True, stop=True)
                        last.then_inc(o_mm, 1)

                if ts.has(1):
                    t, p = ts.at(1)
                    pe.wait_ge(xT_done, t + 1)
                    for h in range(2):
                        ge(pe, vd_done, 2 * t - 1 + h)
                        ge(pe, (h_done, hiT_done)[h], t - 1 + (HID, HI)[h])
                        for c in range(4):
                            last = pe.matmul(ps_r[:, h, P * c:P * c + P], wq[:, P * (4 * h + c):P * (4 * h + c + 1)], xT[p][:, :], start=True, stop=True)
                        last.then_inc(q_mm, 1)
                head_outputs(0)
                if ts.has(1):
                    t, p = ts.at(1)
                    pe.wait_ge(c_ld[p], (ts.lap(1) + 1) * 16)
                    for h in range(2):
                        pe.wait_ge(q_done, 2 * t + 1 + h)
                        for c in range(4):
                            last = pe.matmul(ps_r[:, h, P * c:P * c + P], wk[:, P * (4 * h + c):P * (4 * h + c + 1)], cT[p][:, :], start=True, stop=True)
                        last.then_inc(k_mm, 1)
                head_outputs(1)
                if ts.has(HID):
                    t, p = ts.at(HID)
                    pe.wait_ge(xi_done, t + 1)
                    pe.wait_ge(xT_done, upto(t, 2 - HID))
                    pe.transpose(ps_xi, xi[p][:, :], idb[:, :]).then_inc(xi_mm, 1)
                if ts.has(RES):
                    t, p = ts.at(RES)
                    pe.wait_ge(hiT_done, t + 1)
                    pe.wait_ge(x3_done, upto(t, -1 - RES))
                    ge(pe, y_done, t)
                    for c in range(FC):
                        last = pe.matmul(ps_w[:, P:2 * P], hiT[p][:, c, :], wi[1][:, P * c:P * c + P], start=(c == 0), stop=(c == FC - 1))
                    last.then_inc(y_mm, 1)
                if ts.has(1):
                    t, p = ts.at(1)
                    for b in range(2):
                        pe.wait_ge(k0_done, 2 * t + 1 + b)
                        pe.wait_ge(k1_done, 2 * t + 1 + b)
                        for x in range(2):
                            last = pe.matmul(ps_r[64 * x:64 * x + 64, b, :], cT[p][:, S * b:S * b + S], wv[:, 512 * x:512 * x + 512], start=True, stop=True)
                        last.then_inc(v_mm, 1)
                if ts.has(HID):
                    t, p = ts.at(HID)
                    pe.wait_ge(xiT_done, t + 1)
                    pe.wait_ge(vd_done, 2 * upto(t, 2 - HID) - 1)
                    ge(pe, h_done, t)
                    pe.matmul(ps_r[:, 0, :], xiT[p][:, :], wi[0][:, :], start=True, stop=True).then_inc(h_mm, 1)
                if ts.has(2):
                    t, p = ts.at(2)
                    pe.wait_ge(xln_done, t + 1)
                    ge(pe, xiT_done, t - 2 + HID + 1)
                    ge(pe, xT_done, t)
                    pe.transpose(ps_x[:, 0:P], xln[p][:, :], ident).then_inc(turned_x, 1)
                if ts.has(-1):
                    t, p = ts.at(-1)
                    pe.wait_ge(oT_done, 2 * t + 2)
                    ge(pe, x3_done, t)
                    ge(pe, y_done, t + 1 + RES + 1)
                    for c in range(HP):
                        last = pe.matmul(ps_w[:, 0:D], oT[p][:, c, :, :], wo[:, c, :], start=(c == 0), stop=(c == HP - 1))
                    last.then_inc(ao_mm, 1)
                if ts.has(HI):
                    t, p = ts.at(HI)
                    pe.wait_ge(hi_done, t + 1)
                    pe.wait_ge(vd_done, 2 * upto(t, 2 - HI))
                    ge(pe, hiT_done, t)
                    for c in range(FC):
                        last = pe.transpose(ps_hi[:, P * c:P * c + P], hi[p][:, c, :], idb[:, :])
                    last.then_inc(hi_mm, 1)
            turns(pe, NT, BACK, AHEAD, turn, U, 2)

        @block.scalar
        def _(act):

            def turn(ts):
                if ts.has(0):
                    t, p = ts.at(0)
                    for b in range(2):
                        act.wait_ge(sub_done, 2 * t + 1 + b)
                        act.activation(pr[p][:, b, :, :], pr[p][:, b, :, :], ACT.Exp).then_inc(exp_done, 1)

                def head_outputs(b):
                    if ts.has(-1):
                        t, p = ts.at(-1)
                        act.wait_ge(o_mm, 2 * t + 1 + b)
                        ge(act, ao_mm, t - 1)
                        act.activation(oT[p][:, :, b, :], ps_o[:, b, :, :], ACT.Copy).then_inc(oT_done, 1)

                if ts.has(1):
                    t, p = ts.at(1)
                    ge(act, s_mm, 2 * t - 2)
                    for h in range(2):
                        act.wait_ge(q_mm, 2 * t + 1 + h)
                        for c in range(4):
                            last = act.activation(qT[p][:, 4 * h + c, :, :], ps_r[:, h, P * c:P * c + P], ACT.Identity, bias=bq[:, 4 * h + c:4 * h + c + 1])
                        last.then_inc(q_done, 1)
                head_outputs(0)
                if ts.has(1):
                    t, p = ts.at(1)
                    for h in range(2):
                        act.wait_ge(k_mm, 2 * t + 1 + h)
                        for c in range(4):
                            last = act.activation(kb[p][0:64, 4 * h + c, :, 0, :], ps_r[0:64, h, P * c:P * c + P].rearrange("p (b s) -> p b s", b=2), ACT.Identity,
                                                  bias=bk[0:64, 4 * h + c:4 * h + c + 1])
                        last.then_inc(k0_done, 1)
                head_outputs(1)
                if ts.has(HID):
                    t, p = ts.at(HID)
                    act.wait_ge(xi_mm, t + 1)
                    ge(act, h_mm, t - 1)
                    act.activation(xiT[p][:, :], ps_xi, ACT.Copy).then_inc(xiT_done, 1)
                if ts.has(HID):
                    t, p = ts.at(HID)
                    act.wait_ge(h_mm, t + 1)
                    ge(act, hi_done, t - 1)
                    act.activation(hid[p][:, :], ps_r[:, 0, :], ACT.Gelu, scale=ds[p][:, :]).then_inc(h_done, 1)
                if ts.has(2):
                    t, p = ts.at(2)
                    act.wait_ge(turned_x, t + 1)
                    ge(act, q_mm, 2 * t - 2)
                    act.activation(xT[p][:, :], ps_x[:, 0:P], ACT.Copy).then_inc(xT_done, 1)
                if ts.has(HI):
                    t, p = ts.at(HI)
                    act.wait_ge(hi_mm, t + 1)
                    ge(act, y_mm, t - 1)
                    act.activation(hiT[p][:, :, :], ps_hi, ACT.Copy).then_inc(hiT_done, 1)
            turns(act, NT, BACK, AHEAD, turn, U, 2)

        @block.gpsimd
        def _(g):
            half = cst[:, C_HALF:C_HALF + 1]
            steps = Steps(g, g_step)

            def turn(ts):
                steps.turn(ts, NT, {"eps4": (XI, 1), "eps": (3, 1), "idx": (4, 1)})
                if ts.has(XI):
                    t, p = ts.at(XI)
                    g.wait_ge(mv4_done, t + 1)
                    ge(g, xi_done, t - 1)
                    alone(g, passed)
                    steps.did("eps4", g.tensor_scalar(rstd4[p][:, :], mv4[p][:, 1:2], EPS, None, ALU.add))
                    g.tensor_tensor(rstd4[p][:, :], rstd4[p][:, :], half, ALU.pow).then_inc(rs4_done, 1)
                if ts.has(2):
                    t, p = ts.at(2)
                    g.wait_ge(xln_done, t + 1)
                    alone(g, passed)
                    g.tensor_tensor(mid(x_all, t), mid(x_all, t), bo[:, :], ALU.add).then_inc(bo_done, 1)
                if ts.has(4):
                    t, p = ts.at(4)
                    ge(g, mixed, t - 1)
                    steps.did("idx", g.tensor_copy(idx[p][:, :], mid(idx_all, t)))
                    for k in range(2):
                        alone(g, passed)
                        g.indirect_dma_start(gy[p][k][:, :], None, ybuf, bass.IndirectOffsetOnAxis(ap=idx[p][:, k:k + 1], axis=0)
                                             ).then_inc(got[p], 16)
                if ts.has(3):
                    t, p = ts.at(3)
                    g.wait_ge(mv_done, t + 1)
                    ge(g, xln_done, t - 1)
                    alone(g, passed)
                    steps.did("eps", g.tensor_scalar(rstd[p][:, :], mv[p][:, 1:2], EPS, None, ALU.add))
                    g.tensor_tensor(rstd[p][:, :], rstd[p][:, :], half, ALU.pow).then_inc(rs_done, 1)
                if ts.has(0):
                    t, p = ts.at(0)
                    g.wait_ge(rc_done, t + 1)
                    g.wait_ge(vd_done, 2 * t + 2)
                    ge(g, o_mm, 2 * t - 2)
                    g.tensor_tensor(vb[p][:, :, :, :, :].rearrange("p b c x d -> p (b c) x d"),
                                    vd[p][:, :, :, :].rearrange("p b c d -> p (b c) d").unsqueeze(2).broadcast_to([P, 2 * HP, 2, D1]),
                                    rc[p][:, :, :].unsqueeze(3).broadcast_to([P, 2 * HP, 2, D1]), ALU.mult).then_inc(vb_done, 1)
            turns(g, NT, BACK, AHEAD, turn, U, 2)

        @block.vector
        def _(v):
            steps = Steps(v, v_step)
            done = [0]

            def step(ins):
                ins.then_inc(w_step, 1)
                done[0] += 1
                v.wait_ge(w_step, done[0])

            v.tensor_copy(idb[:, :], ident)
            for i in range(2):
                ins = v.tensor_reduce(wsum[:, i:i + 1], wf[i][:, :], AX.X, ALU.add, apply_absolute_value=True)
            ins.then_inc(w_sized, 1)
            v.wait_ge(w_mm, 1)
            step(v.tensor_scalar(ws[:, :], ps_w[:, 2 * P:2 * P + 2], 1.0 / (FF * D), EPS, ALU.mult, ALU.max))
            step(v.reciprocal(wrs[:, :], ws[:, :]))
            for i in range(2):
                step(v.tensor_scalar(wr[:, :], wf[i][:, :], wrs[:, i:i + 1], MAGIC, ALU.mult, ALU.add))
                step(v.tensor_scalar(wr[:, :], wr[:, :], -MAGIC, 1.0, ALU.add, ALU.min))
                ins = v.tensor_scalar(wi[i][:, :], wr[:, :], -1.0, None, ALU.max)
                if i == 0:
                    step(ins)
            ins.then_inc(w_rounded, 1)

            def turn(ts):
                steps.turn(ts, NT, {"max": (0, 2), "sum": (0, 1), "mix": (3, 2), "st4": (-1, 1), "xi": (XI, 5), "hi": (HI, 2), "hi2": (HI, 1)})
                if ts.has(0):
                    t, p = ts.at(0)
                    ge(v, o_mm, 2 * t - 2)
                    for b in range(2):
                        v.wait_ge(s_mm, 2 * t + 1 + b)
                        steps.did("max", v.tensor_reduce(mx[p][:, b, :], ps_s[:, b, :, :], AX.X, ALU.max))
                        v.tensor_tensor(pr[p][:, b, :, :], ps_s[:, b, :, :], mx[p][:, b, :].unsqueeze(2).broadcast_to([P, HP, S]),
                                        ALU.subtract).then_inc(sub_done, 1)
                if ts.has(3):
                    t, p = ts.at(3)
                    v.wait_ge(got[p], (ts.lap(3) + 1) * 32)
                    wt = mid(w_all, t)
                    steps.did("mix", v.scalar_tensor_tensor(mid(x_all, t), gy[p][0][:, :], wt[:, 0:1], mid(x_all, t), ALU.mult, ALU.add))
                    v.scalar_tensor_tensor(mid(x_all, t), gy[p][1][:, :], wt[:, 1:2], mid(x_all, t), ALU.mult, ALU.add).then_inc(mixed, 1)
                    v.wait_ge(mixed, t + 1)
                    alone(v, passed)
                    steps.did("mix", v.bn_stats(stat[p][:, :], mid(x_all, t)))
                    alone(v, passed)
                    v.bn_aggr(mv[p][:, :], stat[p][:, :]).then_inc(mv_done, 1)
                if ts.has(0):
                    t, p = ts.at(0)
                    ge(v, vb_done, t - 1)
                    v.wait_ge(exp_done, 2 * t + 2)
                    steps.did("sum", v.reduce_sum(sm[p][:, :, :], pr[p][:, :, :, :], AX.X))
                    for x in range(2):
                        rows = slice(64 * x, 64 * x + 64)
                        last = v.reciprocal(rc[p][rows, :, x], sm[p][rows, :, :].rearrange("p b c -> p (b c)"))
                    last.then_inc(rc_done, 1)
                if ts.has(1):
                    t, p = ts.at(1)
                    ge(v, s_mm, 2 * t - 2)
                    for h in range(2):
                        v.wait_ge(k_mm, 2 * t + 1 + h)
                        v.tensor_tensor(kb[p][64:128, 4 * h:4 * h + 4, :, 1, :], ps_r[64:128, h, :].rearrange("p (c b s) -> p c b s", c=4, b=2),
                                        bk[64:128, 4 * h:4 * h + 4].unsqueeze(2).unsqueeze(3).broadcast_to([64, 4, 2, S]), ALU.add).then_inc(k1_done, 1)
                if ts.has(HI):
                    t, p = ts.at(HI)
                    v.wait_ge(h_done, t + 1)
                    ge(v, y_done, t - 1)
                    steps.did("hi", v.tensor_reduce(am2[p][:, :], hid[p][:, :], AX.X, ALU.max, apply_absolute_value=True))
                    steps.did("hi", v.tensor_scalar(am2[p][:, :], am2[p][:, :], EPS, 1.0 / 127.0, ALU.max, ALU.mult))
                    v.tensor_scalar(ds2[p][:, :], am2[p][:, :], ws[:, 1:2], None, ALU.mult)
                    v.reciprocal(qs2[p][:, :], am2[p][:, :]).then_inc(qs2_done, 1)
                if ts.has(RES):
                    t, p = ts.at(RES)
                    v.wait_ge(y_mm, t + 1)
                    ge(v, st[p], ts.lap(RES) * 16)
                    v.scalar_tensor_tensor(y[p][:, :], ps_w[:, P:2 * P], ds2[p][:, :], mid(x_all, t), ALU.mult, ALU.add).then_inc(y_done, 1)
                if ts.has(3):
                    t, p = ts.at(3)
                    v.wait_ge(rs_done, t + 1)
                    ge(v, turned_x, t - 1)
                    v.tensor_scalar(xln[p][:, :], mid(x_all, t), mv[p][:, 0:1], rstd[p][:, :], ALU.subtract, ALU.mult).then_inc(xln_done, 1)
                if ts.has(1):
                    t, p = ts.at(1)
                    ge(v, vb_done, t - 1)
                    for b in range(2):
                        v.wait_ge(v_mm, 2 * t + 1 + b)
                        v.tensor_tensor(vd[p][:, b, :, :], ps_r[:, b, :], bv[:, :], ALU.add).then_inc(vd_done, 1)
                if ts.has(HI):
                    t, p = ts.at(HI)
                    v.wait_ge(qs2_done, t + 1)
                    steps.did("hi2", v.tensor_scalar(hf[:, :], hid[p][:, :], qs2[p][:, :], MAGIC, ALU.mult, ALU.add))
                    ge(v, hi_mm, t - 1)
                    v.tensor_scalar(hi[p][:, :, :], hf[:, :], -MAGIC, None, ALU.add).then_inc(hi_done, 1)
                if ts.has(XI):
                    t, p = ts.at(XI)
                    v.wait_ge(rs4_done, t + 1)
                    steps.did("xi", v.tensor_scalar(xln4[:, :], mid(x_all, t), mv4[p][:, 0:1], rstd4[p][:, :], ALU.subtract, ALU.mult))
                    steps.did("xi", v.tensor_reduce(am[p][:, :], xln4[:, :], AX.X, ALU.max, apply_absolute_value=True))
                    steps.did("xi", v.tensor_scalar(am[p][:, :], am[p][:, :], EPS, 1.0 / 127.0, ALU.max, ALU.mult))
                    ge(v, h_done, t - 1)
                    v.tensor_scalar(ds[p][:, :], am[p][:, :], ws[:, 0:1], None, ALU.mult)
                    steps.did("xi", v.reciprocal(qs[p][:, :], am[p][:, :]))
                    steps.did("xi", v.tensor_scalar(xf[:, :], xln4[:, :], qs[p][:, :], MAGIC, ALU.mult, ALU.add))
                    ge(v, xi_mm, t - 1)
                    v.tensor_scalar(xi[p][:, :], xf[:, :], -MAGIC, None, ALU.add).then_inc(xi_done, 1)
                if ts.has(-1):
                    t, p = ts.at(-1)
                    v.wait_ge(ao_mm, t + 1)
                    v.wait_ge(bo_done, t + 1)
                    v.tensor_tensor(mid(x_all, t), ps_w[:, 0:D], mid(x_all, t), ALU.add).then_inc(x3_done, 1)
                    v.wait_ge(x3_done, t + 1)
                    alone(v, passed)
                    steps.did("st4", v.bn_stats(stat4[p][:, :], mid(x_all, t)))
                    alone(v, passed)
                    v.bn_aggr(mv4[p][:, :], stat4[p][:, :]).then_inc(mv4_done, 1)
            turns(v, NT, BACK, AHEAD, turn, U, 2)


def program(nc, NT, a, out):
    xbuf = nc.dram_tensor("slots_in", [ZERO + P, D], F32).ap()
    ybuf = nc.dram_tensor("slots_out", [(slot_tiles(NT * P) + 1) * P, D], F32).ap()
    with ExitStack() as ctx:
        def sb(name, shape, dt=F32):
            return ctx.enter_context(nc.sbuf_tensor(name, shape, dt))

        keep = dict(x_all=sb("x_all", [P, NT, D]), idx_all=sb("idx_all", [P, NT, 2], I32), w_all=sb("w_all", [P, NT, 2]),
                    nt=sb("nt", [P, E]), end=sb("end", [P, E]), lim=sb("lim", [P, X]), table=sb("table", [1, 2, P], I32),
                    cst=sb("cst", [P, N_CONST]), gu=sb("gu", [D, E * 2 * P]), dn=sb("dn", [P, E * D]),
                    wq=sb("l1_wq", [D, H1 * D1]), wk=sb("l1_wk", [D, H1 * D1]), wv=sb("l1_wv", [D, H1 * D1]), wo=sb("l1_wo", [P, H1 // 2, D]),
                    bq=sb("l1_bq", [P, H1 // 2]), bk=sb("l1_bk", [P, H1 // 2]), bv=sb("l1_bv", [P, H1 * D1 // 2]), bo=sb("l1_bo", [P, D]))
        names = dict(wq="Wq", wk="Wk", wv="Wv", wo="Wo", bq="bq", bk="bk", bv="bv", bo="bo")
        w0 = {k: a["L0_xattn_" + n] for k, n in names.items()} | {"wr": a["L0_ffn_router_w"]}
        w1 = {k: a["L1_xattn_" + n] for k, n in names.items()}
        later = [(keep["gu"][:, :].rearrange("d (e h) -> d e h", e=E)[:, :, 0:P], a["L0_ffn_gate_w"]),
                 (keep["gu"][:, :].rearrange("d (e h) -> d e h", e=E)[:, :, P:2 * P], a["L0_ffn_up_w"]),
                 (keep["dn"][:, :].rearrange("h (e d) -> h e d", e=E), a["L0_ffn_down_w"])]
        keep["wo_raw"], keep["wo"] = keep["wo"], sb("l1_wo8", [P, H1 // 2, D])
        keep["kb"] = [sb(f"l1_kb{i}", [P, H1 // 2, 2, 2, S]) for i in range(2)]
        keep["rc"] = [sb(f"l1_rc{i}", [P, H1, 2]) for i in range(2)]
        keep["wf"] = [sb(f"l1_wf{i}", [P, FF]) for i in range(2)]
        later.append((keep["wf"][0][:, :], a["L1_ffn_w1"]))
        later.append((keep["wf"][1][:, :].rearrange("p (c d) -> p c d", d=D), a["L1_ffn_w2"].rearrange("(c p) d -> p c d", p=P)))
        HP = H1 // 2
        for n in ("wq", "wk", "bq", "bk"):
            later.append((keep[n][:, :], w1[n]))
        later.append((keep["wo_raw"][:, :, :], w1["wo"].rearrange("(c p) n -> p c n", p=P)))
        later.append((keep["bo"][:, :], spread(w1["bo"])))
        for x in range(2):
            later.append((keep["wv"][:, :].rearrange("p (x c d) -> p x c d", x=2, c=HP)[:, x], w1["wv"].rearrange("p (c x d) -> p x c d", x=2, c=HP)[:, x]))
            later.append((keep["bv"][64 * x:64 * x + 64, :].rearrange("p (c d) -> p c d", c=HP), spread(w1["bv"].rearrange("(c x d) -> x c d", x=2, c=HP)[x], 64)))
        phase1(nc, NT, a["x"], a["ctx_twice"], a["constants"], w0, keep, xbuf, ybuf, later)
        phase2(nc, NT, keep, xbuf, ybuf)
        phase3(nc, NT, a["ctx_turned"], keep, ybuf, out)


def kernel(x, ctx_1024, **weights):
    import numpy as np
    import concourse.bacc as bacc
    from concourse.bass_utils import run_bass_kernel_spmd

    batch, s, d = x.shape
    nt = batch * s // P
    ctx_t = np.asarray(ctx_1024).reshape(nt, 2, s, d).transpose(0, 3, 1, 2)
    laid = {
        "x": np.asarray(x).reshape(batch * s, d),
        "ctx_turned": ctx_t.reshape(nt, d, 2 * s),
        "ctx_twice": np.broadcast_to(ctx_t[:, :, :, None, :], (nt, d, 2, 2, s)),
        "constants": constants(),
    }
    for name, v in weights.items():
        laid[name] = np.asarray(v)
    for name in ("L0_ffn_gate_w", "L0_ffn_up_w", "L0_ffn_down_w"):
        laid[name] = laid[name].transpose(1, 0, 2)
    for name in ("L1_ffn_w1", "L1_ffn_w2"):
        laid[name] = laid[name].T
    for name in ("L1_xattn_bq", "L1_xattn_bk"):
        laid[name] = laid[name].reshape(H1 // 2, P).T
    laid = {k: np.ascontiguousarray(v) for k, v in laid.items()}
    nc = bacc.Bacc("TRN2", target_bir_lowering=False, num_devices=1)
    a = {k: nc.dram_tensor(f"in_{k}", v.shape, mybir.dt.from_np(v.dtype), kind="ExternalInput").ap() for k, v in laid.items()}
    out = nc.dram_tensor("out_x", [nt, P, d], F32, kind="ExternalOutput").ap()
    program(nc, nt, a, out)
    r = run_bass_kernel_spmd(nc, [{f"in_{k}": v for k, v in laid.items()}], core_ids=[0])
    return r.results[0]["out_x"].reshape(batch, s, d)
```
